# Optimizing a Trainium2 kernel written in Bass

```python
import numpy as np
import jax
import jax.numpy as jnp

def _softmax(x, axis=-1):
    return jax.nn.softmax(x, axis=axis)

def _gelu(x):
    return jax.nn.gelu(x, approximate=True)

def _silu(x):
    return jax.nn.silu(x)

def _sigmoid(x):
    return jax.nn.sigmoid(x)

def _layernorm(x, axis=-1, eps=1e-05):
    m = jnp.mean(x, axis=axis, keepdims=True)
    v = jnp.var(x, axis=axis, keepdims=True)
    return (x - m) / jnp.sqrt(v + eps)

def _scatter_add(tgt, idx, src, axis=0):
    return tgt.at[idx].add(src)

def _segment_sum(src, seg, n):
    return jax.ops.segment_sum(src, seg, n)
kernel_name = 'mk_gnn_resnorm_d4_gnn_r32_4e3367'

def setup_inputs(seed: int=0):
    np.random.seed(seed)
    _w = jnp.asarray

    def _rec_inputs():
        import jax
        import jax.numpy as jnp
        _gk = jax.random.key(seed)
        x = -0.000202 + 1 * jax.random.normal(jax.random.fold_in(_gk, 1), (3125, 128), jnp.float32)
        _s = jax.random.randint(jax.random.fold_in(_gk, 2), (50000,), 0, 3125, jnp.int32)
        _d = jax.random.randint(jax.random.fold_in(_gk, 3), (50000,), 0, 3125, jnp.int32)
        _loop = jnp.arange(3125, dtype=jnp.int32)
        src = jnp.concatenate([_s, _d, _loop])
        dst = jnp.concatenate([_d, _s, _loop])
        _o = jnp.argsort(dst, stable=True)
        src = src[_o]
        dst = dst[_o]
        edge_attr_32 = 0.000189758 + 1.00013 * jax.random.normal(jax.random.fold_in(_gk, 11), (103125, 32), jnp.float32)
        edge_type_50 = jax.random.randint(jax.random.fold_in(_gk, 13), (103125,), 0, 50, jnp.int32)
        return (x, src, dst, edge_attr_32, edge_type_50)
    x, src, dst, edge_attr_32, edge_type_50 = _rec_inputs()

    def _L0_gnn_setup():
        import jax, jax.numpy as jnp
        import numpy as np
        N, E, IN, H, C = (50000, 25000, 128, 4, 32)
        HC = H * C
        EPS = 1e-05
        NEG_SLOPE = 0.2

        def _bn(z, gamma, beta):
            mu = z.mean(0)
            var = z.var(0)
            return (z - mu) * jax.lax.rsqrt(var + EPS) * gamma + beta

        def _ln(z, gamma, beta):
            mu = z.mean(-1, keepdims=True)
            var = z.var(-1, keepdims=True)
            return (z - mu) * jax.lax.rsqrt(var + EPS) * gamma + beta
        key = jax.random.key(seed)
        ks = jax.random.split(key, 12)
        s = 1.0 / np.sqrt(IN)
        return {'x': jax.random.normal(ks[0], (N, IN), jnp.float32), 'edge_index': jax.random.randint(ks[1], (2, E), 0, N, jnp.int64), 'W': jax.random.normal(ks[2], (IN, HC), jnp.float32) * s, 'att_src': jax.random.normal(ks[3], (H, C), jnp.float32) * s, 'att_dst': jax.random.normal(ks[4], (H, C), jnp.float32) * s, 'bias': jnp.zeros((HC,), jnp.float32), 'bn_gamma': jnp.ones((HC,), jnp.float32), 'bn_beta': jnp.zeros((HC,), jnp.float32), 'ln_gamma': jnp.ones((HC,), jnp.float32), 'ln_beta': jnp.zeros((HC,), jnp.float32), 'res_W': jax.random.normal(ks[5], (IN, HC), jnp.float32) * s, 'res_b': jnp.zeros((HC,), jnp.float32), 'bnres_gamma': jnp.ones((HC,), jnp.float32), 'bnres_beta': jnp.zeros((HC,), jnp.float32)}
    _L0_gnn_all = _L0_gnn_setup()
    _L0_gnn_in = {k: v for k, v in _L0_gnn_all.items() if k in ('W', 'att_src', 'att_dst', 'bias', 'bn_gamma', 'bn_beta', 'ln_gamma', 'ln_beta', 'res_W', 'res_b', 'bnres_gamma', 'bnres_beta')}
    del _L0_gnn_all

    def _L1_gnn_setup():
        import jax, jax.numpy as jnp
        import numpy as np
        LN_EPS = 1e-05
        key = jax.random.key(seed)
        ks = jax.random.split(key, 6)
        N, E, D = (50000, 25000, 128)
        x = jax.random.normal(ks[0], (N, D), dtype=jnp.float32)
        edge_index = jax.random.randint(ks[1], (2, E), 0, N, dtype=jnp.int64)
        W = jax.random.normal(ks[2], (D, D), dtype=jnp.float32) / np.sqrt(D)
        b = jax.random.normal(ks[3], (D,), dtype=jnp.float32) * 0.01
        gamma = jnp.ones((D,), dtype=jnp.float32)
        beta = jnp.zeros((D,), dtype=jnp.float32)
        return {'x': x, 'edge_index': edge_index, 'W': W, 'b': b, 'gamma': gamma, 'beta': beta}
    _L1_gnn_all = _L1_gnn_setup()
    _L1_gnn_in = {k: v for k, v in _L1_gnn_all.items() if k in ('W', 'b', 'gamma', 'beta')}
    del _L1_gnn_all

    def _L2_gnn_setup():
        import jax, jax.numpy as jnp
        import numpy as np
        N_ENT = 512
        N_REL = 50
        D = 128
        B = 4
        E = 8192
        key = jax.random.key(seed)
        k1, k2, k3, k4, k5, k6 = jax.random.split(key, 6)
        x = jax.random.normal(k1, (N_ENT, D), dtype=jnp.float32)
        bases = jax.random.normal(k2, (B, D, D), dtype=jnp.float32) * 0.05
        comps = jax.random.normal(k3, (N_REL, B), dtype=jnp.float32)
        alpha = jax.random.normal(k4, (N_REL, 1), dtype=jnp.float32)
        edge_index = jax.random.randint(k5, (2, E), 0, N_ENT, dtype=jnp.int64)
        edge_type = jax.random.randint(k6, (E,), 0, N_REL, dtype=jnp.int64)
        return {'x': x, 'bases': bases, 'comps': comps, 'alpha': alpha, 'edge_index': edge_index, 'edge_type': edge_type}
    _L2_gnn_all = _L2_gnn_setup()
    _L2_gnn_in = {k: v for k, v in _L2_gnn_all.items() if k in ('bases', 'comps', 'alpha')}
    del _L2_gnn_all

    def _L3_gnn_setup():
        import jax, jax.numpy as jnp
        import numpy as np
        N_NODES = 3125
        N_EDGES = 50000
        IN_DIM = 128
        OUT_DIM = 128
        EDGE_DIM = 32
        EPS = 1e-05

        def _layernorm(h, gamma, beta):
            mu = jnp.mean(h, axis=-1, keepdims=True)
            var = jnp.var(h, axis=-1, keepdims=True)
            return (h - mu) * jax.lax.rsqrt(var + EPS) * gamma + beta
        key = jax.random.key(seed)
        ks = jax.random.split(key, 10)
        hid = OUT_DIM * 2
        x = jax.random.normal(ks[0], (N_NODES, IN_DIM), dtype=jnp.float32)
        edge_index = jax.random.randint(ks[1], (2, N_EDGES), 0, N_NODES, dtype=jnp.int64)
        edge_attr = jax.random.normal(ks[2], (N_EDGES, EDGE_DIM), dtype=jnp.float32)
        W1 = jax.random.normal(ks[3], (IN_DIM + EDGE_DIM, hid), dtype=jnp.float32) / np.sqrt(IN_DIM + EDGE_DIM)
        b1 = jnp.zeros((hid,), jnp.float32)
        g1 = jnp.ones((hid,), jnp.float32)
        be1 = jnp.zeros((hid,), jnp.float32)
        W2 = jax.random.normal(ks[4], (hid, OUT_DIM), dtype=jnp.float32) / np.sqrt(hid)
        b2 = jnp.zeros((OUT_DIM,), jnp.float32)
        Wu = jax.random.normal(ks[5], (IN_DIM + OUT_DIM, OUT_DIM), dtype=jnp.float32) / np.sqrt(IN_DIM + OUT_DIM)
        bu = jnp.zeros((OUT_DIM,), jnp.float32)
        gu = jnp.ones((OUT_DIM,), jnp.float32)
        beu = jnp.zeros((OUT_DIM,), jnp.float32)
        return {'x': x, 'edge_index': edge_index, 'edge_attr': edge_attr, 'W1': W1, 'b1': b1, 'g1': g1, 'be1': be1, 'W2': W2, 'b2': b2, 'Wu': Wu, 'bu': bu, 'gu': gu, 'beu': beu}
    _L3_gnn_all = _L3_gnn_setup()
    _L3_gnn_in = {k: v for k, v in _L3_gnn_all.items() if k in ('W1', 'b1', 'g1', 'be1', 'W2', 'b2', 'Wu', 'bu', 'gu', 'beu')}
    del _L3_gnn_all
    return {'x': x, 'src': src, 'dst': dst, 'edge_attr_32': edge_attr_32, 'edge_type_50': edge_type_50, 'L0_gnn_W': _L0_gnn_in['W'], 'L0_gnn_att_src': _L0_gnn_in['att_src'], 'L0_gnn_att_dst': _L0_gnn_in['att_dst'], 'L0_gnn_bias': _L0_gnn_in['bias'], 'L0_gnn_bn_gamma': _L0_gnn_in['bn_gamma'], 'L0_gnn_bn_beta': _L0_gnn_in['bn_beta'], 'L0_gnn_ln_gamma': _L0_gnn_in['ln_gamma'], 'L0_gnn_ln_beta': _L0_gnn_in['ln_beta'], 'L0_gnn_res_W': _L0_gnn_in['res_W'], 'L0_gnn_res_b': _L0_gnn_in['res_b'], 'L0_gnn_bnres_gamma': _L0_gnn_in['bnres_gamma'], 'L0_gnn_bnres_beta': _L0_gnn_in['bnres_beta'], 'L1_gnn_W': _L1_gnn_in['W'], 'L1_gnn_b': _L1_gnn_in['b'], 'L1_gnn_gamma': _L1_gnn_in['gamma'], 'L1_gnn_beta': _L1_gnn_in['beta'], 'L2_gnn_bases': _L2_gnn_in['bases'], 'L2_gnn_comps': _L2_gnn_in['comps'], 'L2_gnn_alpha': _L2_gnn_in['alpha'], 'L3_gnn_W1': _L3_gnn_in['W1'], 'L3_gnn_b1': _L3_gnn_in['b1'], 'L3_gnn_g1': _L3_gnn_in['g1'], 'L3_gnn_be1': _L3_gnn_in['be1'], 'L3_gnn_W2': _L3_gnn_in['W2'], 'L3_gnn_b2': _L3_gnn_in['b2'], 'L3_gnn_Wu': _L3_gnn_in['Wu'], 'L3_gnn_bu': _L3_gnn_in['bu'], 'L3_gnn_gu': _L3_gnn_in['gu'], 'L3_gnn_beu': _L3_gnn_in['beu']}

def reference(x, src, dst, edge_attr_32, edge_type_50, L0_gnn_W, L0_gnn_att_src, L0_gnn_att_dst, L0_gnn_bias, L0_gnn_bn_gamma, L0_gnn_bn_beta, L0_gnn_ln_gamma, L0_gnn_ln_beta, L0_gnn_res_W, L0_gnn_res_b, L0_gnn_bnres_gamma, L0_gnn_bnres_beta, L1_gnn_W, L1_gnn_b, L1_gnn_gamma, L1_gnn_beta, L2_gnn_bases, L2_gnn_comps, L2_gnn_alpha, L3_gnn_W1, L3_gnn_b1, L3_gnn_g1, L3_gnn_be1, L3_gnn_W2, L3_gnn_b2, L3_gnn_Wu, L3_gnn_bu, L3_gnn_gu, L3_gnn_beu):
    import jax
    import jax.numpy as jnp

    def _L0_gnn_ref(x, edge_index, W, att_src, att_dst, bias, bn_gamma, bn_beta, ln_gamma, ln_beta, res_W, res_b, bnres_gamma, bnres_beta):
        import jax, jax.numpy as jnp
        import numpy as np
        N, E, IN, H, C = (50000, 25000, 128, 4, 32)
        HC = H * C
        EPS = 1e-05
        NEG_SLOPE = 0.2

        def _bn(z, gamma, beta):
            mu = z.mean(0)
            var = z.var(0)
            return (z - mu) * jax.lax.rsqrt(var + EPS) * gamma + beta

        def _ln(z, gamma, beta):
            mu = z.mean(-1, keepdims=True)
            var = z.var(-1, keepdims=True)
            return (z - mu) * jax.lax.rsqrt(var + EPS) * gamma + beta
        n = x.shape[0]
        loops = jnp.tile(jnp.arange(n, dtype=edge_index.dtype), (2, 1))
        ei = jnp.concatenate([edge_index, loops], axis=1)
        src, dst = (ei[0], ei[1])
        h = (x @ W).reshape(n, H, C)
        a_src = (h * att_src).sum(-1)
        a_dst = (h * att_dst).sum(-1)
        alpha = a_src[src] + a_dst[dst]
        alpha = jnp.where(alpha >= 0, alpha, NEG_SLOPE * alpha)
        m = jax.ops.segment_max(alpha, dst, num_segments=n)
        ex = jnp.exp(alpha - m[dst])
        denom = jax.ops.segment_sum(ex, dst, num_segments=n)
        alpha = ex / denom[dst]
        msg = h[src] * alpha[..., None]
        out = jax.ops.segment_sum(msg, dst, num_segments=n).reshape(n, HC) + bias
        out = _bn(out, bn_gamma, bn_beta)
        out = _ln(out, ln_gamma, ln_beta)
        identity = _bn(x @ res_W + res_b, bnres_gamma, bnres_beta)
        return jax.nn.relu(out + identity)

    def _L1_gnn_ref(x, edge_index, W, b, gamma, beta):
        import jax, jax.numpy as jnp
        import numpy as np
        LN_EPS = 1e-05
        N = x.shape[0]
        loops = jnp.arange(N, dtype=edge_index.dtype)
        row = jnp.concatenate([edge_index[0], loops])
        col = jnp.concatenate([edge_index[1], loops])
        h = x @ W.T + b
        deg = jax.ops.segment_sum(jnp.ones(row.shape, dtype=h.dtype), row, num_segments=N)
        dis = deg ** (-0.5)
        norm = dis[row] * dis[col]
        msg = norm[:, None] * h[row]
        agg = jax.ops.segment_sum(msg, col, num_segments=N)
        out = jax.nn.relu(agg)
        mu = jnp.mean(out, axis=-1, keepdims=True)
        var = jnp.var(out, axis=-1, keepdims=True)
        out = (out - mu) * jax.lax.rsqrt(var + LN_EPS) * gamma + beta
        return out + x

    def _L2_gnn_ref(x, bases, comps, alpha, edge_index, edge_type):
        import jax, jax.numpy as jnp
        import numpy as np
        N_ENT = 512
        N_REL = 50
        D = 128
        B = 4
        E = 8192
        n = x.shape[0]
        row, col = (edge_index[0], edge_index[1])
        ones = jnp.ones(row.shape, x.dtype)
        deg = jax.ops.segment_sum(ones, row, num_segments=n)
        deg_inv = jnp.where(deg > 0, jax.lax.rsqrt(jnp.maximum(deg, 1.0)), 0.0)
        norm = deg_inv[row] * deg_inv[col]
        h_j = x[col]
        c_e = comps[edge_type]
        hj_b = c_e[:, :, None] * h_j[:, None, :]
        msg = jnp.einsum('ebd,bdf->ef', hj_b, bases)
        msg = msg * alpha[edge_type] * norm[:, None]
        out = jax.ops.segment_sum(msg, row, num_segments=n)
        return out

    def _L3_gnn_ref(x, edge_index, edge_attr, W1, b1, g1, be1, W2, b2, Wu, bu, gu, beu):
        import jax, jax.numpy as jnp
        import numpy as np
        N_NODES = 3125
        N_EDGES = 50000
        IN_DIM = 128
        OUT_DIM = 128
        EDGE_DIM = 32
        EPS = 1e-05

        def _layernorm(h, gamma, beta):
            mu = jnp.mean(h, axis=-1, keepdims=True)
            var = jnp.var(h, axis=-1, keepdims=True)
            return (h - mu) * jax.lax.rsqrt(var + EPS) * gamma + beta
        row, col = (edge_index[0], edge_index[1])
        msg_in = jnp.concatenate([x[row], edge_attr], axis=-1)
        h = msg_in @ W1 + b1
        h = jax.nn.gelu(_layernorm(h, g1, be1), approximate=False)
        msg = h @ W2 + b2
        agg = jax.ops.segment_sum(msg, col, num_segments=x.shape[0])
        u = jnp.concatenate([x, agg], axis=-1) @ Wu + bu
        u = jax.nn.gelu(_layernorm(u, gu, beu), approximate=False)
        return u + x
    edge_index = jnp.stack([src, dst])
    x = _layernorm(x + _L0_gnn_ref(x, edge_index, L0_gnn_W, L0_gnn_att_src, L0_gnn_att_dst, L0_gnn_bias, L0_gnn_bn_gamma, L0_gnn_bn_beta, L0_gnn_ln_gamma, L0_gnn_ln_beta, L0_gnn_res_W, L0_gnn_res_b, L0_gnn_bnres_gamma, L0_gnn_bnres_beta), axis=-1)
    x = _layernorm(x + _L1_gnn_ref(x, edge_index, L1_gnn_W, L1_gnn_b, L1_gnn_gamma, L1_gnn_beta), axis=-1)
    x = _layernorm(x + _L2_gnn_ref(x, L2_gnn_bases, L2_gnn_comps, L2_gnn_alpha, edge_index, edge_type_50), axis=-1)
    x = _layernorm(x + _L3_gnn_ref(x, edge_index, edge_attr_32, L3_gnn_W1, L3_gnn_b1, L3_gnn_g1, L3_gnn_be1, L3_gnn_W2, L3_gnn_b2, L3_gnn_Wu, L3_gnn_bu, L3_gnn_gu, L3_gnn_beu), axis=-1)
    return x

_drawn_inputs = setup_inputs


def setup_inputs(seed=0):
    import zlib

    import numpy as np

    out = dict(_drawn_inputs(seed))
    spreads = {'L0_gnn_bias': (0.0, 0.8),
     'L0_gnn_bn_gamma': (1.0, 0.2),
     'L0_gnn_bn_beta': (0.0, 0.1),
     'L0_gnn_ln_gamma': (1.0, 0.2),
     'L0_gnn_ln_beta': (0.0, 0.1),
     'L0_gnn_res_b': (0.0, 0.8),
     'L0_gnn_bnres_gamma': (1.0, 0.2),
     'L0_gnn_bnres_beta': (0.0, 0.1),
     'L1_gnn_gamma': (1.0, 0.2),
     'L1_gnn_beta': (0.0, 0.1),
     'L3_gnn_b1': (0.0, 0.1),
     'L3_gnn_g1': (1.0, 0.2),
     'L3_gnn_be1': (0.0, 0.1),
     'L3_gnn_b2': (0.0, 0.1),
     'L3_gnn_bu': (0.0, 0.8),
     'L3_gnn_gu': (1.0, 0.2),
     'L3_gnn_beu': (0.0, 0.1)}
    factors = {}
    for name, (base, spread) in spreads.items():
        noise = np.random.default_rng([zlib.crc32(name.encode()), seed]).standard_normal(out[name].shape)
        drawn = base * np.exp(spread * noise) if base else spread * noise
        out[name] = jnp.asarray(drawn.astype(out[name].dtype))
    for name, factor in factors.items():
        out[name] = (out[name] * factor).astype(out[name].dtype)
    return out
```

```python
from contextlib import ExitStack

import concourse.bass as bass
from concourse import mybir

F32 = mybir.dt.float32
BF16 = mybir.dt.bfloat16
F16 = mybir.dt.float16
I32 = mybir.dt.int32
ALU = mybir.AluOpType
ACT = mybir.ActivationFunctionType
AX_X = mybir.AxisListType.X
ENG = mybir.EngineType

P = 128
N, E, D = 3125, 103125, 128
HEADS, HC = 4, 32
EDIM, HID = 32, 256
REL, BASES = 50, 4
NT = -(-N // P)
LAST = N - (NT - 1) * P
NPAD = NT * P
PAD_NODE = NPAD - 1
ET = -(-E // P)
SLOTS = ET + NT - 1
SG = -(-SLOTS // P)
SPAD = SG * P
RING = 10
HALF = RING // 2
ITER = SLOTS // RING
assert ITER * RING == SLOTS
MS = 5
COLS0 = D + 2 * HEADS + 1
COLS3 = HID + 1
NACC = 5
TRASH = NPAD
ACC_ROWS = NPAD + P
BIG = 1e30
EPS = 1e-5
STAGES = ["slots_made", "rows_made", "att_made", "a_zeros", "edge_values", "slot_max_made", "carries_made",
          "max_made", "ex_argument", "loop_argument", "l0_attention_out", "x1_made", "l1_h_copied", "h1_made",
          "zeros_made", "scatter_rows_made", "l2_scaled", "l2_y_parts", "l2_coef_tail", "x3_made",
          "l3_w1_centered", "p_made", "u_normed", "out_made"]
STAGE = {name: n + 1 for n, name in enumerate(STAGES)}
VECS = ["att_src", "att_dst", "bias", "bn_g", "bn_b", "ln_g", "ln_b", "res_b", "bnres_g", "bnres_b",
        "b_l1", "g_l1", "be_l1", "bu", "gu", "beu"]


def gnn_stack(nc, x, src_t, dst_t, typ_t, attr_t, W0, resW, vec, W1T, bases, comps, alpha, W1x, W1e, b1, g1, be1,
              W2, b2, Wu, out, layers=4):
    with ExitStack() as ctx:
        def sb(name, shape, dt=F32):
            return ctx.enter_context(nc.sbuf_tensor(name, shape, dt))

        def sem(name):
            return ctx.enter_context(nc.semaphore(name))

        events = {}

        def ev(name):
            if name not in events:
                events[name] = sem(name)
            return events[name]

        h_dram = nc.dram_tensor("h_dram", (NPAD, D), F32, kind="Internal").ap()
        as_dram = nc.dram_tensor("as_dram", (NPAD, HEADS), F32, kind="Internal").ap()
        p_dram = nc.dram_tensor("p_dram", (NPAD, HID), F32, kind="Internal").ap()
        slot_dram = [nc.dram_tensor(f"slot_dram{k}", (SPAD, 1), I32, kind="Internal").ap() for k in range(2)]
        acc_dram = [nc.dram_tensor(f"acc_dram{k}", (ACC_ROWS, D), F32, kind="Internal").ap() for k in range(NACC)]

        X = sb("X", [P, NT, D])
        H = sb("H", [P, NT, D])
        ACCB = sb("ACCB", [P, NT * COLS3])
        T12 = sb("T12", [P, SPAD * 8])
        T1 = T12[:, 0:NT * D].rearrange("p (t f) -> p t f", f=D)
        T2 = T12[:, NT * D:2 * NT * D].rearrange("p (t f) -> p t f", f=D)
        ACC0 = ACCB[:, 0:NT * COLS0].rearrange("p (t f) -> p t f", f=COLS0)
        ACC1 = ACCB[:, 0:NT * D].rearrange("p (t f) -> p t f", f=D)
        ACC1B = ACCB[:, NT * D:2 * NT * D].rearrange("p (t f) -> p t f", f=D)
        ACC3 = ACCB[:, :].rearrange("p (t f) -> p t f", f=COLS3)
        ARENA = sb("ARENA", [P, SPAD * 21])

        def carve(buf, at, *dims):
            n = 1
            for d in dims:
                n *= d
            names = "abcd"[:len(dims)]
            return buf[:, at:at + n].rearrange("p (" + " ".join(names) + ") -> p " + " ".join(names),
                                               **dict(zip(names[1:], dims[1:])))

        AS = carve(ARENA, 0, SPAD, 4)
        ADAS = carve(ARENA, SPAD * 4, SPAD, 8)
        EXF = carve(ARENA, SPAD * 12, SPAD, 9)
        DR, SR, TR, DL, HI, LO, VALID, FIRST, SPARE = [carve(ARENA, SPAD * (12 + k), SG, P) for k in range(9)]
        RI = T12[:, 0:3 * SPAD].bitcast(I32).rearrange("p (k g l) -> p k g l", k=3, l=P)
        HII = T12[:, 3 * SPAD:4 * SPAD].bitcast(I32).rearrange("p (g l) -> p g l", l=P)
        HIC, LOC = ACCB[:, 0:SPAD], ACCB[:, SPAD:2 * SPAD]
        OHA = carve(ACCB[:, 2 * SPAD:2 * SPAD + RING * 64].bitcast(BF16), 0, 2, HALF, P)
        LOA = carve(ACCB[:, 2 * SPAD + RING * 64:2 * SPAD + RING * 128].bitcast(BF16), 0, 2, HALF, P)
        HIA = carve(ACCB[:, 2 * SPAD + RING * 128:2 * SPAD + RING * 141].bitcast(BF16), 0, 2, HALF, 26)
        OTA = carve(ACCB, 2 * SPAD + RING * 141, 2, HALF, P)
        VT, AT = carve(T12, 0, SG, HEADS, P), carve(T12, SPAD * 4, SG, HEADS, P)
        FT = carve(ACCB, 0, SG, HEADS, P)
        MT = carve(ACCB, 0, SPAD, HEADS)
        FIRSTC = T12[:, SPAD * 4:SPAD * 5]
        R_FM, R_LM, R_FD, R_LD, R_LINK, R_W = [ARENA[0:HEADS, SPAD * (12 + k):SPAD * (13 + k)] for k in (1, 2, 3, 4, 5, 8)]
        R_CF, R_CB, R_A = [ACCB[0:HEADS, SPAD * (4 + k):SPAD * (5 + k)] for k in range(3)]
        R_OUT = R_LD
        MSG0 = carve(ARENA, 0, MS, COLS0)
        COEF = carve(ARENA, 0, SPAD, BASES)
        YP = [carve(b[:, o:o + NT * 2 * D].bitcast(BF16), 0, NT, BASES * D)
              for b, o in ((ARENA, SPAD * 4), (ARENA, SPAD * 4 + NT * 2 * D), (ACCB, 0))]
        YREST = carve(H[:, 0:8, :].rearrange("p a b -> p (a b)"), 0, 2, BASES * D)
        l1r = SPAD * 4
        OHT = carve(ARENA[:, l1r:l1r + RING * 64].bitcast(BF16), 0, 2, HALF, P)
        OTT = carve(ARENA, l1r + RING * 64, 2, HALF, P)
        DUP = carve(ARENA, l1r + RING * 192, 2, HALF)
        NDUP = carve(ARENA, l1r + RING * 193, 2, HALF)
        SRCST = carve(ARENA, l1r + RING * 194, 2, HALF)
        JUNK = carve(ARENA, l1r + RING * 195, 2, P)
        l2r = SPAD * 4 + NT * BASES * D
        OH2 = carve(ARENA[:, l2r:l2r + P].bitcast(BF16), 0, 2, P)
        OT2 = carve(ARENA[:, l2r + P:l2r + 2 * P].bitcast(BF16), 0, 2, P)
        MSG2L = carve(ARENA, l2r + 2 * P, 2, P)
        EQ = carve(ARENA, l2r + 4 * P, 2, P)
        MSG2 = carve(ARENA, l2r + 6 * P, 2, P)
        SRC2 = ARENA[:, l2r + 8 * P:l2r + 8 * P + 1].bitcast(F16)
        PN = carve(ARENA, 0, NT, HID)
        l3r = NT * HID
        GR3 = carve(ARENA, l3r, RING, HID)
        HC3 = carve(ARENA, l3r + RING * HID, RING, HID)
        ZB = carve(ARENA, l3r + 2 * RING * HID, MS, HID)
        GE = carve(ARENA, l3r + 2 * RING * HID + MS * HID, MS, COLS3)
        A3 = carve(ARENA, l3r + 3 * RING * HID + MS * HID, RING, P)
        SQ = carve(ARENA, l3r + 4 * RING * HID, 2, HID)
        DLC = sb("DLC", [P, SPAD])
        SRC = sb("SRC", [P, SPAD])
        SRCI = sb("SRCI", [P, SPAD], I32)
        TYC = sb("TYC", [P, SPAD])
        SCI = ARENA[:, SPAD * 20:SPAD * 21].bitcast(I32)
        ttab = sb("ttab", [1, 2, SPAD], I32)
        iota = sb("iota", [P, P])
        iotab = sb("iotab", [P, P], BF16)
        pcol = sb("pcol", [P, 1])
        trashcol = sb("trashcol", [P, 1])
        ident = sb("ident", [P, P])
        identb = sb("identb", [P, P], BF16)
        identh = sb("identh", [P, P], F16)
        tri = sb("tri", [P, P])
        ones = sb("ones", [P, P])
        VEC = sb("VEC", [P, len(VECS), D])
        B1 = sb("B1", [P, HID])
        G1 = sb("G1", [P, HID])
        BE1 = sb("BE1", [P, HID])
        b2c = sb("b2c", [P, 1])
        B2U = sb("B2U", [P, D])
        W0s = sb("W0s", [P, D])
        resWs = sb("resWs", [P, D])
        W1Ts = sb("W1Ts", [P, D])
        bas = sb("bas", [P, BASES, D])
        coef = sb("coef", [REL, BASES + 1])
        W1xs = sb("W1xs", [P, HID])
        W1es = sb("W1es", [EDIM, HID])
        W2s = sb("W2s", [P, 2, D])
        W2T = carve(ARENA, SPAD * 20, 2, D)
        W2U = carve(ARENA, SPAD * 20 + 2 * D, 2, D)
        Wus = sb("Wus", [P, 2, D])
        ADN = sb("ADN", [P, NT, 8])
        SMN = sb("SMN", [P, 4, NT, 4])
        DIS = sb("DIS", [P, 2, NT])
        HAS = sb("HAS", [P, NT])
        stat = sb("stat", [P, 4, P])
        jcol = sb("jcol", [P, SG])
        slots = sb("slots", [P, 3, SG])
        sloti = sb("sloti", [P, 2, SG], I32)
        jend = carve(T12, SPAD * 5, 2, ET)
        jendi = carve(ACCB[:, 0:2 * ET].bitcast(I32), 0, 2, ET)
        carry = sb("carry", [P, 3, SG, HEADS])
        wsum = sb("wsum", [P, 4])
        SS = sb("SS", [P, 4, RING])
        istage = sb("istage", [P, 2, HALF], I32)
        GR = sb("GR", [P, RING, D])
        OH = sb("OH", [P, MS, P])

        WIDE = ctx.enter_context(nc.psum_tensor("WIDE", [P, 7 * 512], F32))
        LASTB = ctx.enter_context(nc.psum_tensor("LASTB", [P, 512], F32))

        def bank(b, n=512):
            return LASTB[:, 0:n] if b == 7 else WIDE[:, b * 512:b * 512 + n]

        NODES = WIDE[:, 0:NT * D].rearrange("p (t f) -> p t f", f=D)

        def V(name):
            return VEC[:, VECS.index(name), :]

        def over_tiles(v):
            return v.unsqueeze(1).broadcast_to([P, NT, v.shape[-1]])

        def over_features(v, n=D):
            return v.unsqueeze(2).broadcast_to([P, v.shape[1], n])

        landed = [sem(f"gather_landed{q}") for q in range(RING)]
        attr_landed = [sem(f"attr_landed{q}") for q in range(RING)]
        weights_loaded = sem("weights_loaded")
        stage_done = sem("stage_done")
        dve_step, act_step, pool_step = sem("dve_step"), sem("act_step"), sem("pool_step")
        var_ready, dev_ready = sem("var_ready"), sem("dev_ready")
        bn_in, bn_sums = sem("bn_in"), sem("bn_sums")
        WLOADS = 14 + len(VECS)

        class Chain:

            def __init__(self, eng, s):
                self.eng, self.s, self.n = eng, s, 0

            def __call__(self, ins):
                ins.then_inc(self.s, 1)
                self.n += 1
                self.eng.wait_ge(self.s, self.n)

        ctx.enter_context(nc.allow_non_contiguous_dma(reason="columns of the slot tables, once"))
        block = ctx.enter_context(nc.Block())

        def tile_registers(engine, i, ahead=0):
            return nc.values_load_multi_w_load_instructions(
                ttab[0:1, 1, bass.ds(i * RING + ahead, RING)], engines=[engine], min_val=0, max_val=NT - 1,
                skip_runtime_bounds_check_because="the slot table is clamped to the node tiles when it is made")[1]

        @block.sync
        def _(sp):
            def store_nodes(table, tile):
                return sp.dma_start(table.rearrange("(t p) f -> p t f", p=P), tile)

            sp.dma_start(jendi[0:1, 0, :], dst_t[:, P - 1:P].rearrange("t a -> a t")).then_inc(ev("ends_loaded"), 16)
            sp.wait_ge(ev("x_padding_zero"), 1)
            sp.dma_start(X[:, 0:NT - 1, :], x[0:(NT - 1) * P, :].rearrange("(t p) f -> p t f", p=P)).then_inc(ev("x_loaded"), 16)
            sp.dma_start(X[0:LAST, NT - 1, :], x[(NT - 1) * P:N, :]).then_inc(ev("x_loaded"), 16)
            w = [(W0s[:, :], W0), (resWs[:, :], resW), (W1Ts[:, :], W1T),
                 (bas[:, :, :], bases.rearrange("b d f -> d b f")),
                 (coef[:, 0:BASES], comps), (coef[:, BASES:BASES + 1], alpha),
                 (W1xs[:, :], W1x), (W1es[:, :], W1e),
                 (W2s[:, :, :], W2.rearrange("(k p) f -> p k f", p=P)),
                 (Wus[:, :, :], Wu.rearrange("(k p) f -> p k f", p=P)),
                 (B1[:, :], b1.partition_broadcast(P)), (G1[:, :], g1.partition_broadcast(P)),
                 (BE1[:, :], be1.partition_broadcast(P)), (b2c[:, :], b2.unsqueeze(1))]
            w += [(VEC[:, k, :], vec[name].partition_broadcast(P)) for k, name in enumerate(VECS)]
            assert len(w) == WLOADS
            for dst, s in w:
                sp.dma_start(dst, s).then_inc(weights_loaded, 16)
            sp.wait_ge(stage_done, STAGE["slots_made"])
            for k in range(2):
                sp.dma_start(slot_dram[k].rearrange("(g p) a -> p (g a)", p=P), sloti[:, k, :]).then_inc(ev("slots_stored"), 16)
            sp.wait_ge(ev("slots_stored"), 32)
            for k in range(2):
                sp.dma_start(ttab[0:1, k, :], slot_dram[k].rearrange("s a -> a s")).then_inc(ev("slots_loaded"), 16)
            sp.wait_ge(stage_done, STAGE["att_made"])
            store_nodes(as_dram, ADN[:, :, 4:8]).then_inc(ev("as_stored"), 16)
            store_nodes(h_dram, H[:, :, :]).then_inc(ev("h0_stored"), 16)
            if layers > 1:
                sp.wait_ge(stage_done, STAGE["h1_made"])
                store_nodes(h_dram, H[:, :, :]).then_inc(ev("h1_stored"), 16)
            if layers > 2:
                sp.wait_ge(stage_done, STAGE["zeros_made"])
                for k in range(NACC):
                    sp.dma_start(acc_dram[k].rearrange("(t p) f -> p t f", p=P),
                                 carve(T12, 0, NT + 1, D)).then_inc(ev("acc_zero_stored"), 16)
                sp.wait_ge(ev("scatters_done"), 1)
                for k, dst in enumerate([T1, T2, ACC1, ACC1B, H[:, :, :]]):
                    sp.dma_start(dst, acc_dram[k][0:NPAD, :].rearrange("(t p) f -> p t f", p=P)).then_inc(ev("acc_loaded"), 16)
            if layers > 3:
                sp.wait_ge(stage_done, STAGE["p_made"])
                store_nodes(p_dram, PN).then_inc(ev("p_stored"), 16)
                with sp.Fori(0, ITER) as i:
                    tiles = nc.values_load_multi_w_load_instructions(
                        ttab[0:1, 0, bass.ds(i * RING, RING)], engines=[ENG.SP], min_val=0, max_val=ET - 1,
                        skip_runtime_bounds_check_because="the slot table is clamped to the edge tiles when it is made")[1]
                    for q in range(RING):
                        sp.wait_ge(ev("l3_edge_part"), i * RING + q + 1)
                        sp.dma_start(A3[0:EDIM, q, :], attr_t[bass.ds(tiles[q], 1), :].rearrange("a (f e) -> (a f) e", f=EDIM)
                                     ).then_inc(attr_landed[q], 16)
            sp.wait_ge(stage_done, STAGE["out_made"])
            sp.dma_start(out[0:(NT - 1) * P, :].rearrange("(t p) f -> p t f", p=P), X[:, 0:NT - 1, :]).then_inc(ev("out_stored"), 16)
            sp.dma_start(out[(NT - 1) * P:N, :], X[0:LAST, NT - 1, :]).then_inc(ev("out_stored"), 16)
            sp.wait_ge(ev("out_stored"), 32)

        @block.gpsimd
        def _(pool):
            pool.iota(iota[:, :], pattern=[[1, P]], base=0, channel_multiplier=0,
                      allow_small_or_imprecise_dtypes=True).then_inc(ev("iotas"), 1)
            pool.iota(pcol[:, :], pattern=[[0, 1]], base=0, channel_multiplier=1,
                      allow_small_or_imprecise_dtypes=True).then_inc(ev("iotas"), 1)
            pool.iota(jcol[:, :], pattern=[[P, SG]], base=0, channel_multiplier=1,
                      allow_small_or_imprecise_dtypes=True).then_inc(ev("iotas"), 1)
            pool.iota(jend[0:1, 1, :], pattern=[[1, ET]], base=0, channel_multiplier=0,
                      allow_small_or_imprecise_dtypes=True).then_inc(ev("iotas"), 1)
            pool.wait_ge(stage_done, STAGE["slots_made"])
            for k, table in enumerate((dst_t, src_t, typ_t)):
                for g in range(SG):
                    pool.indirect_dma_start(RI[:, k, g, :], None, table[:, :],
                                            bass.IndirectOffsetOnAxis(ap=sloti[:, 0, g:g + 1], axis=0)
                                            ).then_inc(ev("rows_gathered"), 16)

            def carry_waits():
                pool.sem_inc(ev("pool_waits_met"), 1)

            def gather_loop(name, table, ring, free):
                staged = sem(name + "_indices_staged")
                with pool.Fori(0, ITER) as i:
                    for h in range(2):
                        pool.wait_ge(free, i * RING + (h + 1) * HALF)
                        pool.tensor_copy(istage[:, h, :], SRCI[:, bass.ds(i * RING + h * HALF, HALF)]).then_inc(staged, 1)
                        pool.wait_ge(staged, i * 2 + h + 1)
                        carry_waits()
                        for k in range(HALF):
                            q = h * HALF + k
                            pool.indirect_dma_start(ring[:, q, :], None, table[:, :],
                                                    bass.IndirectOffsetOnAxis(ap=istage[:, h, k:k + 1], axis=0)
                                                    ).then_inc(landed[q], 16)

            pool.wait_ge(ev("column_copied"), 5)
            pool.wait_ge(ev("as_stored"), 16)
            gather_loop("a", as_dram, GR[:, :, 0:HEADS], ev("a_ring_free"))
            pool.wait_ge(ev("h0_stored"), 16)
            gather_loop("l0", h_dram, GR[:, :, :], ev("l0_messages"))
            if layers > 1:
                pool.wait_ge(ev("h1_stored"), 16)
                gather_loop("l1", h_dram, GR[:, :, :], ev("l1_sums"))
            if layers > 2:
                base = 3 * ITER * 16
                staged = sem("l2_indices_staged")
                pool.wait_ge(ev("acc_zero_stored"), 16 * NACC)
                pool.wait_ge(stage_done, STAGE["scatter_rows_made"])
                with pool.Fori(0, ITER) as i:
                    for h in range(2):
                        for q in range(h * HALF, (h + 1) * HALF):
                            pool.wait_ge(landed[q], i * 16 + base)
                        pool.tensor_copy(istage[:, h, :], SCI[:, bass.ds(i * RING + h * HALF, HALF)]).then_inc(staged, 1)
                        pool.wait_ge(staged, i * 2 + h + 1)
                        for k in range(HALF):
                            q = h * HALF + k
                            pool.wait_ge(ev("l2_sum_copied"), i * RING + q + 3)
                            pool.wait_ge(landed[(q + NACC) % RING], i * 16 + base + (16 if q >= NACC else 0))
                            carry_waits()
                            pool.indirect_dma_start(acc_dram[q % NACC][:, :],
                                                    bass.IndirectOffsetOnAxis(ap=istage[:, h, k:k + 1], axis=0),
                                                    GR[:, q, :], None, compute_op=ALU.add).then_inc(landed[q], 16)
                for q in range(RING):
                    pool.wait_ge(landed[q], base + ITER * 16)
                pool.sem_inc(ev("scatters_done"), 1)
            if layers > 3:
                pool.wait_ge(ev("p_stored"), 16)
                gather_loop("l3", p_dram, GR3, ev("l3_ring_free"))

        @block.tensor
        def _(pe):
            def transpose_nodes(tile):
                for t in range(NT):
                    last = pe.transpose(NODES[:, t, :], tile[:, t, :], ident[:, :])
                return last

            def project(tile_t, w):
                for t in range(NT):
                    last = pe.matmul(NODES[:, t, :], tile_t[:, t, :], w, start=True, stop=True)
                return last

            def node_sums(tile, n):
                pe.wait_ge(bn_in, n)
                for t in range(NT):
                    k = P if t < NT - 1 else LAST
                    last = pe.matmul(bank(7, D), ones[0:k, :], tile[0:k, t, :], start=(t == 0), stop=(t == NT - 1))
                last.then_inc(bn_sums, 1)

            pe.wait_ge(ev("ends_made"), 1)
            for a in range(0, ET, 512):
                n = min(512, ET - a)
                last = pe.matmul(WIDE[:, a:a + n], ones[0:1, :], jend[0:1, 0, a:a + n], start=True, stop=True)
            last.then_inc(ev("ends_spread"), 1)
            for n, (arr, b) in enumerate([(DL, 2), (SR, 4), (TR, 0), (HI, 2), (LO, 4)]):
                pe.wait_ge(stage_done, STAGE["rows_made"])
                if n >= 3:
                    pe.wait_ge(ev("column_copied"), n - 2)
                for g in range(SG):
                    last = pe.transpose(WIDE[:, b * 512 + g * P:b * 512 + (g + 1) * P], arr[:, g, :], ident[:, :])
                last.then_inc(ev("column_turned"), 1)
            pe.wait_ge(ev("x_loaded"), 32)
            pe.wait_ge(ev("column_copied"), 5)
            transpose_nodes(X).then_inc(ev("l0_xt"), 1)
            pe.wait_ge(ev("l0_xt_copied"), 1)
            pe.wait_ge(weights_loaded, 16 * WLOADS)
            project(T1, W0s[:, :]).then_inc(ev("l0_h"), 1)
            pe.wait_ge(stage_done, STAGE["a_zeros"])
            pe.wait_ge(stage_done, STAGE["att_made"])
            pe.matmul(bank(7, NT), ones[:, :], OTA[:, 0, 0, 0:NT], start=True, stop=False, skip_group_check=True
                      ).then_inc(ev("deg_cleared"), 1)
            pe.wait_ge(ev("deg_cleared"), 1)
            pe.sem_inc(ev("deg_ready"), 1)
            pe.wait_ge(ev("slots_loaded"), 32)
            pe.sem_inc(ev("a_turned"), 2)
            pe.sem_inc(ev("a_onehot_read"), 2)
            pe.sem_inc(ev("a_adas"), 2)
            with pe.Fori(0, ITER) as i:
                ts = tile_registers(ENG.PE, i)
                for h in range(2):
                    n = i * 2 + h + 1
                    pe.wait_ge(ev("a_onehot"), n)
                    pe.wait_ge(ev("a_turned_copied"), n)
                    for k in range(HALF):
                        last = pe.transpose(bank(h).bitcast(BF16)[:, k * P:(k + 1) * P], OHA[:, h, k, :], identb[:, :])
                    last.then_inc(ev("a_turned"), 1)
                    for k in range(HALF):
                        last = pe.matmul(bank(7, NT), LOA[:, h, k, :], HIA[:, h, k, 0:NT], start=False, stop=False,
                                         skip_group_check=True)
                    last.then_inc(ev("a_onehot_read"), 1)
                    pe.wait_ge(ev("a_turned_copied"), n + 2)
                    pe.wait_ge(ev("a_adas_copied"), n)
                    for k in range(HALF):
                        last = pe.matmul(bank(2 + h)[:, k * 8:(k + 1) * 8], OTA[:, h, k, :],
                                         ADN[:, bass.ds(ts[h * HALF + k], 1), :].rearrange("p a b -> p (a b)"),
                                         start=True, stop=True)
                    last.then_inc(ev("a_adas"), 1)
            pe.wait_ge(stage_done, STAGE["edge_values"])
            for hd in range(HEADS):
                if hd >= 2:
                    pe.wait_ge(ev("as_row_copied"), hd - 1)
                for g in range(SG):
                    last = pe.transpose(WIDE[:, (hd % 2) * 1024 + g * P:(hd % 2) * 1024 + (g + 1) * P],
                                        AS[:, g * P:(g + 1) * P, hd], ident[:, :])
                last.then_inc(ev("as_row"), 1)
            pe.wait_ge(stage_done, STAGE["slot_max_made"])
            for n in range(4):
                if n >= 2:
                    pe.wait_ge(ev("end_row_copied"), n - 1)
                for g in range(SG):
                    lane = 0 if n % 2 == 0 else P - 1
                    in_ = VT[:, g, :, lane] if n < 2 else DR[:, g, lane:lane + 1].broadcast_to([P, HEADS])
                    last = pe.transpose(WIDE[0:HEADS, (n % 2) * 1024 + g * P:(n % 2) * 1024 + (g + 1) * P], in_, ident[:, :])
                last.then_inc(ev("end_row"), 1)
            pe.wait_ge(stage_done, STAGE["carries_made"])
            for n, row in enumerate((R_CF, R_CB, R_LINK)):
                for g in range(SG):
                    last = pe.transpose(WIDE[:, 3072 + (n * SG + g) * HEADS:3072 + (n * SG + g + 1) * HEADS],
                                        row[:, g * P:(g + 1) * P], ident[0:HEADS, 0:HEADS])
            last.then_inc(ev("carries_turned"), 1)
            pe.wait_ge(stage_done, STAGE["max_made"])
            for n in range(HEADS + 1):
                if n >= 2:
                    pe.wait_ge(ev("max_copied"), n - 1)
                for g in range(SG):
                    in_ = VT[:, g, n, :] if n < HEADS else FIRST[:, g, :]
                    last = pe.transpose(WIDE[:, (n % 2) * 1024 + g * P:(n % 2) * 1024 + (g + 1) * P], in_, ident[:, :])
                last.then_inc(ev("max_turned"), 1)

            pe.wait_ge(ev("max_copied"), HEADS + 1)
            pe.sem_inc(ev("l0_sums"), RING)
            with pe.Fori(0, ITER) as i:
                for q in range(RING):
                    j = i * RING + q
                    pe.wait_ge(ev("l0_sums_added"), j + 1)
                    pe.wait_ge(ev("l0_messages"), j + 1 + RING)
                    pe.matmul(bank(q % MS, COLS0), OH[:, q % MS, :], MSG0[:, q % MS, :], start=True, stop=True
                              ).then_inc(ev("l0_sums"), 1)
            node_sums(T1, 1)
            node_sums(T1, 2)
            pe.wait_ge(stage_done, STAGE["l0_attention_out"])
            transpose_nodes(X).then_inc(ev("l0_xt2"), 1)
            pe.wait_ge(ev("l0_xt2_copied"), 1)
            project(ACC1, resWs[:, :]).then_inc(ev("l0_res"), 1)
            node_sums(H, 3)
            node_sums(H, 4)
            if layers > 1:
                pe.wait_ge(stage_done, STAGE["x1_made"])
                transpose_nodes(X).then_inc(ev("l1_xt"), 1)
                pe.wait_ge(ev("l1_xt_copied"), 1)
                project(T1, W1Ts[:, :]).then_inc(ev("l1_h"), 1)
                pe.wait_ge(stage_done, STAGE["l1_h_copied"])
                pe.sem_inc(ev("l1_sums"), RING)
                pe.sem_inc(ev("l1_types_turned"), 2)
                pe.sem_inc(ev("l1_coefs"), 2)
                pe.sem_inc(ev("l1_sources"), 2)
                with pe.Fori(0, ITER) as i:
                    for h in range(2):
                        n = i * 2 + h + 1
                        pe.wait_ge(ev("l1_type_onehot"), n)
                        pe.wait_ge(ev("l1_types_copied"), n)
                        for k in range(HALF):
                            last = pe.transpose(bank(5 + h).bitcast(BF16)[:, k * P:(k + 1) * P], OHT[:, h, k, :], identb[:, :])
                        last.then_inc(ev("l1_types_turned"), 1)
                        for k in range(HALF):
                            q = h * HALF + k
                            j = i * RING + q
                            pe.wait_ge(ev("l1_repeats"), j + 1)
                            pe.matmul(bank(2 + q % 2, P), SRCST[:, h, k:k + 1].broadcast_to([P, P]),
                                      ident[:, :], start=True, stop=True).then_inc(ev("l1_sources"), 1)
                            pe.wait_ge(ev("l1_sums_added"), j + 1)
                            pe.wait_ge(ev("l1_onehot"), j + 1)
                            pe.wait_ge(landed[q], i * 16 + (2 * ITER * 16 + 16))
                            pe.matmul(bank(q % 2, D), OH[:, q % MS, :], GR[:, q, :], start=True, stop=True
                                      ).then_inc(ev("l1_sums"), 1)
                        pe.wait_ge(ev("l1_types_copied"), n + 2)
                        pe.wait_ge(ev("l1_coefs_copied"), n)
                        for k in range(HALF):
                            c = k * BASES
                            last = pe.matmul(bank(4 + 3 * h)[:, c:c + BASES], OTT[0:REL, h, k, :], coef[:, 0:BASES], start=True, stop=True)
                        last.then_inc(ev("l1_coefs"), 1)
            if layers > 2:
                pe.wait_ge(stage_done, STAGE["l2_scaled"])
                transpose_nodes(T1).then_inc(ev("l2_xt"), 1)
                pe.wait_ge(ev("l2_xt_copied"), 1)
                for t in range(NT):
                    if t >= 4:
                        pe.wait_ge(ev("l2_y_copied"), t - 3)
                    pe.matmul(bank(t % 4), T2[:, t, :], bas[:, :, :].rearrange("p b f -> p (b f)"), start=True, stop=True
                              ).then_inc(ev("l2_y"), 1)
                pe.wait_ge(stage_done, STAGE["l2_y_parts"])
                for name in ("l2_turned", "l2_gathered", "l2_summed"):
                    pe.sem_inc(ev(name), 2)

                def turn(j, r):
                    pe.wait_ge(ev("l2_onehot"), j + 3)
                    pe.wait_ge(ev("l2_turned_copied"), j + 1)
                    pe.wait_ge(ev("l2_equal"), j + 1)
                    pe.transpose(bank(r, 64).bitcast(BF16), OH2[:, r, :], identb[:, :])
                    pe.matmul(bank(6 + r, P), SRC2[:, r:r + 1].broadcast_to([P, P]), identh[:, :], start=True, stop=True
                              ).then_inc(ev("l2_turned"), 1)

                def gather(j, r, t):
                    pe.wait_ge(ev("l2_turned_copied"), j + 3)
                    pe.wait_ge(ev("l2_mixed"), j + 1)
                    pe.wait_ge(ev("l2_sum_copied"), j + 1)
                    for k, part in enumerate(YP):
                        pe.matmul(bank(2 + r, 3 * D), OT2[:, r, :], part[:, bass.ds(t, 1), 0:3 * D].rearrange("p a b -> p (a b)"),
                                  start=(k == 0), stop=(k == 2))
                    for k, part in enumerate(YP):
                        last = pe.matmul(bank(4 + r, D), OT2[:, r, :],
                                         part[:, bass.ds(t, 1), 3 * D:4 * D].rearrange("p a b -> p (a b)"),
                                         start=(k == 0), stop=(k == 2))
                    last.then_inc(ev("l2_gathered"), 1)

                turn(0, 0)
                turn(1, 1)
                gather(0, 0, tile_registers(ENG.PE, 0)[0])
                with pe.Fori(0, ITER) as i:
                    ts = tile_registers(ENG.PE, i, 1)
                    for q in range(RING):
                        j = i * RING + q
                        r = q % 2
                        gather(j + 1, 1 - r, ts[q])
                        pe.wait_ge(ev("l2_mixed"), j + 3)
                        pe.wait_ge(ev("l2_mixed_last"), j + 3)
                        pe.wait_ge(ev("l2_equal"), j + 3)
                        pe.matmul(bank(4 + r)[:, D:2 * D], EQ[:, r, :], MSG2[:, r, :], start=True, stop=False)
                        pe.matmul(bank(4 + r)[:, D:2 * D], EQ[:, r, :], MSG2L[:, r, :], start=False, stop=True
                                  ).then_inc(ev("l2_summed"), 1)
                        turn(j + 2, r)
            if layers > 3:
                pe.wait_ge(stage_done, STAGE["x3_made"])
                transpose_nodes(X).then_inc(ev("l3_xt"), 1)
                pe.wait_ge(ev("l3_xt_copied"), 1)
                pe.wait_ge(stage_done, STAGE["l3_w1_centered"])
                for t in range(NT):
                    if t >= 4:
                        pe.wait_ge(ev("l3_p_copied"), t - 3)
                    pe.matmul(bank(t % 4, HID), T1[:, t, :], W1xs[:, :], start=True, stop=True).then_inc(ev("l3_p"), 1)
                pe.wait_ge(ev("l3_p_copied"), NT)
                pe.sem_inc(ev("l3_sums"), MS)
                pe.sem_inc(ev("l3_edge_part"), RING)
                with pe.Fori(0, ITER) as i:
                    for q in range(RING):
                        pe.wait_ge(attr_landed[q], i * 16 + 16)
                        pe.wait_ge(ev("l3_hidden"), i * RING + q + 1)
                        pe.matmul(bank(5 + q % 2, HID), A3[0:EDIM, q, :], W1es[:, :], start=True, stop=True
                                  ).then_inc(ev("l3_edge_part"), 1)
                    for q in range(RING):
                        pe.wait_ge(ev("l3_sums_added"), i * RING + q + 1)
                        pe.wait_ge(ev("l3_gelu"), i * RING + q + 1)
                        pe.wait_ge(ev("l3_onehot"), i * RING + q + 1)
                        pe.matmul(bank(q % MS, COLS3), OH[:, q % MS, :], GE[:, q % MS, :], start=True, stop=True
                                  ).then_inc(ev("l3_sums"), 1)
                pe.wait_ge(ev("l3_sums_added"), SLOTS + MS)
                for k in range(2):
                    last = pe.transpose(WIDE[:, k * P:(k + 1) * P], W2s[:, k, :], ident[:, :])
                last.then_inc(ev("w2_turned"), 1)
                pe.wait_ge(ev("w2t_copied"), 1)
                for k in range(2):
                    last = pe.matmul(WIDE[:, k * P:(k + 1) * P], W2T[:, k, :], Wus[:, 1, :], start=True, stop=True)
                last = pe.matmul(WIDE[:, 2 * P:3 * P], b2c[:, :].broadcast_to([P, P]), Wus[:, 1, :], start=True, stop=True)
                last.then_inc(ev("w2u"), 1)
                pe.wait_ge(ev("w2u_copied"), 1)
                for n, src in enumerate((ACC3[:, :, 0:D], ACC3[:, :, D:2 * D], X)):
                    transpose_nodes(src).then_inc(ev("l3_turned"), 1)
                    pe.wait_ge(ev("l3_turned_copied"), n + 1)
                for t in range(NT):
                    pe.matmul(NODES[:, t, :], T1[:, t, :], W2U[:, 0, :], start=True, stop=False)
                    pe.matmul(NODES[:, t, :], T2[:, t, :], W2U[:, 1, :], start=False, stop=False)
                    last = pe.matmul(NODES[:, t, :], H[:, t, :], Wus[:, 0, :], start=False, stop=True)
                last.then_inc(ev("l3_u"), 1)

        @block.scalar
        def _(act):
            link = Chain(act, act_step)
            devs = [0]

            def copy(dst, src):
                return act.activation(dst, src, ACT.Copy)

            def deviation(n):
                devs[0] += 1
                act.wait_ge(var_ready, devs[0])
                act.activation(stat[:, 2, 0:n], stat[:, 1, 0:n], ACT.Sqrt).then_inc(dev_ready, 1)

            for n, (dst, b) in enumerate([(DLC[:, :], 2), (SRC[:, :], 4), (TYC[:, :], 0), (HIC, 2), (LOC, 4)]):
                act.wait_ge(ev("column_turned"), n + 1)
                if n == 1:
                    link(copy(SRCI[:, :], WIDE[:, b * 512:b * 512 + SPAD]))
                copy(dst, WIDE[:, b * 512:b * 512 + SPAD]).then_inc(ev("column_copied"), 1)
            act.wait_ge(ev("l0_xt"), 1)
            copy(T1, NODES).then_inc(ev("l0_xt_copied"), 1)
            act.wait_ge(ev("deg_ready"), 1)
            act.sem_inc(ev("a_turned_copied"), 2)
            act.sem_inc(ev("a_adas_copied"), 2)
            with act.Fori(0, ITER) as i:
                for h in range(2):
                    act.wait_ge(ev("a_turned"), i * 2 + h + 3)
                    act.wait_ge(ev("a_adas"), i * 2 + h + 1)
                    copy(OTA[:, h, :, :].rearrange("p k e -> p (k e)"), bank(h).bitcast(BF16)[:, 0:HALF * P]
                         ).then_inc(ev("a_turned_copied"), 1)
                    act.wait_ge(ev("a_adas"), i * 2 + h + 3)
                    copy(ADAS[:, bass.ds(i * RING + h * HALF, HALF), :],
                         bank(2 + h)[:, 0:HALF * 8].rearrange("p (k c) -> p k c", c=8)).then_inc(ev("a_adas_copied"), 1)
            act.wait_ge(stage_done, STAGE["ex_argument"])
            act.activation(EXF[:, :, 0:HEADS], ADAS[:, :, 0:HEADS], ACT.Exp).then_inc(ev("ex"), 1)
            act.wait_ge(stage_done, STAGE["loop_argument"])
            act.activation(SMN[:, 1, :, :], SMN[:, 0, :, :], ACT.Exp).then_inc(ev("loop_ex"), 1)
            deviation(D)
            deviation(NT)
            act.wait_ge(ev("l0_xt2"), 1)
            copy(ACC1, NODES).then_inc(ev("l0_xt2_copied"), 1)
            deviation(D)
            deviation(NT)
            if layers > 1:
                deviation(2 * NT)
                act.wait_ge(ev("l1_xt"), 1)
                copy(T1, NODES).then_inc(ev("l1_xt_copied"), 1)
                act.sem_inc(ev("l1_types_copied"), 2)
                with act.Fori(0, ITER) as i:
                    for h in range(2):
                        act.wait_ge(ev("l1_types_turned"), i * 2 + h + 3)
                        act.wait_ge(ev("l1_coefs"), i * 2 + h + 1)
                        copy(OTT[:, h, :, :].rearrange("p k e -> p (k e)"), bank(5 + h).bitcast(BF16)[:, 0:HALF * P]
                             ).then_inc(ev("l1_types_copied"), 1)
                deviation(NT)
                deviation(NT)
            if layers > 2:
                act.wait_ge(ev("l2_xt"), 1)
                copy(T2, NODES).then_inc(ev("l2_xt_copied"), 1)
                for t in range(NT):
                    act.wait_ge(ev("l2_y"), t + 1)
                    copy(YP[0][:, t, :], bank(t % 4)).then_inc(ev("l2_y_high"), 1)
                act.sem_inc(ev("l2_turned_copied"), 2)
                act.sem_inc(ev("l2_sum_copied"), 2)
                act.sem_inc(ev("l2_mixed_last"), 2)

                def copy_turned(j, r):
                    act.wait_ge(ev("l2_turned"), j + 3)
                    act.wait_ge(ev("l2_gathered"), j + 1)
                    copy(OT2[:, r, :], bank(r, 64).bitcast(BF16)).then_inc(ev("l2_turned_copied"), 1)

                def mix_last(j, r):
                    act.wait_ge(ev("l2_gathered"), j + 3)
                    act.wait_ge(ev("l2_summed"), j + 1)
                    act.activation(MSG2L[:, r, :], bank(4 + r, D), ACT.Copy,
                                   scale=COEF[:, bass.ds(j, 1), BASES - 1:BASES].rearrange("p a b -> p (a b)")
                                   ).then_inc(ev("l2_mixed_last"), 1)

                copy_turned(0, 0)
                copy_turned(1, 1)
                act.wait_ge(stage_done, STAGE["l2_coef_tail"])
                mix_last(0, 0)
                with act.Fori(0, ITER) as i:
                    for q in range(RING):
                        j = i * RING + q
                        r = q % 2
                        mix_last(j + 1, 1 - r)
                        act.wait_ge(ev("l2_summed"), j + 3)
                        act.wait_ge(landed[q], i * 16 + 3 * ITER * 16)
                        copy(GR[:, q, :], bank(4 + r)[:, D:2 * D]).then_inc(ev("l2_sum_copied"), 1)
                        copy_turned(j + 2, r)
                deviation(NT)
            if layers > 3:
                act.wait_ge(ev("l3_xt"), 1)
                copy(T1, NODES).then_inc(ev("l3_xt_copied"), 1)
                with act.Fori(0, ITER) as i:
                    act.wait_ge(ev("l3_inverse"), i + 1)
                    for q in range(RING):
                        act.wait_ge(ev("l3_hidden"), i * RING + q + 3)
                        act.activation(SQ[:, q % 2, :], HC3[:, q, :], ACT.Square, accum_out=SS[:, 0, q:q + 1]).then_inc(ev("l3_squares"), 1)
                        act.wait_ge(ev("l3_squares"), i * RING + q + 1)
                    act.wait_ge(ev("l3_var"), i + 1)
                    act.activation(SS[:, 2, :], SS[:, 1, :], ACT.Sqrt).then_inc(ev("l3_dev"), 1)
                    for q in range(RING):
                        act.wait_ge(ev("l3_normed"), i * RING + q + 1)
                        act.wait_ge(ev("l3_sums"), i * RING + q + 1)
                        act.activation(GE[:, q % MS, 0:HID], ZB[:, q % MS, :], ACT.Gelu).then_inc(ev("l3_gelu"), 1)
                act.wait_ge(ev("w2_turned"), 1)
                copy(W2T.rearrange("p k f -> p (k f)"), WIDE[:, 0:2 * P]).then_inc(ev("w2t_copied"), 1)
                act.wait_ge(ev("w2u"), 1)
                link(copy(W2U.rearrange("p k f -> p (k f)"), WIDE[:, 0:2 * P]))
                copy(B2U[:, :], WIDE[:, 2 * P:3 * P]).then_inc(ev("w2u_copied"), 1)
                for n, dst in enumerate((T1, T2, H[:, :, :])):
                    act.wait_ge(ev("l3_turned"), n + 1)
                    copy(dst, NODES).then_inc(ev("l3_turned_copied"), 1)
                deviation(NT)
                act.wait_ge(stage_done, STAGE["u_normed"])
                act.activation(T1, T1, ACT.Gelu).then_inc(ev("u_gelu"), 1)
                deviation(NT)

        @block.vector
        def _(v):
            link = Chain(v, dve_step)
            devs, bns = [0], [0]

            def tt(out, a, b, op):
                return v.tensor_tensor(out, a, b, op)

            def ts1(out, a, s, op, s2=None, op2=None):
                if op2 is None:
                    return v.tensor_scalar(out, a, s, None, op)
                return v.tensor_scalar(out, a, s, s2, op, op2)

            def inverse_deviation(n):
                devs[0] += 1
                v.wait_ge(dev_ready, devs[0])
                link(v.reciprocal(stat[:, 3, 0:n], stat[:, 2, 0:n]))

            def layer_norm(dst, src, centered):
                link(v.tensor_reduce(stat[:, 0, 0:NT], src, AX_X, ALU.add))
                link(ts1(stat[:, 0, 0:NT], stat[:, 0, 0:NT], 1.0 / D, ALU.mult))
                link(tt(centered, src, over_features(stat[:, 0, 0:NT]), ALU.subtract))
                link(tt(dst, centered, centered, ALU.mult))
                link(v.tensor_reduce(stat[:, 1, 0:NT], dst, AX_X, ALU.add))
                link(ts1(stat[:, 1, 0:NT], stat[:, 1, 0:NT], 1.0 / D, ALU.mult, EPS, ALU.add))
                v.sem_inc(var_ready, 1)
                inverse_deviation(NT)
                link(tt(dst, centered, over_features(stat[:, 3, 0:NT]), ALU.mult))

            def affine(tile, gain, shift):
                link(tt(tile, tile, over_tiles(gain), ALU.mult))
                link(tt(tile, tile, over_tiles(shift), ALU.add))

            def batch_norm(tile, squares, gain, shift):
                v.sem_inc(bn_in, 1)
                v.wait_ge(bn_sums, bns[0] + 1)
                link(ts1(stat[:, 0, :], bank(7, D), 1.0 / N, ALU.mult))
                link(tt(squares, tile, over_tiles(stat[:, 0, :]), ALU.subtract))
                link(tt(tile, squares, squares, ALU.mult))
                v.sem_inc(bn_in, 1)
                v.wait_ge(bn_sums, bns[0] + 2)
                bns[0] += 2
                link(ts1(stat[:, 1, :], bank(7, D), 1.0 / N, ALU.mult, EPS, ALU.add))
                v.sem_inc(var_ready, 1)
                inverse_deviation(D)
                link(tt(stat[:, 3, :], stat[:, 3, :], gain, ALU.mult))
                link(tt(tile, squares, over_tiles(stat[:, 3, :]), ALU.mult))
                link(tt(tile, tile, over_tiles(shift), ALU.add))

            def leaky(out, z):
                return v.scalar_tensor_tensor(out=out, in0=z, scalar=0.2, in1=z, op0=ALU.mult, op1=ALU.max)

            v.memset(X[:, NT - 1, :], 0.0).then_inc(ev("x_padding_zero"), 1)
            link(v.memset(ones[:, :], 1.0))
            v.wait_ge(ev("iotas"), 4)
            link(ts1(ident[:, :], iota[:, :], pcol[:, 0:1], ALU.is_equal))
            link(ts1(identb[:, :], iota[:, :], pcol[:, 0:1], ALU.is_equal))
            link(v.tensor_copy(identh[:, :], ident[:, :]))
            link(ts1(tri[:, :], iota[:, :], pcol[:, 0:1], ALU.is_lt))
            link(ts1(trashcol[:, :], pcol[:, :], float(TRASH), ALU.add))
            link(v.tensor_copy(iotab[:, :], iota[:, :]))
            v.wait_ge(ev("ends_loaded"), 16)
            link(v.tensor_single_scalar(jendi[0:1, 1, :], jendi[0:1, 0, :], 7, ALU.arith_shift_right))
            link(v.tensor_copy(jend[0:1, 0, :], jendi[0:1, 1, :]))
            tt(jend[0:1, 0, :], jend[0:1, 0, :], jend[0:1, 1, :], ALU.add).then_inc(ev("ends_made"), 1)
            v.wait_ge(ev("ends_spread"), 1)
            for g in range(SG):
                link(v.tensor_scalar(T12[:, 0:ET], WIDE[:, 0:ET], jcol[:, g:g + 1], 0.0, ALU.is_lt, ALU.add,
                                     accum_out=slots[:, 0, g:g + 1]))
            link(ts1(slots[:, 0, :], slots[:, 0, :], float(ET - 1), ALU.min))
            link(tt(slots[:, 1, :], jcol[:, :], slots[:, 0, :], ALU.subtract))
            link(ts1(slots[:, 1, :], slots[:, 1, :], float(NT - 1), ALU.min))
            link(ts1(slots[:, 2, :], slots[:, 1, :], -float(P), ALU.mult))
            link(v.tensor_copy(sloti[:, :, :], slots[:, 0:2, :]))
            v.sem_inc(stage_done, 1)
            v.wait_ge(ev("rows_gathered"), 16 * 3 * SG)
            link(v.tensor_copy(DR, RI[:, 0]))
            link(v.tensor_copy(SR, RI[:, 1]))
            link(v.tensor_copy(TR, RI[:, 2]))
            link(v.tensor_single_scalar(HII, RI[:, 1], 7, ALU.arith_shift_right))
            link(v.tensor_copy(HI, HII))
            link(v.scalar_tensor_tensor(out=LO, in0=HI, scalar=-float(P), in1=SR, op0=ALU.mult, op1=ALU.add))
            for g in range(SG):
                link(ts1(DL[:, g, :], DR[:, g, :], slots[:, 2, g:g + 1], ALU.add))
            link(ts1(VALID, DL, 0.0, ALU.is_ge))
            link(v.scalar_tensor_tensor(out=VALID, in0=DL, scalar=float(P), in1=VALID, op0=ALU.is_lt, op1=ALU.mult))
            link(v.scalar_tensor_tensor(out=HI, in0=HI, scalar=-float(P), in1=VALID, op0=ALU.add, op1=ALU.mult))
            link(ts1(HI, HI, float(P), ALU.add))
            v.sem_inc(stage_done, 1)
            v.wait_ge(weights_loaded, 16 * WLOADS)
            link(ts1(coef[:, 0:BASES], coef[:, 0:BASES], coef[:, BASES:BASES + 1], ALU.mult))
            v.wait_ge(ev("l0_h"), 1)
            link(v.tensor_copy(H[:, :, :], NODES))
            for n, (name, lo) in enumerate((("att_dst", 0), ("att_src", 4))):
                link(tt(T2, H[:, :, :], over_tiles(V(name)), ALU.mult))
                link(v.tensor_reduce(ADN[:, :, lo:lo + 4], T2.rearrange("p t (h c) -> p t h c", h=HEADS), AX_X, ALU.add))
            v.sem_inc(stage_done, 1)
            link(v.memset(OTA[:, 0, 0, :], 0.0))
            link(v.memset(AS[:, SLOTS:SPAD, :], 0.0))
            link(v.memset(ADAS[:, SLOTS:SPAD, :], 0.0))
            v.sem_inc(stage_done, 1)
            v.wait_ge(ev("column_copied"), 5)
            v.sem_inc(ev("a_ring_free"), RING)
            with v.Fori(0, ITER) as i:
                for h in range(2):
                    n = i * 2 + h + 1
                    at = i * RING + h * HALF
                    v.wait_ge(ev("a_onehot_read"), n)
                    v.wait_ge(ev("a_turned"), n)
                    for k in range(HALF):
                        j = at + k
                        ts1(OHA[:, h, k, :], iotab[:, :], DLC[:, bass.ds(j, 1)], ALU.is_equal)
                        ts1(LOA[:, h, k, :], iotab[:, :], LOC[:, bass.ds(j, 1)], ALU.is_equal)
                        last = ts1(HIA[:, h, k, 0:NT], iotab[:, 0:NT], HIC[:, bass.ds(j, 1)], ALU.is_equal)
                    last.then_inc(ev("a_onehot"), 1)
                    for q in range(h * HALF, (h + 1) * HALF):
                        v.wait_ge(landed[q], i * 16 + 16)
                    v.tensor_copy(AS[:, bass.ds(at, HALF), :], GR[:, h * HALF:(h + 1) * HALF, 0:HEADS]).then_inc(ev("a_ring_free"), HALF)
            v.wait_ge(ev("a_ring_free"), SLOTS + RING)
            v.wait_ge(ev("a_adas_copied"), 2 * ITER + 2)
            v.wait_ge(ev("a_onehot_read"), 2 * ITER + 2)
            link(v.tensor_copy(DIS[:, 1, :], bank(7, NT)))
            v.sem_inc(stage_done, 1)
            link(tt(FIRST[:, :, 1:P], DR[:, :, 1:P], DR[:, :, 0:P - 1], ALU.is_equal))
            link(v.memset(FIRST[:, :, 0:1], 0.0))
            link(ts1(AT, FIRST.unsqueeze(2).broadcast_to([P, SG, HEADS, P]), BIG, ALU.mult, -BIG, ALU.add))
            for hd in range(HEADS):
                v.wait_ge(ev("as_row"), hd + 1)
                b = (hd % 2) * 1024
                last = v.tensor_copy(VT[:, :, hd, :], WIDE[:, b:b + SPAD].rearrange("p (g l) -> p g l", l=P))
                last.then_inc(ev("as_row_copied"), 1)
            v.wait_ge(ev("as_row_copied"), HEADS)
            flat = SPAD * HEADS
            link(v.tensor_tensor_scan(ACCB[:, 0:flat], T12[:, flat:2 * flat], T12[:, 0:flat], -BIG, ALU.add, ALU.max))
            link(ts1(AT[:, :, :, 0:P - 1], FIRST[:, :, 1:P].unsqueeze(2).broadcast_to([P, SG, HEADS, P - 1]), BIG, ALU.mult,
                     -BIG, ALU.add))
            link(v.memset(AT[:, :, :, P - 1:P], -BIG))
            link(v.tensor_tensor_scan(T12[:, 0:flat][:, ::-1], T12[:, flat:2 * flat][:, ::-1], ACCB[:, 0:flat][:, ::-1],
                                      -BIG, ALU.add, ALU.max))
            v.sem_inc(stage_done, 1)
            for n, row in enumerate((R_FM, R_LM, R_FD, R_LD)):
                v.wait_ge(ev("end_row"), n + 1)
                b = (n % 2) * 1024
                link(v.tensor_copy(row, WIDE[0:HEADS, b:b + SPAD]))
                v.sem_inc(ev("end_row_copied"), 1)
            link(tt(R_W, R_FD, R_LD, ALU.is_equal))
            link(v.memset(R_LINK[:, 0:1], 0.0))
            link(tt(R_LINK[:, 1:SPAD], R_FD[:, 1:SPAD], R_LD[:, 0:SPAD - 1], ALU.is_equal))
            link(tt(R_A, R_LINK, R_W, ALU.mult))
            link(ts1(R_A, R_A, BIG, ALU.mult, -BIG, ALU.add))
            link(v.tensor_tensor_scan(R_OUT, R_A, R_LM, -BIG, ALU.add, ALU.max))
            link(v.memset(R_CF[:, 0:1], -BIG))
            link(ts1(R_CF[:, 1:SPAD], R_LINK[:, 1:SPAD], BIG, ALU.mult, -BIG, ALU.add))
            link(tt(R_CF[:, 1:SPAD], R_CF[:, 1:SPAD], R_OUT[:, 0:SPAD - 1], ALU.add))
            link(tt(R_A[:, 0:SPAD - 1], R_LINK[:, 1:SPAD], R_W[:, 0:SPAD - 1], ALU.mult))
            link(v.memset(R_A[:, SPAD - 1:SPAD], 0.0))
            link(ts1(R_A, R_A, BIG, ALU.mult, -BIG, ALU.add))
            link(v.tensor_tensor_scan(R_OUT[:, ::-1], R_A[:, ::-1], R_FM[:, ::-1], -BIG, ALU.add, ALU.max))
            link(v.memset(R_CB[:, SPAD - 1:SPAD], -BIG))
            link(ts1(R_CB[:, 0:SPAD - 1], R_LINK[:, 1:SPAD], BIG, ALU.mult, -BIG, ALU.add))
            link(tt(R_CB[:, 0:SPAD - 1], R_CB[:, 0:SPAD - 1], R_OUT[:, 1:SPAD], ALU.add))
            v.sem_inc(stage_done, 1)
            v.wait_ge(ev("carries_turned"), 1)
            link(v.tensor_copy(carry[:, :, :, :].rearrange("p n g h -> p (n g h)"), WIDE[:, 3072:3072 + 3 * SG * HEADS]))
            for c, lane in ((0, 0), (1, P - 1)):
                link(tt(AT[:, :, 0, :], DR, DR[:, :, lane:lane + 1].broadcast_to([P, SG, P]), ALU.is_equal))
                link(ts1(AT[:, :, 0, :], AT[:, :, 0, :], BIG, ALU.mult, -BIG, ALU.add))
                for g in range(SG):
                    for hd in range(HEADS):
                        last = v.scalar_tensor_tensor(out=VT[:, g, hd, :], in0=AT[:, g, 0, :], scalar=carry[:, c, g, hd:hd + 1],
                                                      in1=VT[:, g, hd, :], op0=ALU.add, op1=ALU.max)
                link(last)
            link(ts1(FIRST[:, :, 0], carry[:, 2, :, 0], 1.0, ALU.mult))
            link(v.scalar_tensor_tensor(out=FIRST, in0=FIRST, scalar=0.5, in1=VALID, op0=ALU.is_lt, op1=ALU.mult))
            v.sem_inc(stage_done, 1)
            for n in range(HEADS + 1):
                v.wait_ge(ev("max_turned"), n + 1)
                b = (n % 2) * 1024
                dst = MT[:, :, n] if n < HEADS else FIRSTC
                link(v.tensor_copy(dst, WIDE[:, b:b + SPAD]))
                v.sem_inc(ev("max_copied"), 1)
            link(tt(MT, MT, ADAS[:, :, 4:8], ALU.max))
            link(tt(EXF[:, :, 4:8], MT, FIRSTC.unsqueeze(2).broadcast_to([P, SPAD, HEADS]), ALU.mult))
            link(v.tensor_copy(EXF[:, :, 8], FIRSTC))
            link(tt(AS, AS, ADAS[:, :, 0:4], ALU.add))
            link(leaky(AS, AS))
            link(tt(MT, MT, ADAS[:, :, 0:4], ALU.add))
            link(leaky(MT, MT))
            link(tt(ADAS[:, :, 0:4], AS, MT, ALU.subtract))
            v.sem_inc(stage_done, 1)
            v.wait_ge(ev("ex"), 1)

            def zero_sums():
                link(v.memset(ACCB[:, :], 0.0))

            def add_sums(name, acc, q, j, t, credit, banks=MS):
                v.wait_ge(ev(name + "_sums"), j + 1 + credit)
                v.wait_ge(ev(name + "_sums_added"), j + banks)
                a = acc[:, bass.ds(t, 1), :].rearrange("p a b -> p (a b)")
                tt(a, a, bank(q % banks, acc.shape[-1]), ALU.add).then_inc(ev(name + "_sums_added"), 1)

            zero_sums()
            v.wait_ge(ev("slots_loaded"), 32)
            v.sem_inc(ev("l0_sums_added"), MS)
            v.sem_inc(ev("l0_messages"), RING)
            with v.Fori(0, ITER) as i:
                tiles = tile_registers(ENG.DVE, i)
                for q in range(RING + 1):
                    if q < RING:
                        j = i * RING + q
                        r = q % MS
                        v.wait_ge(ev("l0_sums"), j + 1 + RING - MS)
                        ts1(OH[:, r, :], iota[:, :], DLC[:, bass.ds(j, 1)], ALU.is_equal)
                        v.tensor_copy(MSG0[:, r, D:COLS0], EXF[:, bass.ds(j, 1), :].rearrange("p a b -> p (a b)")
                                      )
                        v.wait_ge(landed[q], i * 16 + (ITER * 16 + 16))
                        tt(MSG0[:, r, 0:D].rearrange("p (h c) -> p h c", h=HEADS), GR[:, q, :].rearrange("p (h c) -> p h c", h=HEADS),
                           EXF[:, bass.ds(j, 1), 0:HEADS].rearrange("p a b -> p (a b)").unsqueeze(2).broadcast_to([P, HEADS, HC]),
                           ALU.mult).then_inc(ev("l0_messages"), 1)
                    if q >= 1:
                        add_sums("l0", ACC0, q - 1, i * RING + q - 1, tiles[q - 1], RING)
            v.wait_ge(ev("l0_sums_added"), SLOTS + MS)
            EXL = SMN[:, 1, :, :]
            link(ts1(HAS[:, :], ACC0[:, :, COLS0 - 1], BIG, ALU.mult, -BIG, ALU.add))
            link(tt(SMN[:, 2, :, :], ACC0[:, :, D + 4:D + 8], HAS[:, :].unsqueeze(2).broadcast_to([P, NT, HEADS]), ALU.add))
            link(tt(SMN[:, 2, :, :], SMN[:, 2, :, :], ADN[:, :, 4:8], ALU.max))
            link(tt(SMN[:, 2, :, :], SMN[:, 2, :, :], ADN[:, :, 0:4], ALU.add))
            link(leaky(SMN[:, 2, :, :], SMN[:, 2, :, :]))
            link(tt(SMN[:, 3, :, :], ADN[:, :, 4:8], ADN[:, :, 0:4], ALU.add))
            link(leaky(SMN[:, 3, :, :], SMN[:, 3, :, :]))
            link(tt(SMN[:, 0, :, :], SMN[:, 3, :, :], SMN[:, 2, :, :], ALU.subtract))
            v.sem_inc(stage_done, 1)
            v.wait_ge(ev("loop_ex"), 1)
            link(tt(SMN[:, 2, :, :], ACC0[:, :, D:D + 4], EXL, ALU.add))
            link(v.reciprocal(SMN[:, 3, :, :], SMN[:, 2, :, :]))
            by_head = [P, NT, HEADS, HC]
            T1H, HH = T1.rearrange("p t (h c) -> p t h c", h=HEADS), H[:, :, :].rearrange("p t (h c) -> p t h c", h=HEADS)
            link(tt(T1H, HH, EXL.unsqueeze(3).broadcast_to(by_head), ALU.mult))
            link(tt(T1, T1, ACC0[:, :, 0:D], ALU.add))
            link(tt(T1H, T1H, SMN[:, 3, :, :].unsqueeze(3).broadcast_to(by_head), ALU.mult))
            link(tt(T1, T1, over_tiles(V("bias")), ALU.add))
            batch_norm(T1, T2, V("bn_g"), V("bn_b"))
            layer_norm(T1, T1, T2)
            affine(T1, V("ln_g"), V("ln_b"))
            v.sem_inc(stage_done, 1)
            v.wait_ge(ev("l0_res"), 1)
            link(tt(H[:, :, :], NODES, over_tiles(V("res_b")), ALU.add))
            batch_norm(H[:, :, :], T2, V("bnres_g"), V("bnres_b"))
            link(tt(T1, T1, H[:, :, :], ALU.add))
            link(v.scalar_tensor_tensor(out=X[:, :, :], in0=T1, scalar=0.0, in1=X[:, :, :], op0=ALU.max, op1=ALU.add))
            layer_norm(X[:, :, :], X[:, :, :], T2)
            if layers > 1:
                v.sem_inc(stage_done, 1)
                link(ts1(stat[:, 1, 0:NT], DIS[:, 1, :], 1.0, ALU.add))
                link(ts1(stat[:, 1, NT:2 * NT], DIS[:, 1, :], 1.0, ALU.max))
                link(ts1(HAS[:, :], DIS[:, 1, :], 0.0, ALU.is_gt))
                v.sem_inc(var_ready, 1)
                inverse_deviation(2 * NT)
                link(v.tensor_copy(DIS[:, 0, :], stat[:, 3, 0:NT]))
                link(tt(DIS[:, 1, :], stat[:, 3, NT:2 * NT], HAS[:, :], ALU.mult))
                v.wait_ge(ev("l1_h"), 1)
                link(tt(H[:, :, :], NODES, over_tiles(V("b_l1")), ALU.add))
                v.sem_inc(stage_done, 1)
                link(tt(H[:, :, :], H[:, :, :], over_features(DIS[:, 0, :]), ALU.mult))
                v.sem_inc(stage_done, 1)
                zero_sums()
                link(v.memset(T12[:, 0:(NT + 1) * D], 0.0))
                v.sem_inc(stage_done, 1)
                v.sem_inc(ev("l1_sums_added"), 2)
                v.sem_inc(ev("l1_repeats"), 2)
                v.sem_inc(ev("l1_coefs_copied"), 2)
                link(v.memset(OHT, 0.0))
                with v.Fori(0, ITER) as i:
                    tiles = tile_registers(ENG.DVE, i)
                    for h in range(2):
                        n = i * 2 + h + 1
                        at = i * RING + h * HALF
                        v.wait_ge(ev("l1_types_turned"), n)
                        v.wait_ge(ev("l1_sources"), at + 2)
                        v.tensor_copy(SRCST[:, h, :], SRC[:, bass.ds(at, HALF)])
                        for k in range(HALF):
                            last = ts1(OHT[:, h, k, 0:REL], iotab[:, 0:REL], TYC[:, bass.ds(at + k, 1)], ALU.is_equal)
                        last.then_inc(ev("l1_type_onehot"), 1)
                        for k in range(HALF + 1):
                            q = h * HALF + k
                            if k < HALF:
                                j = at + k
                                v.wait_ge(ev("l1_sums"), j + 1 + RING - MS)
                                ts1(OH[:, q % MS, :], iota[:, :], DLC[:, bass.ds(j, 1)], ALU.is_equal).then_inc(ev("l1_onehot"), 1)
                                v.wait_ge(ev("l1_sources"), j + 3)
                                v.wait_ge(ev("l1_repeats"), j + 1)
                                v.scalar_tensor_tensor(out=JUNK[:, q % 2, :], in0=bank(2 + q % 2, P),
                                                       scalar=SRC[:, bass.ds(j, 1)], in1=tri[:, :], op0=ALU.is_equal,
                                                       op1=ALU.mult, accum_out=DUP[:, h, k:k + 1]).then_inc(ev("l1_repeats"), 1)
                            if k >= 1:
                                add_sums("l1", ACC1, q - 1, at + k - 1, tiles[q - 1], RING, 2)
                        v.wait_ge(ev("l1_repeats"), at + HALF + 2)
                        ts1(NDUP[:, h, :], DUP[:, h, :], 0.5, ALU.is_lt).then_inc(ev("l1_row_step"), 1)
                        v.wait_ge(ev("l1_row_step"), n * 2 - 1)
                        v.scalar_tensor_tensor(out=NDUP[:, h, :], in0=SRCST[:, h, :], scalar=trashcol[:, 0:1],
                                               in1=NDUP[:, h, :], op0=ALU.subtract, op1=ALU.mult).then_inc(ev("l1_row_step"), 1)
                        v.wait_ge(ev("l1_row_step"), n * 2)
                        ts1(SCI[:, bass.ds(at, HALF)], NDUP[:, h, :], trashcol[:, 0:1], ALU.add)
                        v.wait_ge(ev("l1_coefs"), n + 2)
                        v.tensor_copy(COEF[:, bass.ds(at, HALF), :], bank(4 + 3 * h)[:, 0:HALF * BASES].rearrange("p (k b) -> p k b", b=BASES)
                                      ).then_inc(ev("l1_coefs_copied"), 1)
                v.wait_ge(ev("l1_coefs_copied"), 2 * ITER + 2)
                v.sem_inc(stage_done, 1)
                v.wait_ge(ev("l1_sums_added"), SLOTS + 2)
                v.wait_ge(ev("h1_stored"), 16)
                v.wait_ge(ev("acc_zero_stored"), 16 * NACC)
                link(tt(T1, ACC1, H[:, :, :], ALU.add))
                link(tt(T1, T1, over_features(DIS[:, 0, :]), ALU.mult))
                link(ts1(T1, T1, 0.0, ALU.max))
                layer_norm(T1, T1, T2)
                affine(T1, V("g_l1"), V("be_l1"))
                link(v.scalar_tensor_tensor(out=X[:, :, :], in0=X[:, :, :], scalar=2.0, in1=T1, op0=ALU.mult, op1=ALU.add))
                layer_norm(X[:, :, :], X[:, :, :], T2)
            if layers > 2:
                link(tt(T1, X[:, :, :], over_features(DIS[:, 1, :]), ALU.mult))
                v.sem_inc(stage_done, 1)
                for t in range(NT):
                    v.wait_ge(ev("l2_y_high"), t + 1)
                    rest = YREST[:, t % 2, :]
                    link(tt(rest, bank(t % 4), YP[0][:, t, :], ALU.subtract))
                    v.sem_inc(ev("l2_y_copied"), 1)
                    link(v.tensor_copy(YP[1][:, t, :], rest))
                    link(tt(YP[2][:, t, :], rest, YP[1][:, t, :], ALU.subtract))
                link(v.memset(COEF[:, SLOTS:SPAD, :], 0.0))
                v.sem_inc(stage_done, 1)
                v.sem_inc(stage_done, 1)
                v.sem_inc(ev("l2_onehot"), 2)
                v.sem_inc(ev("l2_equal"), 2)
                v.sem_inc(ev("l2_mixed"), 2)

                def onehot(j, r):
                    v.wait_ge(ev("l2_turned"), j + 1)
                    ts1(SRC2[:, r:r + 1], SRC[:, bass.ds(j, 1)], -float(NPAD // 2), ALU.add)
                    ts1(OH2[:, r, :], iotab[:, :], DLC[:, bass.ds(j, 1)], ALU.is_equal).then_inc(ev("l2_onehot"), 1)

                def equal(j, r):
                    v.wait_ge(ev("l2_turned"), j + 3)
                    v.wait_ge(ev("l2_summed"), j + 1)
                    v.tensor_scalar(EQ[:, r, :], bank(6 + r, P), float(NPAD // 2), SRC[:, bass.ds(j, 1)], ALU.add, ALU.is_equal
                                    ).then_inc(ev("l2_equal"), 1)

                onehot(0, 0)
                onehot(1, 1)
                equal(0, 0)
                with v.Fori(0, ITER) as i:
                    for q in range(RING):
                        j = i * RING + q
                        r = q % 2

                        def mix(b):
                            c = COEF[:, bass.ds(j, 1), b:b + 1].rearrange("p a b -> p (a b)")
                            g = bank(2 + r)[:, b * D:(b + 1) * D]
                            if b == 0:
                                ts1(MSG2[:, r, :], g, c, ALU.mult).then_inc(ev("l2_mixing"), 1)
                                return
                            v.wait_ge(ev("l2_mixing"), j * 2 + b)
                            v.scalar_tensor_tensor(out=MSG2[:, r, :], in0=g, scalar=c, in1=MSG2[:, r, :], op0=ALU.mult,
                                                   op1=ALU.add).then_inc(ev("l2_mixing" if b == 1 else "l2_mixed"), 1)

                        v.wait_ge(ev("l2_gathered"), j + 3)
                        v.wait_ge(ev("l2_summed"), j + 1)
                        mix(0)
                        onehot(j + 2, r)
                        mix(1)
                        equal(j + 1, 1 - r)
                        mix(2)
                v.wait_ge(ev("acc_loaded"), 16 * NACC)
                for part in (T2, ACC1, ACC1B, H[:, :, :]):
                    link(tt(T1, T1, part, ALU.add))
                link(tt(T1, T1, over_features(DIS[:, 1, :]), ALU.mult))
                link(tt(X[:, :, :], X[:, :, :], T1, ALU.add))
                layer_norm(X[:, :, :], X[:, :, :], T2)
            if layers > 3:
                v.sem_inc(stage_done, 1)
                for n, w in enumerate((W1xs[:, :], W1es[:, :], B1[:, :])):
                    k = w.shape[0]
                    link(v.tensor_reduce(wsum[0:k, n:n + 1], w, AX_X, ALU.add))
                    link(ts1(wsum[0:k, n:n + 1], wsum[0:k, n:n + 1], -1.0 / HID, ALU.mult))
                    link(ts1(w, w, wsum[0:k, n:n + 1], ALU.add))
                v.sem_inc(stage_done, 1)
                for t in range(NT):
                    v.wait_ge(ev("l3_p"), t + 1)
                    tt(PN[:, t, :], bank(t % 4, HID), B1[:, :], ALU.add).then_inc(ev("l3_p_copied"), 1)
                v.wait_ge(ev("l3_p_copied"), NT)
                v.sem_inc(stage_done, 1)
                zero_sums()
                link(v.memset(GE, 1.0))
                v.sem_inc(ev("l3_sums_added"), MS)
                v.sem_inc(ev("l3_hidden"), 2)
                v.sem_inc(ev("l3_inverse"), 1)
                v.sem_inc(ev("l3_ring_free"), RING)
                with v.Fori(0, ITER) as i:
                    tiles = tile_registers(ENG.DVE, i)
                    for q in range(RING):
                        j = i * RING + q
                        v.wait_ge(landed[q], i * 16 + (4 * ITER * 16 + 16))
                        v.wait_ge(ev("l3_edge_part"), j + 1 + RING)
                        tt(HC3[:, q, :], GR3[:, q, :], bank(5 + q % 2, HID), ALU.add).then_inc(ev("l3_hidden"), 1)
                        v.wait_ge(ev("l3_hidden"), j + 3)
                        v.sem_inc(ev("l3_ring_free"), 1)
                    v.wait_ge(ev("l3_squares"), (i + 1) * RING)
                    ts1(SS[:, 1, :], SS[:, 0, :], 1.0 / HID, ALU.mult, EPS, ALU.add).then_inc(ev("l3_var"), 1)
                    v.wait_ge(ev("l3_dev"), i + 1)
                    v.reciprocal(SS[:, 3, :], SS[:, 2, :]).then_inc(ev("l3_inverse"), 1)
                    v.wait_ge(ev("l3_inverse"), i + 2)
                    for q in range(RING + 2):
                        if q < RING:
                            j = i * RING + q
                            r = q % MS
                            v.wait_ge(ev("l3_sums"), j + 1)
                            ts1(OH[:, r, :], iota[:, :], DLC[:, bass.ds(j, 1)], ALU.is_equal).then_inc(ev("l3_onehot"), 1)
                            v.scalar_tensor_tensor(out=HC3[:, q, :], in0=HC3[:, q, :], scalar=SS[:, 3, q:q + 1], in1=G1[:, :],
                                                   op0=ALU.mult, op1=ALU.mult).then_inc(ev("l3_scaled"), 1)
                            v.wait_ge(ev("l3_scaled"), j + 1)
                            tt(ZB[:, r, :], HC3[:, q, :], BE1[:, :], ALU.add).then_inc(ev("l3_normed"), 1)
                        if q >= 2:
                            add_sums("l3", ACC3, q - 2, i * RING + q - 2, tiles[q - 2], MS)
                v.wait_ge(ev("l3_sums_added"), SLOTS + MS)
                v.wait_ge(ev("l3_u"), 1)
                link(tt(T1, NODES, over_tiles(V("bu")), ALU.add))
                link(tt(T2, over_features(ACC3[:, :, HID]), over_tiles(B2U[:, :]), ALU.mult))
                link(tt(T1, T1, T2, ALU.add))
                layer_norm(T1, T1, T2)
                affine(T1, V("gu"), V("beu"))
                v.sem_inc(stage_done, 1)
                v.wait_ge(ev("u_gelu"), 1)
                link(v.scalar_tensor_tensor(out=X[:, :, :], in0=X[:, :, :], scalar=2.0, in1=T1, op0=ALU.mult, op1=ALU.add))
                layer_norm(X[:, :, :], X[:, :, :], T2)
            v.sem_inc(stage_done, 1)


def kernel(**inputs):
    import numpy as np
    import concourse.bacc as bacc
    from concourse.bass_utils import run_bass_kernel_spmd

    nc = bacc.Bacc("TRN2", target_bir_lowering=False, num_devices=1)
    arrays = {}

    def feed(name, a):
        a = np.ascontiguousarray(a)
        arrays[name] = a
        return nc.dram_tensor(name, a.shape, mybir.dt.from_np(a.dtype), kind="ExternalInput").ap()

    def tiles_of_edges(a, pad):
        whole = np.full((ET * P,) + a.shape[1:], pad, a.dtype)
        whole[:E] = a
        return whole.reshape((ET, P) + a.shape[1:])

    g = {k: np.asarray(a) for k, a in inputs.items()}
    vec_from = {"att_src": "L0_gnn_att_src", "att_dst": "L0_gnn_att_dst", "bias": "L0_gnn_bias", "bn_g": "L0_gnn_bn_gamma",
                "bn_b": "L0_gnn_bn_beta", "ln_g": "L0_gnn_ln_gamma", "ln_b": "L0_gnn_ln_beta", "res_b": "L0_gnn_res_b",
                "bnres_g": "L0_gnn_bnres_gamma", "bnres_b": "L0_gnn_bnres_beta", "b_l1": "L1_gnn_b", "g_l1": "L1_gnn_gamma",
                "be_l1": "L1_gnn_beta", "bu": "L3_gnn_bu", "gu": "L3_gnn_gu", "beu": "L3_gnn_beu"}
    args = dict(
        x=feed("in_x", g["x"]),
        src_t=feed("in_src", tiles_of_edges(g["src"], PAD_NODE)),
        dst_t=feed("in_dst", tiles_of_edges(g["dst"], PAD_NODE)),
        typ_t=feed("in_type", tiles_of_edges(g["edge_type_50"], 0)),
        attr_t=feed("in_attr", tiles_of_edges(g["edge_attr_32"], 0).transpose(0, 2, 1).reshape(ET, EDIM * P)),
        W0=feed("in_w0", g["L0_gnn_W"]),
        resW=feed("in_res_w", g["L0_gnn_res_W"]),
        vec={k: feed("in_" + k, g[s].reshape(D)) for k, s in vec_from.items()},
        W1T=feed("in_l1_w", g["L1_gnn_W"].T),
        bases=feed("in_bases", g["L2_gnn_bases"]),
        comps=feed("in_comps", g["L2_gnn_comps"]),
        alpha=feed("in_alpha", g["L2_gnn_alpha"]),
        W1x=feed("in_l3_w1x", g["L3_gnn_W1"][:D]),
        W1e=feed("in_l3_w1e", g["L3_gnn_W1"][D:]),
        b1=feed("in_l3_b1", g["L3_gnn_b1"]),
        g1=feed("in_l3_g1", g["L3_gnn_g1"]),
        be1=feed("in_l3_be1", g["L3_gnn_be1"]),
        W2=feed("in_l3_w2", g["L3_gnn_W2"]),
        b2=feed("in_l3_b2", g["L3_gnn_b2"]),
        Wu=feed("in_l3_wu", g["L3_gnn_Wu"]),
    )
    out = nc.dram_tensor("out_0", (N, D), F32, kind="ExternalOutput").ap()
    gnn_stack(nc, out=out, **args)
    r = run_bass_kernel_spmd(nc, [arrays], core_ids=[0])
    return r.results[0]["out_0"]
```

```python
from contextlib import ExitStack

import concourse.bass as bass
from concourse import mybir

F32 = mybir.dt.float32
BF16 = mybir.dt.bfloat16
F16 = mybir.dt.float16
I32 = mybir.dt.int32
ALU = mybir.AluOpType
ACT = mybir.ActivationFunctionType
AX_X = mybir.AxisListType.X
ENG = mybir.EngineType

P = 128
N, E, D = 3125, 103125, 128
HEADS, HC = 4, 32
EDIM, HID = 32, 256
REL, BASES = 50, 4
NT = -(-N // P)
LAST = N - (NT - 1) * P
NPAD = NT * P
PAD_NODE = NPAD - 1
ET = -(-E // P)
SLOTS = ET + NT - 1
SG = -(-SLOTS // P)
SPAD = SG * P
RING = 10
HALF = RING // 2
ITER = SLOTS // RING
assert ITER * RING == SLOTS
RING3 = 2 * RING
ITER3 = SLOTS // RING3 - 1
EDGE_AHEAD, COPY_AHEAD, SQUARES_AHEAD = 16, 15, 10
INV_STEPS = 12
MS = 5
COLS0 = D + 2 * HEADS + 1
COLS3 = HID + 1
NACC = 5
TRASH = NPAD
ACC_ROWS = NPAD + P
BIG = 1e30
EPS = 1e-5
STAGES = ["slots_made", "rows_made", "base_max", "att_made", "base_scale", "a_zeros", "edge_values", "slot_max_made", "carries_made",
          "max_made", "ex_argument", "loop_argument", "l0_attention_out", "x1_made", "h1_made",
          "zeros_made", "l1_ready", "scatter_rows_made", "l2_scaled", "l2_y_parts", "l2_coef_tail", "x3_made",
          "l3_w1_centered", "p_made", "l3_ready", "u_normed", "out_made"]
STAGE = {name: n + 1 for n, name in enumerate(STAGES)}
VECS = ["att_src", "att_dst", "bias", "bn_g", "bn_b", "ln_g", "ln_b", "res_b", "bnres_g", "bnres_b",
        "b_l1", "g_l1", "be_l1", "bu", "gu", "beu"]


def gnn_stack(nc, x, src_t, dst_t, typ_t, attr_t, W0, resW, vec, W1T, bases, comps, alpha, W1x, W1e, b1, g1, be1,
              W2, b2, Wu, out, layers=4):
    with ExitStack() as ctx:
        def sb(name, shape, dt=F32):
            return ctx.enter_context(nc.sbuf_tensor(name, shape, dt))

        def sem(name):
            return ctx.enter_context(nc.semaphore(name))

        events = {}

        def ev(name):
            if name not in events:
                events[name] = sem(name)
            return events[name]

        h_dram = nc.dram_tensor("h_dram", (NPAD, D), F32, kind="Internal").ap()
        as_dram = nc.dram_tensor("as_dram", (NPAD, HEADS), F32, kind="Internal").ap()
        p_dram = nc.dram_tensor("p_dram", (NPAD, HID), F32, kind="Internal").ap()
        slot_dram = [nc.dram_tensor(f"slot_dram{k}", (SPAD, 1), I32, kind="Internal").ap() for k in range(2)]
        acc_dram = [nc.dram_tensor(f"acc_dram{k}", (ACC_ROWS, D), F32, kind="Internal").ap() for k in range(NACC)]

        X = sb("X", [P, NT, D])
        H = sb("H", [P, NT, D])
        ACCB = sb("ACCB", [P, NT * COLS3])
        T12 = sb("T12", [P, SPAD * 8])
        T1 = T12[:, 0:NT * D].rearrange("p (t f) -> p t f", f=D)
        T2 = T12[:, NT * D:2 * NT * D].rearrange("p (t f) -> p t f", f=D)
        ACC0 = ACCB[:, 0:NT * COLS0].rearrange("p (t f) -> p t f", f=COLS0)
        ACC1 = ACCB[:, 0:NT * D].rearrange("p (t f) -> p t f", f=D)
        ACC1B = ACCB[:, NT * D:2 * NT * D].rearrange("p (t f) -> p t f", f=D)
        ACC3 = ACCB[:, :].rearrange("p (t f) -> p t f", f=COLS3)
        ARENA = sb("ARENA", [P, SPAD * 21])

        def carve(buf, at, *dims):
            n = 1
            for d in dims:
                n *= d
            names = "abcd"[:len(dims)]
            return buf[:, at:at + n].rearrange("p (" + " ".join(names) + ") -> p " + " ".join(names),
                                               **dict(zip(names[1:], dims[1:])))

        AS = carve(ARENA, 0, SPAD, 4)
        ADAS = carve(ARENA, SPAD * 4, SPAD, 8)
        EXF = carve(ARENA, SPAD * 12, SPAD, 9)
        DR, SR, TR, DL, HI, LO, VALID, FIRST, SPARE = [carve(ARENA, SPAD * (12 + k), SG, P) for k in range(9)]
        RI = T12[:, 0:3 * SPAD].bitcast(I32).rearrange("p (k g l) -> p k g l", k=3, l=P)
        HII = T12[:, 3 * SPAD:4 * SPAD].bitcast(I32).rearrange("p (g l) -> p g l", l=P)
        HIC, LOC = ACCB[:, 0:SPAD], ACCB[:, SPAD:2 * SPAD]
        OHA = carve(ACCB[:, 2 * SPAD:2 * SPAD + RING * 64].bitcast(BF16), 0, 2, HALF, P)
        LOA = carve(ACCB[:, 2 * SPAD + RING * 64:2 * SPAD + RING * 128].bitcast(BF16), 0, 2, HALF, P)
        HIA = carve(ACCB[:, 2 * SPAD + RING * 128:2 * SPAD + RING * 141].bitcast(BF16), 0, 2, HALF, 26)
        OTA = carve(ACCB, 2 * SPAD + RING * 141, 2, HALF, P)
        VT, AT = carve(T12, 0, SG, HEADS, P), carve(T12, SPAD * 4, SG, HEADS, P)
        FT = carve(ACCB, 0, SG, HEADS, P)
        MT = carve(ACCB, 0, SPAD, HEADS)
        FIRSTC = T12[:, SPAD * 4:SPAD * 5]
        R_FM, R_LM, R_FD, R_LD, R_LINK, R_W = [ARENA[0:HEADS, SPAD * (12 + k):SPAD * (13 + k)] for k in (1, 2, 3, 4, 5, 8)]
        R_CF, R_CB, R_A = [ACCB[0:HEADS, SPAD * (4 + k):SPAD * (5 + k)] for k in range(3)]
        R_OUT = R_LD
        MSG0 = carve(ARENA, 0, MS, COLS0)
        COEF = carve(ARENA, 0, SPAD, BASES)
        YP = [carve(ARENA[:, o:o + NT * 2 * D].bitcast(F16), 0, NT, BASES * D)
              for o in (SPAD * 4, SPAD * 4 + NT * 2 * D)]
        l1r = SPAD * 4
        OHT = carve(ARENA[:, l1r:l1r + RING * 64].bitcast(BF16), 0, 2, HALF, P)
        OTT = carve(ARENA, l1r + RING * 64, 2, HALF, P)
        JUNK = carve(ARENA, l1r + RING * 192, 2, P)
        DUP = carve(ARENA, SPAD * 8, SPAD)
        FIRSTSRC = carve(ARENA, SPAD * 9, SPAD)
        l2r = SPAD * 4 + NT * BASES * D
        OH2 = carve(ARENA[:, l2r:l2r + P].bitcast(F16), 0, 2, P)
        OT2 = carve(ARENA[:, l2r + P:l2r + 2 * P].bitcast(F16), 0, 2, P)
        EQ = carve(ARENA, l2r + 4 * P, 2, P)
        MSG2 = carve(ARENA, l2r + 6 * P, 2, P)
        SRCH = ARENA[:, l2r + 8 * P:l2r + 8 * P + SPAD // 2].bitcast(F16)
        assert l2r + 8 * P + SPAD // 2 <= SPAD * 20
        PN = carve(ARENA, 0, NT, HID)
        l3r = NT * HID
        HC3 = carve(ARENA, l3r, RING3, HID)
        ZB = carve(ARENA, l3r + 2 * RING * HID, MS, HID)
        GE = carve(ARENA, l3r + 2 * RING * HID + MS * HID, MS, COLS3)
        A3 = carve(ARENA, l3r + 3 * RING * HID + MS * HID, RING, P)
        SQ = carve(ARENA, l3r + 4 * RING * HID, 2, HID)
        DLC = sb("DLC", [P, SPAD])
        SRC = sb("SRC", [P, SPAD])
        SRCI = sb("SRCI", [P, SPAD], I32)
        TYC = sb("TYC", [P, SPAD])
        SCI = ARENA[:, SPAD * 20:SPAD * 21].bitcast(I32)
        ttab = sb("ttab", [1, 2, SPAD], I32)
        iota = sb("iota", [P, P])
        iotab = sb("iotab", [P, P], BF16)
        pcol = sb("pcol", [P, 1])
        trashcol = sb("trashcol", [P, 2])
        ident = sb("ident", [P, P])
        identb = sb("identb", [P, P], BF16)
        identh = sb("identh", [P, P], F16)
        tri = sb("tri", [P, P])
        ones = sb("ones", [P, P])
        VEC = sb("VEC", [P, len(VECS), D])
        B1 = sb("B1", [P, HID])
        G1 = sb("G1", [P, HID])
        BE1 = sb("BE1", [P, HID])
        b2c = sb("b2c", [P, 1])
        B2U = sb("B2U", [P, D])
        W0s = sb("W0s", [P, D])
        resWs = sb("resWs", [P, D])
        W1Ts = sb("W1Ts", [P, D])
        bas = sb("bas", [P, BASES, D])
        coef = sb("coef", [REL, BASES + 1])
        W1xs = sb("W1xs", [P, HID])
        W1es = sb("W1es", [EDIM, HID])
        W2s = sb("W2s", [P, 2, D])
        W2T = carve(ARENA, SPAD * 20, 2, D)
        W2U = carve(ARENA, SPAD * 20 + 2 * D, 2, D)
        Wus = sb("Wus", [P, 2, D])
        ADN = sb("ADN", [P, NT, 8])
        SMN = sb("SMN", [P, 4, NT, 4])
        DIS = sb("DIS", [P, 2, NT])
        HAS = sb("HAS", [P, NT])
        stat = sb("stat", [P, 4, P])
        jcol = sb("jcol", [P, SG])
        slots = sb("slots", [P, 3, SG])
        sloti = sb("sloti", [P, 2, SG], I32)
        jend = carve(T12, SPAD * 5, 2, ET)
        jendi = carve(ACCB[:, 0:2 * ET].bitcast(I32), 0, 2, ET)
        carry = sb("carry", [P, 3, SG, HEADS])
        wsum = sb("wsum", [P, 4])
        scalei = sb("scalei", [1, 1], I32)
        SS = sb("SS", [P, 4, RING3])
        istage = sb("istage", [P, 2, HALF], I32)
        GR = sb("GR", [P, RING, D])
        OH = sb("OH", [P, MS, P])

        WIDE = ctx.enter_context(nc.psum_tensor("WIDE", [P, 7 * 512], F32))
        LASTB = ctx.enter_context(nc.psum_tensor("LASTB", [P, 512], F32))

        def bank(b, n=512):
            return LASTB[:, 0:n] if b == 7 else WIDE[:, b * 512:b * 512 + n]

        NODES = WIDE[:, 0:NT * D].rearrange("p (t f) -> p t f", f=D)

        def V(name):
            return VEC[:, VECS.index(name), :]

        def over_tiles(v):
            return v.unsqueeze(1).broadcast_to([P, NT, v.shape[-1]])

        def over_features(v, n=D):
            return v.unsqueeze(2).broadcast_to([P, v.shape[1], n])

        landed = [sem(f"gather_landed{q}") for q in range(RING)]
        attr_landed = [sem(f"attr_landed{q}") for q in range(RING)]
        weights_loaded = sem("weights_loaded")
        stage_done = sem("stage_done")
        dve_step, act_step, pool_step = sem("dve_step"), sem("act_step"), sem("pool_step")
        var_ready, dev_ready = sem("var_ready"), sem("dev_ready")
        bn_in, bn_sums = sem("bn_in"), sem("bn_sums")
        WLOADS = 14 + len(VECS)

        class Chain:

            def __init__(self, eng, s):
                self.eng, self.s, self.n = eng, s, 0

            def __call__(self, ins):
                ins.then_inc(self.s, 1)
                self.n += 1
                self.eng.wait_ge(self.s, self.n)

        ctx.enter_context(nc.allow_non_contiguous_dma(reason="columns of the slot tables, once"))
        block = ctx.enter_context(nc.Block())

        def steps3(engine, body):
            with engine.Fori(0, ITER3) as i:
                for q in range(RING3):
                    body(i, q)
            for q in range(SLOTS - ITER3 * RING3):
                body(ITER3, q)

        def exists(i, q):
            return not isinstance(i, int) or i * RING3 + q < SLOTS

        def fills3(i, q):
            return i * (RING3 // RING) + (q // RING + 1)

        def tile_registers(engine, i, ahead=0, step=RING):
            return nc.values_load_multi_w_load_instructions(
                ttab[0:1, 1, bass.ds(i * step + ahead, RING)], engines=[engine], min_val=0, max_val=NT - 1,
                skip_runtime_bounds_check_because="the slot table is clamped to the node tiles when it is made")[1]

        @block.sync
        def _(sp):
            def store_nodes(table, tile):
                return sp.dma_start(table.rearrange("(t p) f -> p t f", p=P), tile)

            sp.dma_start(jendi[0:1, 0, :], dst_t[:, P - 1:P].rearrange("t a -> a t")).then_inc(ev("ends_loaded"), 16)
            sp.wait_ge(ev("x_padding_zero"), 1)
            sp.dma_start(X[:, 0:NT - 1, :], x[0:(NT - 1) * P, :].rearrange("(t p) f -> p t f", p=P)).then_inc(ev("x_loaded"), 16)
            sp.dma_start(X[0:LAST, NT - 1, :], x[(NT - 1) * P:N, :]).then_inc(ev("x_loaded"), 16)
            w = [(W0s[:, :], W0), (resWs[:, :], resW), (W1Ts[:, :], W1T),
                 (bas[:, :, :], bases.rearrange("b d f -> d b f")),
                 (coef[:, 0:BASES], comps), (coef[:, BASES:BASES + 1], alpha),
                 (W1xs[:, :], W1x), (W1es[:, :], W1e),
                 (W2s[:, :, :], W2.rearrange("(k p) f -> p k f", p=P)),
                 (Wus[:, :, :], Wu.rearrange("(k p) f -> p k f", p=P)),
                 (B1[:, :], b1.partition_broadcast(P)), (G1[:, :], g1.partition_broadcast(P)),
                 (BE1[:, :], be1.partition_broadcast(P)), (b2c[:, :], b2.unsqueeze(1))]
            w += [(VEC[:, k, :], vec[name].partition_broadcast(P)) for k, name in enumerate(VECS)]
            assert len(w) == WLOADS
            for dst, s in w:
                sp.dma_start(dst, s).then_inc(weights_loaded, 16)
            sp.wait_ge(stage_done, STAGE["slots_made"])
            for k in range(2):
                sp.dma_start(slot_dram[k].rearrange("(g p) a -> p (g a)", p=P), sloti[:, k, :]).then_inc(ev("slots_stored"), 16)
            sp.wait_ge(ev("slots_stored"), 32)
            for k in range(2):
                sp.dma_start(ttab[0:1, k, :], slot_dram[k].rearrange("s a -> a s")).then_inc(ev("slots_loaded"), 16)
            sp.wait_ge(stage_done, STAGE["att_made"])
            store_nodes(as_dram, ADN[:, :, 4:8]).then_inc(ev("as_stored"), 16)
            store_nodes(h_dram, H[:, :, :]).then_inc(ev("h0_stored"), 16)
            if layers > 1:
                sp.wait_ge(stage_done, STAGE["h1_made"])
                store_nodes(h_dram, H[:, :, :]).then_inc(ev("h1_stored"), 16)
            if layers > 2:
                sp.wait_ge(stage_done, STAGE["zeros_made"])
                for k in range(NACC):
                    sp.dma_start(acc_dram[k].rearrange("(t p) f -> p t f", p=P),
                                 carve(T12, 0, NT + 1, D)).then_inc(ev("acc_zero_stored"), 16)
                sp.wait_ge(ev("scatters_done"), 1)
                for k, dst in enumerate([T1, T2, ACC1, ACC1B, H[:, :, :]]):
                    sp.dma_start(dst, acc_dram[k][0:NPAD, :].rearrange("(t p) f -> p t f", p=P)).then_inc(ev("acc_loaded"), 16)
            if layers > 3:
                sp.wait_ge(stage_done, STAGE["p_made"])
                store_nodes(p_dram, PN).then_inc(ev("p_stored"), 16)
                with sp.Fori(0, ITER) as i:
                    tiles = nc.values_load_multi_w_load_instructions(
                        ttab[0:1, 0, bass.ds(i * RING, RING)], engines=[ENG.SP], min_val=0, max_val=ET - 1,
                        skip_runtime_bounds_check_because="the slot table is clamped to the edge tiles when it is made")[1]
                    for q in range(RING):
                        sp.wait_ge(ev("l3_edge_part"), i * RING + q + 1)
                        sp.dma_start(A3[0:EDIM, q, :], attr_t[bass.ds(tiles[q], 1), :].rearrange("a (f e) -> (a f) e", f=EDIM)
                                     ).then_inc(attr_landed[q], 16)
            sp.wait_ge(stage_done, STAGE["out_made"])
            sp.dma_start(out[0:(NT - 1) * P, :].rearrange("(t p) f -> p t f", p=P), X[:, 0:NT - 1, :]).then_inc(ev("out_stored"), 16)
            sp.dma_start(out[(NT - 1) * P:N, :], X[0:LAST, NT - 1, :]).then_inc(ev("out_stored"), 16)
            sp.wait_ge(ev("out_stored"), 32)

        @block.gpsimd
        def _(pool):
            pool.iota(iota[:, :], pattern=[[1, P]], base=0, channel_multiplier=0,
                      allow_small_or_imprecise_dtypes=True).then_inc(ev("iotas"), 1)
            pool.iota(pcol[:, :], pattern=[[0, 1]], base=0, channel_multiplier=1,
                      allow_small_or_imprecise_dtypes=True).then_inc(ev("iotas"), 1)
            pool.iota(jcol[:, :], pattern=[[P, SG]], base=0, channel_multiplier=1,
                      allow_small_or_imprecise_dtypes=True).then_inc(ev("iotas"), 1)
            pool.iota(jend[0:1, 1, :], pattern=[[1, ET]], base=0, channel_multiplier=0,
                      allow_small_or_imprecise_dtypes=True).then_inc(ev("iotas"), 1)
            pool.wait_ge(stage_done, STAGE["slots_made"])
            for k, table in enumerate((dst_t, src_t, typ_t)):
                for g in range(SG):
                    pool.indirect_dma_start(RI[:, k, g, :], None, table[:, :],
                                            bass.IndirectOffsetOnAxis(ap=sloti[:, 0, g:g + 1], axis=0)
                                            ).then_inc(ev("rows_gathered"), 16)

            def carry_waits():
                pool.sem_inc(ev("pool_waits_met"), 1)

            def gather_loop(name, table, ring, free):
                staged = sem(name + "_indices_staged")
                with pool.Fori(0, ITER) as i:
                    for h in range(2):
                        pool.wait_ge(free, i * RING + (h + 1) * HALF)
                        pool.tensor_copy(istage[:, h, :], SRCI[:, bass.ds(i * RING + h * HALF, HALF)]).then_inc(staged, 1)
                        pool.wait_ge(staged, i * 2 + h + 1)
                        carry_waits()
                        for k in range(HALF):
                            q = h * HALF + k
                            pool.indirect_dma_start(ring[:, q, :], None, table[:, :],
                                                    bass.IndirectOffsetOnAxis(ap=istage[:, h, k:k + 1], axis=0)
                                                    ).then_inc(landed[q], 16)

            pool.wait_ge(ev("column_copied"), 5)
            pool.wait_ge(ev("as_stored"), 16)
            gather_loop("a", as_dram, GR[:, :, 0:HEADS], ev("a_ring_free"))
            pool.wait_ge(ev("h0_stored"), 16)
            gather_loop("l0", h_dram, GR[:, :, :], ev("l0_messages"))
            if layers > 1:
                pool.wait_ge(ev("h1_stored"), 16)
                gather_loop("l1", h_dram, GR[:, :, :], ev("l1_sums"))
            if layers > 2:
                base = 3 * ITER * 16
                staged = sem("l2_indices_staged")
                pool.wait_ge(ev("acc_zero_stored"), 16 * NACC)
                pool.wait_ge(stage_done, STAGE["scatter_rows_made"])
                with pool.Fori(0, ITER) as i:
                    for h in range(2):
                        for q in range(h * HALF, (h + 1) * HALF):
                            pool.wait_ge(landed[q], i * 16 + base)
                        pool.tensor_copy(istage[:, h, :], SCI[:, bass.ds(i * RING + h * HALF, HALF)]).then_inc(staged, 1)
                        pool.wait_ge(staged, i * 2 + h + 1)
                        for k in range(HALF):
                            q = h * HALF + k
                            pool.wait_ge(ev("l2_sum_copied"), i * RING + q + 3)
                            pool.wait_ge(landed[(q + NACC) % RING], i * 16 + base + (16 if q >= NACC else 0))
                            carry_waits()
                            pool.indirect_dma_start(acc_dram[q % NACC][:, :],
                                                    bass.IndirectOffsetOnAxis(ap=istage[:, h, k:k + 1], axis=0),
                                                    GR[:, q, :], None, compute_op=ALU.add).then_inc(landed[q], 16)
                for q in range(RING):
                    pool.wait_ge(landed[q], base + ITER * 16)
                pool.sem_inc(ev("scatters_done"), 1)
            if layers > 3:
                pool.wait_ge(ev("p_stored"), 16)
                base = 4 * ITER * 16
                staged = sem("l3_indices_staged")

                def gather_step(i, q):
                    c = q % RING
                    h, k = divmod(c, HALF)
                    if k == 0:
                        for b in range(c, c + HALF):
                            pool.wait_ge(landed[b], (fills3(i, q) - 1) * 16 + base)
                        pool.tensor_copy(istage[:, h, :], SRCI[:, bass.ds(i * RING3 + q, HALF)]).then_inc(staged, 1)
                        pool.wait_ge(staged, fills3(i, q) * 2 - 1 + h)
                    pool.wait_ge(ev("l3_edge_copied"), i * RING3 + q + 3)
                    carry_waits()
                    pool.indirect_dma_start(HC3[:, q % RING3, :], None, p_dram[:, :],
                                            bass.IndirectOffsetOnAxis(ap=istage[:, h, k:k + 1], axis=0),
                                            compute_op=ALU.add).then_inc(landed[c], 16)

                steps3(pool, gather_step)

        @block.tensor
        def _(pe):
            def transpose_nodes(tile):
                for t in range(NT):
                    last = pe.transpose(NODES[:, t, :], tile[:, t, :], ident[:, :])
                return last

            def project(tile_t, w):
                for t in range(NT):
                    last = pe.matmul(NODES[:, t, :], tile_t[:, t, :], w, start=True, stop=True)
                return last

            def node_sums(tile, n):
                pe.wait_ge(bn_in, n)
                for t in range(NT):
                    k = P if t < NT - 1 else LAST
                    last = pe.matmul(bank(7, D), ones[0:k, :], tile[0:k, t, :], start=(t == 0), stop=(t == NT - 1))
                last.then_inc(bn_sums, 1)

            pe.wait_ge(ev("ends_made"), 1)
            for a in range(0, ET, 512):
                n = min(512, ET - a)
                last = pe.matmul(WIDE[:, a:a + n], ones[0:1, :], jend[0:1, 0, a:a + n], start=True, stop=True)
            last.then_inc(ev("ends_spread"), 1)
            for n, (arr, b) in enumerate([(DL, 2), (SR, 4), (TR, 0), (HI, 2), (LO, 4)]):
                pe.wait_ge(stage_done, STAGE["rows_made"])
                if n >= 3:
                    pe.wait_ge(ev("column_copied"), n - 2)
                for g in range(SG):
                    last = pe.transpose(WIDE[:, b * 512 + g * P:b * 512 + (g + 1) * P], arr[:, g, :], ident[:, :])
                last.then_inc(ev("column_turned"), 1)
            pe.wait_ge(ev("x_loaded"), 32)
            pe.wait_ge(ev("column_copied"), 5)
            transpose_nodes(X).then_inc(ev("l0_xt"), 1)
            pe.wait_ge(ev("l0_xt_copied"), 1)
            pe.wait_ge(weights_loaded, 16 * WLOADS)
            project(T1, W0s[:, :]).then_inc(ev("l0_h"), 1)
            pe.wait_ge(stage_done, STAGE["base_max"])
            pe.transpose(bank(7, P)[0:1, :], wsum[:, 0:1], ident[:, :]).then_inc(ev("base_max_turned"), 1)
            pe.wait_ge(stage_done, STAGE["base_scale"])
            pe.matmul(bank(7, 2), ones[0:1, :], wsum[0:1, 2:4], start=True, stop=True).then_inc(ev("base_scale_spread"), 1)
            pe.wait_ge(stage_done, STAGE["a_zeros"])
            pe.wait_ge(stage_done, STAGE["att_made"])
            pe.matmul(bank(7, NT), ones[:, :], OTA[:, 0, 0, 0:NT], start=True, stop=False, skip_group_check=True
                      ).then_inc(ev("deg_cleared"), 1)
            pe.wait_ge(ev("deg_cleared"), 1)
            pe.sem_inc(ev("deg_ready"), 1)
            pe.wait_ge(ev("slots_loaded"), 32)
            pe.sem_inc(ev("a_turned"), 2)
            pe.sem_inc(ev("a_onehot_read"), 2)
            pe.sem_inc(ev("a_adas"), 2)
            with pe.Fori(0, ITER) as i:
                ts = tile_registers(ENG.PE, i)
                for h in range(2):
                    n = i * 2 + h + 1
                    pe.wait_ge(ev("a_onehot"), n)
                    pe.wait_ge(ev("a_turned_copied"), n)
                    for k in range(HALF):
                        last = pe.transpose(bank(h).bitcast(BF16)[:, k * P:(k + 1) * P], OHA[:, h, k, :], identb[:, :])
                    last.then_inc(ev("a_turned"), 1)
                    for k in range(HALF):
                        last = pe.matmul(bank(7, NT), LOA[:, h, k, :], HIA[:, h, k, 0:NT], start=False, stop=False,
                                         skip_group_check=True)
                    last.then_inc(ev("a_onehot_read"), 1)
                    pe.wait_ge(ev("a_turned_copied"), n + 2)
                    pe.wait_ge(ev("a_adas_copied"), n)
                    for k in range(HALF):
                        last = pe.matmul(bank(2 + h)[:, k * 8:(k + 1) * 8], OTA[:, h, k, :],
                                         ADN[:, bass.ds(ts[h * HALF + k], 1), :].rearrange("p a b -> p (a b)"),
                                         start=True, stop=True)
                    last.then_inc(ev("a_adas"), 1)
            pe.wait_ge(stage_done, STAGE["edge_values"])
            for hd in range(HEADS):
                if hd >= 2:
                    pe.wait_ge(ev("as_row_copied"), hd - 1)
                for g in range(SG):
                    last = pe.transpose(WIDE[:, (hd % 2) * 1024 + g * P:(hd % 2) * 1024 + (g + 1) * P],
                                        AS[:, g * P:(g + 1) * P, hd], ident[:, :])
                last.then_inc(ev("as_row"), 1)
            pe.wait_ge(stage_done, STAGE["slot_max_made"])
            for n in range(4):
                if n >= 2:
                    pe.wait_ge(ev("end_row_copied"), n - 1)
                for g in range(SG):
                    lane = 0 if n % 2 == 0 else P - 1
                    in_ = VT[:, g, :, lane] if n < 2 else DR[:, g, lane:lane + 1].broadcast_to([P, HEADS])
                    last = pe.transpose(WIDE[0:HEADS, (n % 2) * 1024 + g * P:(n % 2) * 1024 + (g + 1) * P], in_, ident[:, :])
                last.then_inc(ev("end_row"), 1)
            pe.wait_ge(stage_done, STAGE["carries_made"])
            for n, row in enumerate((R_CF, R_CB, R_LINK)):
                for g in range(SG):
                    last = pe.transpose(WIDE[:, 3072 + (n * SG + g) * HEADS:3072 + (n * SG + g + 1) * HEADS],
                                        row[:, g * P:(g + 1) * P], ident[0:HEADS, 0:HEADS])
            last.then_inc(ev("carries_turned"), 1)
            pe.wait_ge(stage_done, STAGE["max_made"])
            for n in range(HEADS + 1):
                if n >= 2:
                    pe.wait_ge(ev("max_copied"), n - 1)
                for g in range(SG):
                    in_ = VT[:, g, n, :] if n < HEADS else FIRST[:, g, :]
                    last = pe.transpose(WIDE[:, (n % 2) * 1024 + g * P:(n % 2) * 1024 + (g + 1) * P], in_, ident[:, :])
                last.then_inc(ev("max_turned"), 1)

            pe.wait_ge(ev("max_copied"), HEADS + 1)
            pe.sem_inc(ev("l0_sums"), RING)
            with pe.Fori(0, ITER) as i:
                for q in range(RING):
                    j = i * RING + q
                    pe.wait_ge(ev("l0_sums_added"), j + 1)
                    pe.wait_ge(ev("l0_messages"), j + 1 + RING)
                    pe.matmul(bank(q % MS, COLS0), OH[:, q % MS, :], MSG0[:, q % MS, :], start=True, stop=True
                              ).then_inc(ev("l0_sums"), 1)
            node_sums(T1, 1)
            node_sums(T1, 2)
            pe.wait_ge(stage_done, STAGE["l0_attention_out"])
            transpose_nodes(X).then_inc(ev("l0_xt2"), 1)
            pe.wait_ge(ev("l0_xt2_copied"), 1)
            project(ACC1, resWs[:, :]).then_inc(ev("l0_res"), 1)
            node_sums(H, 3)
            node_sums(H, 4)
            if layers > 1:
                pe.wait_ge(stage_done, STAGE["x1_made"])
                transpose_nodes(X).then_inc(ev("l1_xt"), 1)
                pe.wait_ge(ev("l1_xt_copied"), 1)
                project(T1, W1Ts[:, :]).then_inc(ev("l1_h"), 1)
                pe.wait_ge(stage_done, STAGE["l1_ready"])
                pe.sem_inc(ev("l1_sums"), RING)
                pe.sem_inc(ev("l1_types_turned"), 2)
                pe.sem_inc(ev("l1_coefs"), 2)

                def sources(j, r):
                    pe.wait_ge(ev("l1_repeats"), j + 1)
                    pe.matmul(bank(2 + r, P), SRCH[:, bass.ds(j, 1)].broadcast_to([P, P]), identh[:, :], start=True, stop=True
                              ).then_inc(ev("l1_sources"), 1)

                sources(0, 0)
                with pe.Fori(0, ITER) as i:
                    for h in range(2):
                        n = i * 2 + h + 1
                        pe.wait_ge(ev("l1_type_onehot"), n)
                        pe.wait_ge(ev("l1_coefs_copied"), n)
                        for k in range(HALF):
                            last = pe.transpose(bank(4 + h).bitcast(BF16)[:, k * P:(k + 1) * P], OHT[:, h, k, :], identb[:, :])
                        last.then_inc(ev("l1_types_turned"), 1)
                        for k in range(HALF):
                            q = h * HALF + k
                            j = i * RING + q
                            sources(j + 1, (q + 1) % 2)
                            pe.wait_ge(ev("l1_sums_added"), j + 1)
                            pe.wait_ge(ev("l1_onehot"), j + 1)
                            pe.wait_ge(landed[q], i * 16 + (2 * ITER * 16 + 16))
                            pe.matmul(bank(q % 2, D), OH[:, q % MS, :], GR[:, q, :], start=True, stop=True
                                      ).then_inc(ev("l1_sums"), 1)
                        pe.wait_ge(ev("l1_types_copied"), n)
                        for k in range(HALF):
                            c = 3 * P + k * BASES
                            last = pe.matmul(bank(4 + h)[:, c:c + BASES], OTT[0:REL, h, k, :], coef[:, 0:BASES], start=True, stop=True)
                        last.then_inc(ev("l1_coefs"), 1)
            if layers > 2:
                pe.wait_ge(stage_done, STAGE["l2_scaled"])
                transpose_nodes(T1).then_inc(ev("l2_xt"), 1)
                pe.wait_ge(ev("l2_xt_copied"), 1)
                for t in range(NT):
                    if t >= 4:
                        pe.wait_ge(ev("l2_y_copied"), t - 3)
                    pe.matmul(bank(t % 4), T2[:, t, :], bas[:, :, :].rearrange("p b f -> p (b f)"), start=True, stop=True
                              ).then_inc(ev("l2_y"), 1)
                pe.wait_ge(stage_done, STAGE["l2_y_parts"])
                for name in ("l2_turned", "l2_gathered", "l2_summed"):
                    pe.sem_inc(ev(name), 2)

                def turn(j, r):
                    pe.wait_ge(ev("l2_onehot"), j + 3)
                    pe.wait_ge(ev("l2_turned_copied"), j + 1)
                    pe.wait_ge(ev("l2_equal"), j + 1)
                    pe.transpose(bank(r, 64).bitcast(F16), OH2[:, r, :], identh[:, :])
                    pe.matmul(bank(6 + r, P), SRCH[:, bass.ds(j, 1)].broadcast_to([P, P]), identh[:, :], start=True, stop=True
                              ).then_inc(ev("l2_turned"), 1)

                def gather(j, r, t):
                    pe.wait_ge(ev("l2_turned_copied"), j + 3)
                    pe.wait_ge(ev("l2_mixed"), j + 1)
                    for k, part in enumerate(YP):
                        last = pe.matmul(bank(2 + r), OT2[:, r, :], part[:, bass.ds(t, 1), :].rearrange("p a b -> p (a b)"),
                                         start=(k == 0), stop=(k == 1))
                    last.then_inc(ev("l2_gathered"), 1)

                ts = tile_registers(ENG.PE, 0)
                turn(0, 0)
                turn(1, 1)
                gather(0, 0, ts[0])
                turn(2, 0)
                gather(1, 1, ts[1])
                with pe.Fori(0, ITER) as i:
                    ts = tile_registers(ENG.PE, i, 2)
                    for q in range(RING):
                        j = i * RING + q
                        r = q % 2
                        pe.wait_ge(ev("l2_mixed"), j + 3)
                        pe.wait_ge(ev("l2_equal"), j + 3)
                        pe.wait_ge(ev("l2_sum_copied"), j + 1)
                        pe.matmul(bank(4 + r, D), EQ[:, r, :], MSG2[:, r, :], start=True, stop=True).then_inc(ev("l2_summed"), 1)
                        turn(j + 3, 1 - r)
                        gather(j + 2, r, ts[q])
            if layers > 3:
                pe.wait_ge(stage_done, STAGE["x3_made"])
                transpose_nodes(X).then_inc(ev("l3_xt"), 1)
                pe.wait_ge(ev("l3_xt_copied"), 1)
                pe.wait_ge(stage_done, STAGE["l3_w1_centered"])
                for t in range(NT):
                    if t >= 4:
                        pe.wait_ge(ev("l3_p_copied"), t - 3)
                    pe.matmul(bank(t % 4, HID), T1[:, t, :], W1xs[:, :], start=True, stop=True).then_inc(ev("l3_p"), 1)
                pe.wait_ge(ev("l3_p_copied"), NT)
                pe.sem_inc(ev("l3_sums"), MS)
                pe.sem_inc(ev("l3_edge_part"), RING)

                def edge_part(i, q):
                    pe.wait_ge(attr_landed[q % RING], fills3(i, q) * 16)
                    pe.wait_ge(ev("l3_edge_copied"), i * RING3 + q + 1)
                    pe.matmul(bank(5 + q % 2, HID), A3[0:EDIM, q % RING, :], W1es[:, :], start=True, stop=True
                              ).then_inc(ev("l3_edge_part"), 1)

                def sum_step(i, q):
                    if exists(i, q + EDGE_AHEAD):
                        edge_part(i, q + EDGE_AHEAD)
                    j = i * RING3 + q
                    pe.wait_ge(ev("l3_sums_added"), j + 1)
                    pe.wait_ge(ev("l3_gelu"), j + 1 + MS)
                    pe.wait_ge(ev("l3_onehot"), j + 1)
                    pe.matmul(bank(q % MS, COLS3), OH[:, q % MS, :], GE[:, q % MS, :], start=True, stop=True
                              ).then_inc(ev("l3_sums"), 1)

                pe.wait_ge(stage_done, STAGE["l3_ready"])
                for q in range(EDGE_AHEAD):
                    edge_part(0, q)
                steps3(pe, sum_step)
                pe.wait_ge(ev("l3_sums_added"), SLOTS + MS)
                for k in range(2):
                    last = pe.transpose(WIDE[:, k * P:(k + 1) * P], W2s[:, k, :], ident[:, :])
                last.then_inc(ev("w2_turned"), 1)
                pe.wait_ge(ev("w2t_copied"), 1)
                for k in range(2):
                    last = pe.matmul(WIDE[:, k * P:(k + 1) * P], W2T[:, k, :], Wus[:, 1, :], start=True, stop=True)
                last = pe.matmul(WIDE[:, 2 * P:3 * P], b2c[:, :].broadcast_to([P, P]), Wus[:, 1, :], start=True, stop=True)
                last.then_inc(ev("w2u"), 1)
                pe.wait_ge(ev("w2u_copied"), 1)
                for n, src in enumerate((ACC3[:, :, 0:D], ACC3[:, :, D:2 * D], X)):
                    transpose_nodes(src).then_inc(ev("l3_turned"), 1)
                    pe.wait_ge(ev("l3_turned_copied"), n + 1)
                for t in range(NT):
                    pe.matmul(NODES[:, t, :], T1[:, t, :], W2U[:, 0, :], start=True, stop=False)
                    pe.matmul(NODES[:, t, :], T2[:, t, :], W2U[:, 1, :], start=False, stop=False)
                    last = pe.matmul(NODES[:, t, :], H[:, t, :], Wus[:, 0, :], start=False, stop=True)
                last.then_inc(ev("l3_u"), 1)

        @block.scalar
        def _(act):
            link = Chain(act, act_step)
            devs = [0]

            def copy(dst, src):
                return act.activation(dst, src, ACT.Copy)

            def deviation(n):
                devs[0] += 1
                act.wait_ge(var_ready, devs[0])
                act.activation(stat[:, 2, 0:n], stat[:, 1, 0:n], ACT.Sqrt).then_inc(dev_ready, 1)

            for n, (dst, b) in enumerate([(DLC[:, :], 2), (SRC[:, :], 4), (TYC[:, :], 0), (HIC, 2), (LOC, 4)]):
                act.wait_ge(ev("column_turned"), n + 1)
                if n == 1:
                    link(copy(SRCI[:, :], WIDE[:, b * 512:b * 512 + SPAD]))
                copy(dst, WIDE[:, b * 512:b * 512 + SPAD]).then_inc(ev("column_copied"), 1)
            act.wait_ge(ev("l0_xt"), 1)
            copy(T1, NODES).then_inc(ev("l0_xt_copied"), 1)
            act.wait_ge(ev("deg_ready"), 1)
            act.sem_inc(ev("a_turned_copied"), 2)
            act.sem_inc(ev("a_adas_copied"), 2)
            with act.Fori(0, ITER) as i:
                for h in range(2):
                    act.wait_ge(ev("a_turned"), i * 2 + h + 3)
                    act.wait_ge(ev("a_adas"), i * 2 + h + 1)
                    copy(OTA[:, h, :, :].rearrange("p k e -> p (k e)"), bank(h).bitcast(BF16)[:, 0:HALF * P]
                         ).then_inc(ev("a_turned_copied"), 1)
                    act.wait_ge(ev("a_adas"), i * 2 + h + 3)
                    copy(ADAS[:, bass.ds(i * RING + h * HALF, HALF), :],
                         bank(2 + h)[:, 0:HALF * 8].rearrange("p (k c) -> p k c", c=8)).then_inc(ev("a_adas_copied"), 1)
            act.wait_ge(stage_done, STAGE["ex_argument"])
            act.activation(EXF[:, :, 0:HEADS], ADAS[:, :, 0:HEADS], ACT.Exp).then_inc(ev("ex"), 1)
            act.wait_ge(stage_done, STAGE["loop_argument"])
            act.activation(SMN[:, 1, :, :], SMN[:, 0, :, :], ACT.Exp).then_inc(ev("loop_ex"), 1)
            deviation(D)
            deviation(NT)
            act.wait_ge(ev("l0_xt2"), 1)
            copy(ACC1, NODES).then_inc(ev("l0_xt2_copied"), 1)
            deviation(D)
            deviation(NT)
            if layers > 1:
                deviation(2 * NT)
                act.wait_ge(ev("l1_xt"), 1)
                copy(T1, NODES).then_inc(ev("l1_xt_copied"), 1)
                act.sem_inc(ev("l1_coefs_copied"), 2)
                with act.Fori(0, ITER) as i:
                    for h in range(2):
                        n = i * 2 + h + 1
                        act.wait_ge(ev("l1_types_turned"), n + 2)
                        act.wait_ge(ev("l1_coefs"), n)
                        copy(OTT[:, h, :, :].rearrange("p k e -> p (k e)"), bank(4 + h).bitcast(BF16)[:, 0:HALF * P]
                             ).then_inc(ev("l1_types_copied"), 1)
                        act.wait_ge(ev("l1_coefs"), n + 2)
                        copy(COEF[:, bass.ds(i * RING + h * HALF, HALF), :],
                             bank(4 + h)[:, 3 * P:3 * P + HALF * BASES].rearrange("p (k b) -> p k b", b=BASES)
                             ).then_inc(ev("l1_coefs_copied"), 1)
                deviation(NT)
                deviation(NT)
            if layers > 2:
                act.wait_ge(ev("l2_xt"), 1)
                copy(T2, NODES).then_inc(ev("l2_xt_copied"), 1)
                for t in range(NT):
                    act.wait_ge(ev("l2_y"), t + 1)
                    copy(YP[0][:, t, :], bank(t % 4)).then_inc(ev("l2_y_high"), 1)
                act.sem_inc(ev("l2_turned_copied"), 2)
                act.sem_inc(ev("l2_sum_copied"), 2)
                act.sem_inc(ev("l2_mixed_first"), 2)

                def copy_turned(j, r):
                    act.wait_ge(ev("l2_turned"), j + 3)
                    act.wait_ge(ev("l2_gathered"), j + 1)
                    copy(OT2[:, r, :], bank(r, 64).bitcast(F16)).then_inc(ev("l2_turned_copied"), 1)

                def mix_first(j, r):
                    act.wait_ge(ev("l2_gathered"), j + 3)
                    act.wait_ge(ev("l2_summed"), j + 1)
                    act.activation(MSG2[:, r, :], bank(2 + r, D), ACT.Copy,
                                   scale=COEF[:, bass.ds(j, 1), 0:1].rearrange("p a b -> p (a b)")
                                   ).then_inc(ev("l2_mixed_first"), 1)

                copy_turned(0, 0)
                copy_turned(1, 1)
                act.wait_ge(stage_done, STAGE["l2_coef_tail"])
                mix_first(0, 0)
                copy_turned(2, 0)
                with act.Fori(0, ITER) as i:
                    for q in range(RING):
                        j = i * RING + q
                        r = q % 2
                        mix_first(j + 1, 1 - r)
                        act.wait_ge(ev("l2_summed"), j + 3)
                        act.wait_ge(landed[q], i * 16 + 3 * ITER * 16)
                        copy(GR[:, q, :], bank(4 + r, D)).then_inc(ev("l2_sum_copied"), 1)
                        copy_turned(j + 3, 1 - r)
                deviation(NT)
            if layers > 3:
                act.wait_ge(ev("l3_xt"), 1)
                copy(T1, NODES).then_inc(ev("l3_xt_copied"), 1)
                act.sem_inc(ev("l3_edge_copied"), 2)
                act.sem_inc(ev("l3_squares"), 2)
                act.sem_inc(ev("l3_gelu"), MS)

                def copy_edge_part(i, q):
                    j = i * RING3 + q
                    act.wait_ge(ev("l3_edge_part"), j + 1 + RING)
                    act.wait_ge(ev("l3_scaled"), j + 1)
                    copy(HC3[:, q % RING3, :], bank(5 + q % 2, HID)).then_inc(ev("l3_edge_copied"), 1)

                def squares(i, q):
                    c = q % RING3
                    act.wait_ge(landed[q % RING], fills3(i, q) * 16 + 4 * ITER * 16)
                    act.wait_ge(ev("l3_squares"), i * RING3 + q + 1)
                    act.activation(SQ[:, q % 2, :], HC3[:, c, :], ACT.Square, accum_out=SS[:, 0, c:c + 1]
                                   ).then_inc(ev("l3_squares"), 1)

                def gelu_step(i, q):
                    if exists(i, q + COPY_AHEAD):
                        copy_edge_part(i, q + COPY_AHEAD)
                    if exists(i, q + SQUARES_AHEAD):
                        squares(i, q + SQUARES_AHEAD)
                    j = i * RING3 + q
                    act.wait_ge(ev("l3_normed"), j + 1)
                    act.wait_ge(ev("l3_sums"), j + 1)
                    act.activation(GE[:, q % MS, 0:HID], ZB[:, q % MS, :], ACT.Gelu).then_inc(ev("l3_gelu"), 1)

                act.wait_ge(stage_done, STAGE["l3_ready"])
                for q in range(COPY_AHEAD):
                    copy_edge_part(0, q)
                for q in range(SQUARES_AHEAD):
                    squares(0, q)
                steps3(act, gelu_step)
                act.wait_ge(ev("w2_turned"), 1)
                copy(W2T.rearrange("p k f -> p (k f)"), WIDE[:, 0:2 * P]).then_inc(ev("w2t_copied"), 1)
                act.wait_ge(ev("w2u"), 1)
                link(copy(W2U.rearrange("p k f -> p (k f)"), WIDE[:, 0:2 * P]))
                copy(B2U[:, :], WIDE[:, 2 * P:3 * P]).then_inc(ev("w2u_copied"), 1)
                for n, dst in enumerate((T1, T2, H[:, :, :])):
                    act.wait_ge(ev("l3_turned"), n + 1)
                    copy(dst, NODES).then_inc(ev("l3_turned_copied"), 1)
                deviation(NT)
                act.wait_ge(stage_done, STAGE["u_normed"])
                act.activation(T1, T1, ACT.Gelu).then_inc(ev("u_gelu"), 1)
                deviation(NT)

        @block.vector
        def _(v):
            link = Chain(v, dve_step)
            devs, bns, stages = [0], [0], []

            def made(name):
                v.sem_inc(stage_done, STAGE[name] - len(stages))
                stages.extend([name] * (STAGE[name] - len(stages)))

            def tt(out, a, b, op):
                return v.tensor_tensor(out, a, b, op)

            def ts1(out, a, s, op, s2=None, op2=None):
                if op2 is None:
                    return v.tensor_scalar(out, a, s, None, op)
                return v.tensor_scalar(out, a, s, s2, op, op2)

            def inverse_deviation(n):
                devs[0] += 1
                v.wait_ge(dev_ready, devs[0])
                link(v.reciprocal(stat[:, 3, 0:n], stat[:, 2, 0:n]))

            def layer_norm(dst, src, centered):
                link(v.tensor_reduce(stat[:, 0, 0:NT], src, AX_X, ALU.add))
                link(ts1(stat[:, 0, 0:NT], stat[:, 0, 0:NT], 1.0 / D, ALU.mult))
                link(tt(centered, src, over_features(stat[:, 0, 0:NT]), ALU.subtract))
                link(tt(dst, centered, centered, ALU.mult))
                link(v.tensor_reduce(stat[:, 1, 0:NT], dst, AX_X, ALU.add))
                link(ts1(stat[:, 1, 0:NT], stat[:, 1, 0:NT], 1.0 / D, ALU.mult, EPS, ALU.add))
                v.sem_inc(var_ready, 1)
                inverse_deviation(NT)
                link(tt(dst, centered, over_features(stat[:, 3, 0:NT]), ALU.mult))

            def affine(tile, gain, shift):
                link(tt(tile, tile, over_tiles(gain), ALU.mult))
                link(tt(tile, tile, over_tiles(shift), ALU.add))

            def batch_norm(tile, squares, gain, shift):
                v.sem_inc(bn_in, 1)
                v.wait_ge(bn_sums, bns[0] + 1)
                link(ts1(stat[:, 0, :], bank(7, D), 1.0 / N, ALU.mult))
                link(tt(squares, tile, over_tiles(stat[:, 0, :]), ALU.subtract))
                link(tt(tile, squares, squares, ALU.mult))
                v.sem_inc(bn_in, 1)
                v.wait_ge(bn_sums, bns[0] + 2)
                bns[0] += 2
                link(ts1(stat[:, 1, :], bank(7, D), 1.0 / N, ALU.mult, EPS, ALU.add))
                v.sem_inc(var_ready, 1)
                inverse_deviation(D)
                link(tt(stat[:, 3, :], stat[:, 3, :], gain, ALU.mult))
                link(tt(tile, squares, over_tiles(stat[:, 3, :]), ALU.mult))
                link(tt(tile, tile, over_tiles(shift), ALU.add))

            def leaky(out, z):
                return v.scalar_tensor_tensor(out=out, in0=z, scalar=0.2, in1=z, op0=ALU.mult, op1=ALU.max)

            v.memset(X[:, NT - 1, :], 0.0).then_inc(ev("x_padding_zero"), 1)
            link(v.memset(ones[:, :], 1.0))
            v.wait_ge(ev("iotas"), 4)
            link(ts1(ident[:, :], iota[:, :], pcol[:, 0:1], ALU.is_equal))
            link(ts1(identb[:, :], iota[:, :], pcol[:, 0:1], ALU.is_equal))
            link(v.tensor_copy(identh[:, :], ident[:, :]))
            link(ts1(tri[:, :], iota[:, :], pcol[:, 0:1], ALU.is_lt))
            link(ts1(trashcol[:, 0:1], pcol[:, :], float(TRASH), ALU.add))
            link(ts1(trashcol[:, 1:2], pcol[:, :], float(TRASH - NPAD // 2), ALU.add))
            link(v.tensor_copy(iotab[:, :], iota[:, :]))
            v.wait_ge(ev("ends_loaded"), 16)
            link(v.tensor_single_scalar(jendi[0:1, 1, :], jendi[0:1, 0, :], 7, ALU.arith_shift_right))
            link(v.tensor_copy(jend[0:1, 0, :], jendi[0:1, 1, :]))
            tt(jend[0:1, 0, :], jend[0:1, 0, :], jend[0:1, 1, :], ALU.add).then_inc(ev("ends_made"), 1)
            v.wait_ge(ev("ends_spread"), 1)
            for g in range(SG):
                link(v.tensor_scalar(T12[:, 0:ET], WIDE[:, 0:ET], jcol[:, g:g + 1], 0.0, ALU.is_lt, ALU.add,
                                     accum_out=slots[:, 0, g:g + 1]))
            link(ts1(slots[:, 0, :], slots[:, 0, :], float(ET - 1), ALU.min))
            link(tt(slots[:, 1, :], jcol[:, :], slots[:, 0, :], ALU.subtract))
            link(ts1(slots[:, 1, :], slots[:, 1, :], float(NT - 1), ALU.min))
            link(ts1(slots[:, 2, :], slots[:, 1, :], -float(P), ALU.mult))
            link(v.tensor_copy(sloti[:, :, :], slots[:, 0:2, :]))
            made("slots_made")
            v.wait_ge(ev("rows_gathered"), 16 * 3 * SG)
            link(v.tensor_copy(DR, RI[:, 0]))
            link(v.tensor_copy(SR, RI[:, 1]))
            link(v.tensor_copy(TR, RI[:, 2]))
            link(v.tensor_single_scalar(HII, RI[:, 1], 7, ALU.arith_shift_right))
            link(v.tensor_copy(HI, HII))
            link(v.scalar_tensor_tensor(out=LO, in0=HI, scalar=-float(P), in1=SR, op0=ALU.mult, op1=ALU.add))
            for g in range(SG):
                link(ts1(DL[:, g, :], DR[:, g, :], slots[:, 2, g:g + 1], ALU.add))
            link(ts1(VALID, DL, 0.0, ALU.is_ge))
            link(v.scalar_tensor_tensor(out=VALID, in0=DL, scalar=float(P), in1=VALID, op0=ALU.is_lt, op1=ALU.mult))
            link(v.scalar_tensor_tensor(out=HI, in0=HI, scalar=-float(P), in1=VALID, op0=ALU.add, op1=ALU.mult))
            link(ts1(HI, HI, float(P), ALU.add))
            made("rows_made")
            v.wait_ge(weights_loaded, 16 * WLOADS)
            link(ts1(coef[:, 0:BASES], coef[:, 0:BASES], coef[:, BASES:BASES + 1], ALU.mult))
            flat_bases = bas[:, :, :].rearrange("p b f -> p (b f)")
            link(v.tensor_reduce(wsum[:, 0:1], flat_bases, AX_X, ALU.max))
            link(v.tensor_reduce(wsum[:, 1:2], flat_bases, AX_X, ALU.min))
            link(v.scalar_tensor_tensor(out=wsum[:, 0:1], in0=wsum[:, 1:2], scalar=-1.0, in1=wsum[:, 0:1], op0=ALU.mult, op1=ALU.max))
            made("base_max")
            v.wait_ge(ev("l0_h"), 1)
            link(v.tensor_copy(H[:, :, :], NODES))
            for n, (name, lo) in enumerate((("att_dst", 0), ("att_src", 4))):
                link(tt(T2, H[:, :, :], over_tiles(V(name)), ALU.mult))
                link(v.tensor_reduce(ADN[:, :, lo:lo + 4], T2.rearrange("p t (h c) -> p t h c", h=HEADS), AX_X, ALU.add))
            made("att_made")
            v.wait_ge(ev("base_max_turned"), 1)
            link(v.tensor_reduce(wsum[0:1, 1:2], bank(7, P)[0:1, :], AX_X, ALU.max))
            link(ts1(wsum[0:1, 1:2], wsum[0:1, 1:2], 2.0 ** -100, ALU.max))
            link(v.tensor_single_scalar(scalei[0:1, 0:1], wsum[0:1, 1:2].bitcast(I32), 0x7F800000, ALU.bitwise_and))
            link(ts1(wsum[0:1, 2:3], scalei[0:1, 0:1].bitcast(F32), 2.0 ** -7, ALU.mult))
            link(v.reciprocal(wsum[0:1, 3:4], wsum[0:1, 2:3]))
            made("base_scale")
            v.wait_ge(ev("base_scale_spread"), 1)
            link(v.tensor_copy(wsum[:, 2:4], bank(7, 2)))
            link(ts1(bas[:, :, :], bas[:, :, :], wsum[:, 3:4], ALU.mult))
            link(ts1(coef[:, 0:BASES], coef[:, 0:BASES], wsum[0:REL, 2:3], ALU.mult))
            link(v.memset(OTA[:, 0, 0, :], 0.0))
            link(v.memset(AS[:, SLOTS:SPAD, :], 0.0))
            link(v.memset(ADAS[:, SLOTS:SPAD, :], 0.0))
            made("a_zeros")
            v.wait_ge(ev("column_copied"), 5)
            link(ts1(SRC[:, :], SRC[:, :], -float(NPAD // 2), ALU.add))
            v.sem_inc(ev("a_ring_free"), RING)
            with v.Fori(0, ITER) as i:
                for h in range(2):
                    n = i * 2 + h + 1
                    at = i * RING + h * HALF
                    v.wait_ge(ev("a_onehot_read"), n)
                    v.wait_ge(ev("a_turned"), n)
                    for k in range(HALF):
                        j = at + k
                        ts1(OHA[:, h, k, :], iotab[:, :], DLC[:, bass.ds(j, 1)], ALU.is_equal)
                        ts1(LOA[:, h, k, :], iotab[:, :], LOC[:, bass.ds(j, 1)], ALU.is_equal)
                        last = ts1(HIA[:, h, k, 0:NT], iotab[:, 0:NT], HIC[:, bass.ds(j, 1)], ALU.is_equal)
                    last.then_inc(ev("a_onehot"), 1)
                    for q in range(h * HALF, (h + 1) * HALF):
                        v.wait_ge(landed[q], i * 16 + 16)
                    v.tensor_copy(AS[:, bass.ds(at, HALF), :], GR[:, h * HALF:(h + 1) * HALF, 0:HEADS]).then_inc(ev("a_ring_free"), HALF)
            v.wait_ge(ev("a_ring_free"), SLOTS + RING)
            v.wait_ge(ev("a_adas_copied"), 2 * ITER + 2)
            v.wait_ge(ev("a_onehot_read"), 2 * ITER + 2)
            link(v.tensor_copy(DIS[:, 1, :], bank(7, NT)))
            made("edge_values")
            link(tt(FIRST[:, :, 1:P], DR[:, :, 1:P], DR[:, :, 0:P - 1], ALU.is_equal))
            link(v.memset(FIRST[:, :, 0:1], 0.0))
            link(ts1(AT, FIRST.unsqueeze(2).broadcast_to([P, SG, HEADS, P]), BIG, ALU.mult, -BIG, ALU.add))
            for hd in range(HEADS):
                v.wait_ge(ev("as_row"), hd + 1)
                b = (hd % 2) * 1024
                last = v.tensor_copy(VT[:, :, hd, :], WIDE[:, b:b + SPAD].rearrange("p (g l) -> p g l", l=P))
                last.then_inc(ev("as_row_copied"), 1)
            v.wait_ge(ev("as_row_copied"), HEADS)
            flat = SPAD * HEADS
            link(v.tensor_tensor_scan(ACCB[:, 0:flat], T12[:, flat:2 * flat], T12[:, 0:flat], -BIG, ALU.add, ALU.max))
            link(ts1(AT[:, :, :, 0:P - 1], FIRST[:, :, 1:P].unsqueeze(2).broadcast_to([P, SG, HEADS, P - 1]), BIG, ALU.mult,
                     -BIG, ALU.add))
            link(v.memset(AT[:, :, :, P - 1:P], -BIG))
            link(v.tensor_tensor_scan(T12[:, 0:flat][:, ::-1], T12[:, flat:2 * flat][:, ::-1], ACCB[:, 0:flat][:, ::-1],
                                      -BIG, ALU.add, ALU.max))
            made("slot_max_made")
            for n, row in enumerate((R_FM, R_LM, R_FD, R_LD)):
                v.wait_ge(ev("end_row"), n + 1)
                b = (n % 2) * 1024
                link(v.tensor_copy(row, WIDE[0:HEADS, b:b + SPAD]))
                v.sem_inc(ev("end_row_copied"), 1)
            link(tt(R_W, R_FD, R_LD, ALU.is_equal))
            link(v.memset(R_LINK[:, 0:1], 0.0))
            link(tt(R_LINK[:, 1:SPAD], R_FD[:, 1:SPAD], R_LD[:, 0:SPAD - 1], ALU.is_equal))
            link(tt(R_A, R_LINK, R_W, ALU.mult))
            link(ts1(R_A, R_A, BIG, ALU.mult, -BIG, ALU.add))
            link(v.tensor_tensor_scan(R_OUT, R_A, R_LM, -BIG, ALU.add, ALU.max))
            link(v.memset(R_CF[:, 0:1], -BIG))
            link(ts1(R_CF[:, 1:SPAD], R_LINK[:, 1:SPAD], BIG, ALU.mult, -BIG, ALU.add))
            link(tt(R_CF[:, 1:SPAD], R_CF[:, 1:SPAD], R_OUT[:, 0:SPAD - 1], ALU.add))
            link(tt(R_A[:, 0:SPAD - 1], R_LINK[:, 1:SPAD], R_W[:, 0:SPAD - 1], ALU.mult))
            link(v.memset(R_A[:, SPAD - 1:SPAD], 0.0))
            link(ts1(R_A, R_A, BIG, ALU.mult, -BIG, ALU.add))
            link(v.tensor_tensor_scan(R_OUT[:, ::-1], R_A[:, ::-1], R_FM[:, ::-1], -BIG, ALU.add, ALU.max))
            link(v.memset(R_CB[:, SPAD - 1:SPAD], -BIG))
            link(ts1(R_CB[:, 0:SPAD - 1], R_LINK[:, 1:SPAD], BIG, ALU.mult, -BIG, ALU.add))
            link(tt(R_CB[:, 0:SPAD - 1], R_CB[:, 0:SPAD - 1], R_OUT[:, 1:SPAD], ALU.add))
            made("carries_made")
            v.wait_ge(ev("carries_turned"), 1)
            link(v.tensor_copy(carry[:, :, :, :].rearrange("p n g h -> p (n g h)"), WIDE[:, 3072:3072 + 3 * SG * HEADS]))
            for c, lane in ((0, 0), (1, P - 1)):
                link(tt(AT[:, :, 0, :], DR, DR[:, :, lane:lane + 1].broadcast_to([P, SG, P]), ALU.is_equal))
                link(ts1(AT[:, :, 0, :], AT[:, :, 0, :], BIG, ALU.mult, -BIG, ALU.add))
                for g in range(SG):
                    for hd in range(HEADS):
                        last = v.scalar_tensor_tensor(out=VT[:, g, hd, :], in0=AT[:, g, 0, :], scalar=carry[:, c, g, hd:hd + 1],
                                                      in1=VT[:, g, hd, :], op0=ALU.add, op1=ALU.max)
                link(last)
            link(ts1(FIRST[:, :, 0], carry[:, 2, :, 0], 1.0, ALU.mult))
            link(v.scalar_tensor_tensor(out=FIRST, in0=FIRST, scalar=0.5, in1=VALID, op0=ALU.is_lt, op1=ALU.mult))
            made("max_made")
            for n in range(HEADS + 1):
                v.wait_ge(ev("max_turned"), n + 1)
                b = (n % 2) * 1024
                dst = MT[:, :, n] if n < HEADS else FIRSTC
                link(v.tensor_copy(dst, WIDE[:, b:b + SPAD]))
                v.sem_inc(ev("max_copied"), 1)
            link(tt(MT, MT, ADAS[:, :, 4:8], ALU.max))
            link(tt(EXF[:, :, 4:8], MT, FIRSTC.unsqueeze(2).broadcast_to([P, SPAD, HEADS]), ALU.mult))
            link(v.tensor_copy(EXF[:, :, 8], FIRSTC))
            link(tt(AS, AS, ADAS[:, :, 0:4], ALU.add))
            link(leaky(AS, AS))
            link(tt(MT, MT, ADAS[:, :, 0:4], ALU.add))
            link(leaky(MT, MT))
            link(tt(ADAS[:, :, 0:4], AS, MT, ALU.subtract))
            made("ex_argument")
            v.wait_ge(ev("ex"), 1)

            def zero_sums():
                link(v.memset(ACCB[:, :], 0.0))

            def add_sums(name, acc, q, j, t, credit, banks=MS):
                v.wait_ge(ev(name + "_sums"), j + 1 + credit)
                v.wait_ge(ev(name + "_sums_added"), j + banks)
                a = acc[:, bass.ds(t, 1), :].rearrange("p a b -> p (a b)")
                tt(a, a, bank(q % banks, acc.shape[-1]), ALU.add).then_inc(ev(name + "_sums_added"), 1)

            zero_sums()
            v.wait_ge(ev("slots_loaded"), 32)
            v.sem_inc(ev("l0_sums_added"), MS)
            v.sem_inc(ev("l0_messages"), RING)
            with v.Fori(0, ITER) as i:
                tiles = tile_registers(ENG.DVE, i)
                for q in range(RING + 1):
                    if q < RING:
                        j = i * RING + q
                        r = q % MS
                        v.wait_ge(ev("l0_sums"), j + 1 + RING - MS)
                        ts1(OH[:, r, :], iota[:, :], DLC[:, bass.ds(j, 1)], ALU.is_equal)
                        v.tensor_copy(MSG0[:, r, D:COLS0], EXF[:, bass.ds(j, 1), :].rearrange("p a b -> p (a b)")
                                      )
                        v.wait_ge(landed[q], i * 16 + (ITER * 16 + 16))
                        tt(MSG0[:, r, 0:D].rearrange("p (h c) -> p h c", h=HEADS), GR[:, q, :].rearrange("p (h c) -> p h c", h=HEADS),
                           EXF[:, bass.ds(j, 1), 0:HEADS].rearrange("p a b -> p (a b)").unsqueeze(2).broadcast_to([P, HEADS, HC]),
                           ALU.mult).then_inc(ev("l0_messages"), 1)
                    if q >= 1:
                        add_sums("l0", ACC0, q - 1, i * RING + q - 1, tiles[q - 1], RING)
            v.wait_ge(ev("l0_sums_added"), SLOTS + MS)
            EXL = SMN[:, 1, :, :]
            link(ts1(HAS[:, :], ACC0[:, :, COLS0 - 1], BIG, ALU.mult, -BIG, ALU.add))
            link(tt(SMN[:, 2, :, :], ACC0[:, :, D + 4:D + 8], HAS[:, :].unsqueeze(2).broadcast_to([P, NT, HEADS]), ALU.add))
            link(tt(SMN[:, 2, :, :], SMN[:, 2, :, :], ADN[:, :, 4:8], ALU.max))
            link(tt(SMN[:, 2, :, :], SMN[:, 2, :, :], ADN[:, :, 0:4], ALU.add))
            link(leaky(SMN[:, 2, :, :], SMN[:, 2, :, :]))
            link(tt(SMN[:, 3, :, :], ADN[:, :, 4:8], ADN[:, :, 0:4], ALU.add))
            link(leaky(SMN[:, 3, :, :], SMN[:, 3, :, :]))
            link(tt(SMN[:, 0, :, :], SMN[:, 3, :, :], SMN[:, 2, :, :], ALU.subtract))
            made("loop_argument")
            v.wait_ge(ev("loop_ex"), 1)
            link(tt(SMN[:, 2, :, :], ACC0[:, :, D:D + 4], EXL, ALU.add))
            link(v.reciprocal(SMN[:, 3, :, :], SMN[:, 2, :, :]))
            by_head = [P, NT, HEADS, HC]
            T1H, HH = T1.rearrange("p t (h c) -> p t h c", h=HEADS), H[:, :, :].rearrange("p t (h c) -> p t h c", h=HEADS)
            link(tt(T1H, HH, EXL.unsqueeze(3).broadcast_to(by_head), ALU.mult))
            link(tt(T1, T1, ACC0[:, :, 0:D], ALU.add))
            link(tt(T1H, T1H, SMN[:, 3, :, :].unsqueeze(3).broadcast_to(by_head), ALU.mult))
            link(tt(T1, T1, over_tiles(V("bias")), ALU.add))
            batch_norm(T1, T2, V("bn_g"), V("bn_b"))
            layer_norm(T1, T1, T2)
            affine(T1, V("ln_g"), V("ln_b"))
            made("l0_attention_out")
            v.wait_ge(ev("l0_res"), 1)
            link(tt(H[:, :, :], NODES, over_tiles(V("res_b")), ALU.add))
            batch_norm(H[:, :, :], T2, V("bnres_g"), V("bnres_b"))
            link(tt(T1, T1, H[:, :, :], ALU.add))
            link(v.scalar_tensor_tensor(out=X[:, :, :], in0=T1, scalar=0.0, in1=X[:, :, :], op0=ALU.max, op1=ALU.add))
            layer_norm(X[:, :, :], X[:, :, :], T2)
            if layers > 1:
                made("x1_made")
                link(ts1(stat[:, 1, 0:NT], DIS[:, 1, :], 1.0, ALU.add))
                link(ts1(stat[:, 1, NT:2 * NT], DIS[:, 1, :], 1.0, ALU.max))
                link(ts1(HAS[:, :], DIS[:, 1, :], 0.0, ALU.is_gt))
                v.sem_inc(var_ready, 1)
                inverse_deviation(2 * NT)
                link(v.tensor_copy(DIS[:, 0, :], stat[:, 3, 0:NT]))
                link(tt(DIS[:, 1, :], stat[:, 3, NT:2 * NT], HAS[:, :], ALU.mult))
                v.wait_ge(ev("l1_h"), 1)
                link(tt(H[:, :, :], NODES, over_tiles(V("b_l1")), ALU.add))
                link(tt(H[:, :, :], H[:, :, :], over_features(DIS[:, 0, :]), ALU.mult))
                made("h1_made")
                zero_sums()
                link(v.memset(T12[:, 0:(NT + 1) * D], 0.0))
                made("zeros_made")
                link(v.tensor_copy(SRCH, SRC[:, :]))
                link(v.memset(OHT, 0.0))
                link(v.memset(DUP, 0.0))
                v.sem_inc(ev("l1_sums_added"), 2)
                v.sem_inc(ev("l1_repeats"), 2)
                made("l1_ready")
                with v.Fori(0, ITER) as i:
                    tiles = tile_registers(ENG.DVE, i)
                    for h in range(2):
                        n = i * 2 + h + 1
                        at = i * RING + h * HALF
                        v.wait_ge(ev("l1_types_turned"), n)
                        for k in range(HALF):
                            last = ts1(OHT[:, h, k, 0:REL], iotab[:, 0:REL], TYC[:, bass.ds(at + k, 1)], ALU.is_equal)
                        last.then_inc(ev("l1_type_onehot"), 1)
                        for k in range(HALF):
                            q = h * HALF + k
                            j = at + k
                            v.wait_ge(ev("l1_sums"), j + 1 + RING - MS)
                            ts1(OH[:, q % MS, :], iota[:, :], DLC[:, bass.ds(j, 1)], ALU.is_equal).then_inc(ev("l1_onehot"), 1)
                            v.wait_ge(ev("l1_sources"), j + 1)
                            v.wait_ge(ev("l1_repeats"), j + 1)
                            v.scalar_tensor_tensor(out=JUNK[:, q % 2, :], in0=bank(2 + q % 2, P),
                                                   scalar=SRC[:, bass.ds(j, 1)], in1=tri[:, :], op0=ALU.is_equal,
                                                   op1=ALU.mult, accum_out=DUP[:, bass.ds(j, 1)]).then_inc(ev("l1_repeats"), 1)
                            if q >= 1:
                                add_sums("l1", ACC1, q - 1, j - 1, tiles[q - 1], RING, 2)
                    add_sums("l1", ACC1, RING - 1, i * RING + RING - 1, tiles[RING - 1], RING, 2)
                v.wait_ge(ev("l1_repeats"), SLOTS + 2)
                link(ts1(FIRSTSRC, DUP, 0.5, ALU.is_lt))
                link(v.scalar_tensor_tensor(out=FIRSTSRC, in0=SRC[:, :], scalar=trashcol[:, 1:2], in1=FIRSTSRC,
                                            op0=ALU.subtract, op1=ALU.mult))
                link(ts1(SCI, FIRSTSRC, trashcol[:, 0:1], ALU.add))
                v.wait_ge(ev("l1_coefs_copied"), 2 * ITER + 2)
                made("scatter_rows_made")
                v.wait_ge(ev("l1_sums_added"), SLOTS + 2)
                v.wait_ge(ev("h1_stored"), 16)
                v.wait_ge(ev("acc_zero_stored"), 16 * NACC)
                link(tt(T1, ACC1, H[:, :, :], ALU.add))
                link(tt(T1, T1, over_features(DIS[:, 0, :]), ALU.mult))
                link(ts1(T1, T1, 0.0, ALU.max))
                layer_norm(T1, T1, T2)
                affine(T1, V("g_l1"), V("be_l1"))
                link(v.scalar_tensor_tensor(out=X[:, :, :], in0=X[:, :, :], scalar=2.0, in1=T1, op0=ALU.mult, op1=ALU.add))
                layer_norm(X[:, :, :], X[:, :, :], T2)
            if layers > 2:
                link(tt(T1, X[:, :, :], over_features(DIS[:, 1, :]), ALU.mult))
                made("l2_scaled")
                for t in range(NT):
                    v.wait_ge(ev("l2_y_high"), t + 1)
                    tt(YP[1][:, t, :], bank(t % 4), YP[0][:, t, :], ALU.subtract).then_inc(ev("l2_y_copied"), 1)
                v.wait_ge(ev("l2_y_copied"), NT)
                link(v.memset(COEF[:, SLOTS:SPAD, :], 0.0))
                made("l2_y_parts")
                made("l2_coef_tail")
                v.sem_inc(ev("l2_onehot"), 2)
                v.sem_inc(ev("l2_equal"), 2)
                v.sem_inc(ev("l2_mixed"), 2)

                def onehot(j, r):
                    v.wait_ge(ev("l2_turned"), j + 1)
                    ts1(OH2[:, r, :], iotab[:, :], DLC[:, bass.ds(j, 1)], ALU.is_equal).then_inc(ev("l2_onehot"), 1)

                def equal(j, r):
                    v.wait_ge(ev("l2_turned"), j + 3)
                    v.wait_ge(ev("l2_summed"), j + 1)
                    ts1(EQ[:, r, :], bank(6 + r, P), SRC[:, bass.ds(j, 1)], ALU.is_equal).then_inc(ev("l2_equal"), 1)

                onehot(0, 0)
                onehot(1, 1)
                onehot(2, 0)
                equal(0, 0)
                with v.Fori(0, ITER) as i:
                    for q in range(RING):
                        j = i * RING + q
                        r = q % 2

                        def mix(b):
                            v.scalar_tensor_tensor(out=MSG2[:, r, :], in0=bank(2 + r)[:, b * D:(b + 1) * D],
                                                   scalar=COEF[:, bass.ds(j, 1), b:b + 1].rearrange("p a b -> p (a b)"),
                                                   in1=MSG2[:, r, :], op0=ALU.mult, op1=ALU.add
                                                   ).then_inc(ev("l2_mixed" if b == BASES - 1 else "l2_mixing"), 1)

                        v.wait_ge(ev("l2_mixed_first"), j + 3)
                        mix(1)
                        onehot(j + 3, 1 - r)
                        v.wait_ge(ev("l2_mixing"), j * 2 + 1)
                        mix(2)
                        equal(j + 1, 1 - r)
                        v.wait_ge(ev("l2_mixing"), j * 2 + 2)
                        mix(3)
                v.wait_ge(ev("acc_loaded"), 16 * NACC)
                for part in (T2, ACC1, ACC1B, H[:, :, :]):
                    link(tt(T1, T1, part, ALU.add))
                link(tt(T1, T1, over_features(DIS[:, 1, :]), ALU.mult))
                link(tt(X[:, :, :], X[:, :, :], T1, ALU.add))
                layer_norm(X[:, :, :], X[:, :, :], T2)
            if layers > 3:
                made("x3_made")
                for n, w in enumerate((W1xs[:, :], W1es[:, :], B1[:, :])):
                    k = w.shape[0]
                    link(v.tensor_reduce(wsum[0:k, n:n + 1], w, AX_X, ALU.add))
                    link(ts1(wsum[0:k, n:n + 1], wsum[0:k, n:n + 1], -1.0 / HID, ALU.mult))
                    link(ts1(w, w, wsum[0:k, n:n + 1], ALU.add))
                link(ts1(G1[:, :], G1[:, :], HID ** 0.5, ALU.mult))
                made("l3_w1_centered")
                for t in range(NT):
                    v.wait_ge(ev("l3_p"), t + 1)
                    tt(PN[:, t, :], bank(t % 4, HID), B1[:, :], ALU.add).then_inc(ev("l3_p_copied"), 1)
                v.wait_ge(ev("l3_p_copied"), NT)
                made("p_made")
                zero_sums()
                link(v.memset(GE, 1.0))
                v.sem_inc(ev("l3_sums_added"), MS)
                v.sem_inc(ev("l3_scaled"), RING3)
                made("l3_ready")

                def inverse(i, q, n):
                    at = q % RING3
                    vv, half_exp, y, a = [SS[:, k, at:at + HALF] for k in (1, 2, 3, 2)]
                    if n == 0:
                        v.wait_ge(ev("l3_squares"), i * RING3 + q + HALF + 2)
                    else:
                        v.wait_ge(ev("l3_inverse"), (i * (RING3 // HALF) + q // HALF) * INV_STEPS + n)
                    if n == 0:
                        op = ts1(vv, SS[:, 0, at:at + HALF], HID * EPS, ALU.add)
                    elif n == 1:
                        op = v.tensor_single_scalar(half_exp.bitcast(I32), vv.bitcast(I32), 1, ALU.arith_shift_right)
                    elif n == 2:
                        op = ts1(y.bitcast(I32), half_exp.bitcast(I32), -1.0, ALU.mult, float(0x5f3759df), ALU.add)
                    elif n % 3 == 0:
                        op = v.scalar_tensor_tensor(out=a, in0=y, scalar=-0.5, in1=y, op0=ALU.mult, op1=ALU.mult)
                    elif n % 3 == 1:
                        op = tt(a, a, vv, ALU.mult)
                    else:
                        op = v.scalar_tensor_tensor(out=y, in0=a, scalar=1.5, in1=y, op0=ALU.add, op1=ALU.mult)
                    op.then_inc(ev("l3_inverse"), 1)

                def norm(i, q):
                    j = i * RING3 + q
                    c, r = q % RING3, q % MS
                    h, k = q // HALF * HALF + HALF, q % HALF
                    ahead = exists(i, h) and 3 * k < INV_STEPS
                    if k == 0:
                        v.wait_ge(ev("l3_inverse"), (i * (RING3 // HALF) + q // HALF + 1) * INV_STEPS)
                    v.wait_ge(ev("l3_gelu"), j + 1)
                    v.scalar_tensor_tensor(out=ZB[:, r, :], in0=HC3[:, c, :], scalar=SS[:, 3, c:c + 1], in1=G1[:, :],
                                           op0=ALU.mult, op1=ALU.mult).then_inc(ev("l3_scaled"), 1)
                    if ahead:
                        inverse(i, h, 3 * k)
                    v.wait_ge(ev("l3_sums"), j + 1)
                    ts1(OH[:, r, :], iota[:, :], DLC[:, bass.ds(j, 1)], ALU.is_equal).then_inc(ev("l3_onehot"), 1)
                    if ahead:
                        inverse(i, h, 3 * k + 1)
                    v.wait_ge(ev("l3_scaled"), j + 1 + RING3)
                    tt(ZB[:, r, :], ZB[:, r, :], BE1[:, :], ALU.add).then_inc(ev("l3_normed"), 1)
                    if ahead:
                        inverse(i, h, 3 * k + 2)

                def add_step(i, q):
                    if q % RING == 0:
                        tiles[:] = tile_registers(ENG.DVE, i, q, RING3)
                    if exists(i, q + 2):
                        norm(i, q + 2)
                    add_sums("l3", ACC3, q, i * RING3 + q, tiles[q % RING], MS)

                tiles = []
                for n in range(INV_STEPS):
                    inverse(0, 0, n)
                for q in range(2):
                    norm(0, q)
                steps3(v, add_step)
                v.wait_ge(ev("l3_sums_added"), SLOTS + MS)
                v.wait_ge(ev("l3_u"), 1)
                link(tt(T1, NODES, over_tiles(V("bu")), ALU.add))
                link(tt(T2, over_features(ACC3[:, :, HID]), over_tiles(B2U[:, :]), ALU.mult))
                link(tt(T1, T1, T2, ALU.add))
                layer_norm(T1, T1, T2)
                affine(T1, V("gu"), V("beu"))
                made("u_normed")
                v.wait_ge(ev("u_gelu"), 1)
                link(v.scalar_tensor_tensor(out=X[:, :, :], in0=X[:, :, :], scalar=2.0, in1=T1, op0=ALU.mult, op1=ALU.add))
                layer_norm(X[:, :, :], X[:, :, :], T2)
            made("out_made")


def kernel(**inputs):
    import numpy as np
    import concourse.bacc as bacc
    from concourse.bass_utils import run_bass_kernel_spmd

    nc = bacc.Bacc("TRN2", target_bir_lowering=False, num_devices=1)
    arrays = {}

    def feed(name, a):
        a = np.ascontiguousarray(a)
        arrays[name] = a
        return nc.dram_tensor(name, a.shape, mybir.dt.from_np(a.dtype), kind="ExternalInput").ap()

    def tiles_of_edges(a, pad):
        whole = np.full((ET * P,) + a.shape[1:], pad, a.dtype)
        whole[:E] = a
        return whole.reshape((ET, P) + a.shape[1:])

    g = {k: np.asarray(a) for k, a in inputs.items()}
    vec_from = {"att_src": "L0_gnn_att_src", "att_dst": "L0_gnn_att_dst", "bias": "L0_gnn_bias", "bn_g": "L0_gnn_bn_gamma",
                "bn_b": "L0_gnn_bn_beta", "ln_g": "L0_gnn_ln_gamma", "ln_b": "L0_gnn_ln_beta", "res_b": "L0_gnn_res_b",
                "bnres_g": "L0_gnn_bnres_gamma", "bnres_b": "L0_gnn_bnres_beta", "b_l1": "L1_gnn_b", "g_l1": "L1_gnn_gamma",
                "be_l1": "L1_gnn_beta", "bu": "L3_gnn_bu", "gu": "L3_gnn_gu", "beu": "L3_gnn_beu"}
    args = dict(
        x=feed("in_x", g["x"]),
        src_t=feed("in_src", tiles_of_edges(g["src"], PAD_NODE)),
        dst_t=feed("in_dst", tiles_of_edges(g["dst"], PAD_NODE)),
        typ_t=feed("in_type", tiles_of_edges(g["edge_type_50"], 0)),
        attr_t=feed("in_attr", tiles_of_edges(g["edge_attr_32"], 0).transpose(0, 2, 1).reshape(ET, EDIM * P)),
        W0=feed("in_w0", g["L0_gnn_W"]),
        resW=feed("in_res_w", g["L0_gnn_res_W"]),
        vec={k: feed("in_" + k, g[s].reshape(D)) for k, s in vec_from.items()},
        W1T=feed("in_l1_w", g["L1_gnn_W"].T),
        bases=feed("in_bases", g["L2_gnn_bases"]),
        comps=feed("in_comps", g["L2_gnn_comps"]),
        alpha=feed("in_alpha", g["L2_gnn_alpha"]),
        W1x=feed("in_l3_w1x", g["L3_gnn_W1"][:D]),
        W1e=feed("in_l3_w1e", g["L3_gnn_W1"][D:]),
        b1=feed("in_l3_b1", g["L3_gnn_b1"]),
        g1=feed("in_l3_g1", g["L3_gnn_g1"]),
        be1=feed("in_l3_be1", g["L3_gnn_be1"]),
        W2=feed("in_l3_w2", g["L3_gnn_W2"]),
        b2=feed("in_l3_b2", g["L3_gnn_b2"]),
        Wu=feed("in_l3_wu", g["L3_gnn_Wu"]),
    )
    out = nc.dram_tensor("out_0", (N, D), F32, kind="ExternalOutput").ap()
    gnn_stack(nc, out=out, **args)
    r = run_bass_kernel_spmd(nc, [arrays], core_ids=[0])
    return r.results[0]["out_0"]
```

```python
from contextlib import ExitStack

import concourse.bass as bass
from concourse import mybir

F32 = mybir.dt.float32
BF16 = mybir.dt.bfloat16
F16 = mybir.dt.float16
I32 = mybir.dt.int32
ALU = mybir.AluOpType
ACT = mybir.ActivationFunctionType
AX_X = mybir.AxisListType.X
ENG = mybir.EngineType

P = 128
N, E, D = 3125, 103125, 128
HEADS, HC = 4, 32
EDIM, HID = 32, 256
REL, BASES = 50, 4
NT = -(-N // P)
LAST = N - (NT - 1) * P
NPAD = NT * P
PAD_NODE = NPAD - 1
ET = -(-E // P)
SLOTS = ET + NT - 1
SG = -(-SLOTS // P)
SPAD = SG * P
RING = 10
HALF = RING // 2
ITER = SLOTS // RING
assert ITER * RING == SLOTS
RING3 = 3 * RING
ITER3 = SLOTS // RING3 - 1
EDGE_AHEAD, COPY_AHEAD, SQUARES_AHEAD = 23, 22, 16
INV_STEPS, INV_FROM = 12, 5
L1_BANKS = (0, 1, 5, 6, 7)
MS = 5
COLS0 = D + 2 * HEADS + 1
COLS3 = HID + 1
NACC = 5
TRASH = NPAD
ACC_ROWS = NPAD + P
BIG = 1e30
EPS = 1e-5
STAGES = ["slots_made", "base_max", "att_made", "rows_made", "base_scale", "a_zeros", "edge_values",
          "slot_max_made", "carries_made", "max_made", "ex_argument", "loop_argument", "x1_made", "h1_made",
          "l1_ready", "scatter_rows_made", "l2_scaled", "l2_y_parts", "l2_coef_tail", "l2_mixes_done",
          "x3_made", "l3_w1_centered", "p_made", "l3_ready", "u_normed", "out_made"]
STAGE = {name: n + 1 for n, name in enumerate(STAGES)}
VECS = ["att_src", "att_dst", "bias", "bn_g", "bn_b", "ln_g", "ln_b", "res_b", "bnres_g", "bnres_b",
        "b_l1", "g_l1", "be_l1", "bu", "gu", "beu"]


def gnn_stack(nc, x, src_t, dst_t, typ_t, attr_t, W0, resW, vec, W1T, bases, comps, alpha, W1x, W1e, b1, g1, be1,
              W2, b2, Wu, out):
    with ExitStack() as ctx:
        def sb(name, shape, dt=F32):
            return ctx.enter_context(nc.sbuf_tensor(name, shape, dt))

        def sem(name):
            return ctx.enter_context(nc.semaphore(name))

        events = {}

        def ev(name):
            if name not in events:
                events[name] = sem(name)
            return events[name]

        h_dram = nc.dram_tensor("h_dram", (NPAD, D), F32, kind="Internal").ap()
        as_dram = nc.dram_tensor("as_dram", (NPAD, HEADS), F32, kind="Internal").ap()
        p_dram = nc.dram_tensor("p_dram", (NPAD, HID), F32, kind="Internal").ap()
        slot_dram = [nc.dram_tensor(f"slot_dram{k}", (SPAD, 1), I32, kind="Internal").ap() for k in range(2)]
        acc_dram = [nc.dram_tensor(f"acc_dram{k}", (ACC_ROWS, D), F32, kind="Internal").ap() for k in range(NACC)]

        X = sb("X", [P, NT, D])
        H = sb("H", [P, NT, D])
        ACCB = sb("ACCB", [P, NT * COLS3])
        T12 = sb("T12", [P, SPAD * 8])
        T1 = T12[:, 0:NT * D].rearrange("p (t f) -> p t f", f=D)
        T2 = T12[:, NT * D:2 * NT * D].rearrange("p (t f) -> p t f", f=D)
        ACC0 = ACCB[:, 0:NT * COLS0].rearrange("p (t f) -> p t f", f=COLS0)
        ACC1 = ACCB[:, 0:NT * D].rearrange("p (t f) -> p t f", f=D)
        ACC1B = ACCB[:, NT * D:2 * NT * D].rearrange("p (t f) -> p t f", f=D)
        ACC3 = ACCB[:, :].rearrange("p (t f) -> p t f", f=COLS3)
        ARENA = sb("ARENA", [P, SPAD * 21])

        def carve(buf, at, *dims):
            n = 1
            for d in dims:
                n *= d
            names = "abcd"[:len(dims)]
            return buf[:, at:at + n].rearrange("p (" + " ".join(names) + ") -> p " + " ".join(names),
                                               **dict(zip(names[1:], dims[1:])))

        AS = carve(ARENA, 0, SPAD, 4)
        ADAS = carve(ARENA, SPAD * 4, SPAD, 8)
        EXF = carve(ARENA, SPAD * 12, SPAD, 9)
        DR, SR, TR, DL, HI, LO, VALID, FIRST = [carve(ARENA, SPAD * (12 + k), SG, P) for k in range(8)]
        RI = T12[:, 0:3 * SPAD].bitcast(I32).rearrange("p (k g l) -> p k g l", k=3, l=P)
        HII = T12[:, 3 * SPAD:4 * SPAD].bitcast(I32).rearrange("p (g l) -> p g l", l=P)
        HIC, LOC = ACCB[:, 0:SPAD], ACCB[:, SPAD:2 * SPAD]
        OHA = carve(ACCB[:, 2 * SPAD:2 * SPAD + RING * 64].bitcast(BF16), 0, 2, HALF, P)
        LOA = carve(ACCB[:, 2 * SPAD + RING * 64:2 * SPAD + RING * 128].bitcast(BF16), 0, 2, HALF, P)
        HIA = carve(ACCB[:, 2 * SPAD + RING * 128:2 * SPAD + RING * 141].bitcast(BF16), 0, 2, HALF, 26)
        OTA = carve(ACCB, 2 * SPAD + RING * 141, 2, HALF, P)
        VT, AT = carve(T12, 0, SG, HEADS, P), carve(T12, SPAD * 4, SG, HEADS, P)
        FT = carve(ACCB, 0, SG, HEADS, P)
        MT = carve(ACCB, 0, SPAD, HEADS)
        FIRSTC = T12[:, SPAD * 4:SPAD * 5]
        R_FM, R_LM, R_FD, R_LD, R_LINK, R_W = [ARENA[0:HEADS, SPAD * (12 + k):SPAD * (13 + k)] for k in (1, 2, 3, 4, 5, 8)]
        R_CF, R_CB, R_A = [ACCB[0:HEADS, SPAD * (4 + k):SPAD * (5 + k)] for k in range(3)]
        R_OUT = R_LD
        MSG0 = carve(ARENA, 0, MS, COLS0)
        COEF = carve(ARENA, 0, SPAD, BASES)
        YP = [carve(ARENA[:, o:o + NT * 2 * D].bitcast(F16), 0, NT, BASES * D)
              for o in (SPAD * 4, SPAD * 4 + NT * 2 * D)]
        l1r = SPAD * 4
        OHT = carve(ARENA[:, l1r:l1r + RING * 64].bitcast(BF16), 0, 2, HALF, P)
        OTT = carve(ARENA[:, l1r + RING * 64:l1r + RING * 128].bitcast(BF16), 0, 2, HALF, P)
        JUNK = carve(ARENA, l1r + RING * 192, 2, P)
        DUP = carve(ARENA, SPAD * 8, SPAD)
        FIRSTSRC = carve(ARENA, SPAD * 9, SPAD)
        l2r = SPAD * 4 + NT * BASES * D
        OH2 = carve(ACCB[:, 3 * MS * P:3 * MS * P + MS * P // 2].bitcast(F16), 0, MS, P)
        OT2 = carve(ACCB[:, 4 * MS * P:5 * MS * P].bitcast(F16), 0, MS, 2, P)
        EQ = carve(ACCB, 0, MS, P)
        MSG2 = carve(ACCB, MS * P, 2, MS, P)
        SRCH = ARENA[:, l2r + 8 * P:l2r + 8 * P + SPAD // 2].bitcast(F16)
        assert l2r + 8 * P + SPAD // 2 <= SPAD * 20
        PN = carve(ARENA, 0, NT, HID)
        l3r = NT * HID
        HC3 = carve(ARENA, l3r, RING3, HID)
        ZB = carve(ARENA, l3r + RING3 * HID, MS, HID)
        SQ = carve(ARENA, l3r + (RING3 + MS) * HID, 2, HID)
        GE = carve(ARENA, l3r + (RING3 + MS + 2) * HID, MS, COLS3)
        assert l3r + (RING3 + MS + 2) * HID + MS * COLS3 <= SPAD * 20
        DLC = sb("DLC", [P, SPAD])
        SRC = sb("SRC", [P, SPAD])
        SRCI = sb("SRCI", [P, SPAD], I32)
        TYC = sb("TYC", [P, SPAD])
        SCI = ARENA[:, SPAD * 20:SPAD * 21].bitcast(I32)
        ttab = sb("ttab", [1, 2, SPAD], I32)
        iota = sb("iota", [P, P])
        iotab = sb("iotab", [P, P], BF16)
        pcol = sb("pcol", [P, 1])
        trashcol = sb("trashcol", [P, 2])
        ident = sb("ident", [P, P])
        identb = sb("identb", [P, P], BF16)
        identh = sb("identh", [P, P], F16)
        tri = sb("tri", [P, P])
        ones = sb("ones", [P, P])
        VEC = sb("VEC", [P, len(VECS), D])
        B1 = sb("B1", [P, HID])
        G1 = sb("G1", [P, HID])
        BE1 = sb("BE1", [P, HID])
        b2c = sb("b2c", [P, 1])
        B2U = sb("B2U", [P, D])
        W0s = sb("W0s", [P, D])
        resWs = sb("resWs", [P, D])
        W1Ts = sb("W1Ts", [P, D])
        bas = sb("bas", [P, BASES, D])
        coef = sb("coef", [REL, BASES + 1])
        coefb = sb("coefb", [REL, 3, BASES], BF16)
        W1xs = sb("W1xs", [P, HID])
        W1es = sb("W1es", [P, HID])
        W2s = sb("W2s", [P, 2, D])
        W2T = carve(ARENA, SPAD * 20, 2, D)
        W2U = carve(ARENA, SPAD * 20 + 2 * D, 2, D)
        Wus = sb("Wus", [P, 2, D])
        ADN = sb("ADN", [P, NT, 8])
        SMN = sb("SMN", [P, 4, NT, 4])
        DIS = sb("DIS", [P, 2, NT])
        HAS = sb("HAS", [P, NT])
        stat = sb("stat", [P, 4, P])
        jcol = sb("jcol", [P, SG])
        slots = sb("slots", [P, 3, SG])
        sloti = sb("sloti", [P, 2, SG], I32)
        jend = carve(T12, SPAD * 5, 2, ET)
        jendi = carve(ACCB[:, 0:2 * ET].bitcast(I32), 0, 2, ET)
        carry = sb("carry", [P, 3, SG, HEADS])
        wsum = sb("wsum", [P, 4])
        scalei = sb("scalei", [1, 1], I32)
        SS = sb("SS", [P, 4, RING3])
        istage = sb("istage", [P, 2, HALF], I32)
        GR = sb("GR", [P, RING, D])
        A3 = GR[:, :, :]
        OH = sb("OH", [P, MS, P])
        row_stats = carve(OH[:, :, :].rearrange("p a b -> p (a b)"), 0, NT, 6)
        mean_var = carve(OH[:, :, :].rearrange("p a b -> p (a b)"), NT * 6, NT, 2)
        whole_tiles_sum = stat[:, 2, :]

        WIDE = ctx.enter_context(nc.psum_tensor("WIDE", [P, 7 * 512], F32))
        LASTB = ctx.enter_context(nc.psum_tensor("LASTB", [P, 512], F32))

        def bank(b, n=512):
            return LASTB[:, 0:n] if b == 7 else WIDE[:, b * 512:b * 512 + n]

        NODES = WIDE[:, 0:NT * D].rearrange("p (t f) -> p t f", f=D)

        def V(name):
            return VEC[:, VECS.index(name), :]

        def over_tiles(v):
            return v.unsqueeze(1).broadcast_to([P, NT, v.shape[-1]])

        def over_features(v, n=D):
            return v.unsqueeze(2).broadcast_to([P, v.shape[1], n])

        landed = [sem(f"gather_landed{q}") for q in range(RING)]
        attr_landed = [sem(f"attr_landed{q}") for q in range(RING)]
        weights_loaded = sem("weights_loaded")
        stage_done = sem("stage_done")
        dve_step, act_step, pool_step = sem("dve_step"), sem("act_step"), sem("pool_step")
        var_ready, dev_ready = sem("var_ready"), sem("dev_ready")
        bn_in, bn_sums = sem("bn_in"), sem("bn_sums")
        WLOADS = 14 + len(VECS)

        class Chain:

            def __init__(self, eng, s):
                self.eng, self.s, self.n = eng, s, 0

            def __call__(self, ins):
                ins.then_inc(self.s, 1)
                self.n += 1
                self.eng.wait_ge(self.s, self.n)

        ctx.enter_context(nc.allow_non_contiguous_dma(reason="columns of the slot tables, once"))
        block = ctx.enter_context(nc.Block())

        def steps3(engine, body):
            with engine.Fori(0, ITER3) as i:
                for q in range(RING3):
                    body(i, q)
            for q in range(SLOTS - ITER3 * RING3):
                body(ITER3, q)

        def exists(i, q):
            return not isinstance(i, int) or i * RING3 + q < SLOTS

        def fills3(i, q):
            return i * (RING3 // RING) + (q // RING + 1)

        def tile_registers(engine, i, ahead=0, step=RING):
            return nc.values_load_multi_w_load_instructions(
                ttab[0:1, 1, bass.ds(i * step + ahead, RING)], engines=[engine], min_val=0, max_val=NT - 1,
                skip_runtime_bounds_check_because="the slot table is clamped to the node tiles when it is made")[1]

        @block.sync
        def _(sp):
            def store_nodes(table, tile):
                return sp.dma_start(table.rearrange("(t p) f -> p t f", p=P), tile)

            sp.dma_start(jendi[0:1, 0, :], dst_t[:, P - 1:P].rearrange("t a -> a t")).then_inc(ev("ends_loaded"), 16)
            sp.wait_ge(ev("padding_zero"), 1)
            sp.dma_start(X[:, 0:NT - 1, :], x[0:(NT - 1) * P, :].rearrange("(t p) f -> p t f", p=P)).then_inc(ev("x_loaded"), 16)
            sp.dma_start(X[0:LAST, NT - 1, :], x[(NT - 1) * P:N, :]).then_inc(ev("x_loaded"), 16)
            w = [(W0s[:, :], W0), (resWs[:, :], resW), (W1Ts[:, :], W1T),
                 (bas[:, :, :], bases.rearrange("b d f -> d b f")),
                 (coef[:, 0:BASES], comps), (coef[:, BASES:BASES + 1], alpha),
                 (W1xs[:, :], W1x), (W1es[0:EDIM, :], W1e),
                 (W2s[:, :, :], W2.rearrange("(k p) f -> p k f", p=P)),
                 (Wus[:, :, :], Wu.rearrange("(k p) f -> p k f", p=P)),
                 (B1[:, :], b1.partition_broadcast(P)), (G1[:, :], g1.partition_broadcast(P)),
                 (BE1[:, :], be1.partition_broadcast(P)), (b2c[:, :], b2.unsqueeze(1))]
            w += [(VEC[:, k, :], vec[name].partition_broadcast(P)) for k, name in enumerate(VECS)]
            assert len(w) == WLOADS
            for dst, s in w:
                sp.dma_start(dst, s).then_inc(weights_loaded, 16)
            sp.wait_ge(stage_done, STAGE["slots_made"])
            for k in range(2):
                sp.dma_start(slot_dram[k].rearrange("(g p) a -> p (g a)", p=P), sloti[:, k, :]).then_inc(ev("slots_stored"), 16)
            sp.wait_ge(ev("slots_stored"), 32)
            for k in range(2):
                sp.dma_start(ttab[0:1, k, :], slot_dram[k].rearrange("s a -> a s")).then_inc(ev("slots_loaded"), 16)
            sp.wait_ge(stage_done, STAGE["att_made"])
            store_nodes(as_dram, ADN[:, :, 4:8]).then_inc(ev("as_stored"), 16)
            store_nodes(h_dram, H[:, :, :]).then_inc(ev("h0_stored"), 16)
            sp.wait_ge(stage_done, STAGE["h1_made"])
            store_nodes(h_dram, H[:, :, :]).then_inc(ev("h1_stored"), 16)
            sp.wait_ge(ev("zeros_made"), 1)
            for k in range(NACC):
                sp.dma_start(acc_dram[k].rearrange("(t p) f -> p t f", p=P),
                             carve(T12, 0, NT + 1, D)).then_inc(ev("acc_zero_stored"), 16)
            sp.wait_ge(ev("scatters_done"), 1)
            sp.wait_ge(stage_done, STAGE["l2_mixes_done"])
            sp.wait_ge(ev("l2_gathered"), SLOTS + 3 + MS)
            for k, dst in enumerate([T1, T2, ACC1, ACC1B, H[:, :, :]]):
                sp.dma_start(dst, acc_dram[k][0:NPAD, :].rearrange("(t p) f -> p t f", p=P)).then_inc(ev("acc_loaded"), 16)
            sp.wait_ge(stage_done, STAGE["p_made"])
            store_nodes(p_dram, PN).then_inc(ev("p_stored"), 16)
            sp.wait_ge(stage_done, STAGE["l3_ready"])
            with sp.Fori(0, ITER) as i:
                tiles = nc.values_load_multi_w_load_instructions(
                    ttab[0:1, 0, bass.ds(i * RING, RING)], engines=[ENG.SP], min_val=0, max_val=ET - 1,
                    skip_runtime_bounds_check_because="the slot table is clamped to the edge tiles when it is made")[1]
                for q in range(RING):
                    sp.wait_ge(ev("l3_edge_part"), i * RING + q + 1)
                    sp.dma_start(A3[0:EDIM, q, :], attr_t[bass.ds(tiles[q], 1), :].rearrange("a (f e) -> (a f) e", f=EDIM)
                                 ).then_inc(attr_landed[q], 16)
            sp.wait_ge(stage_done, STAGE["out_made"])
            sp.dma_start(out[0:(NT - 1) * P, :].rearrange("(t p) f -> p t f", p=P), X[:, 0:NT - 1, :]).then_inc(ev("out_stored"), 16)
            sp.dma_start(out[(NT - 1) * P:N, :], X[0:LAST, NT - 1, :]).then_inc(ev("out_stored"), 16)
            sp.wait_ge(ev("out_stored"), 32)

        @block.gpsimd
        def _(pool):
            pool.iota(iota[:, :], pattern=[[1, P]], base=0, channel_multiplier=0,
                      allow_small_or_imprecise_dtypes=True).then_inc(ev("iotas"), 1)
            pool.iota(pcol[:, :], pattern=[[0, 1]], base=0, channel_multiplier=1,
                      allow_small_or_imprecise_dtypes=True).then_inc(ev("iotas"), 1)
            pool.iota(jcol[:, :], pattern=[[P, SG]], base=0, channel_multiplier=1,
                      allow_small_or_imprecise_dtypes=True).then_inc(ev("iotas"), 1)
            pool.iota(jend[0:1, 1, :], pattern=[[1, ET]], base=0, channel_multiplier=0,
                      allow_small_or_imprecise_dtypes=True).then_inc(ev("iotas"), 1)
            pool.wait_ge(stage_done, STAGE["slots_made"])
            for k, table in enumerate((dst_t, src_t, typ_t)):
                for g in range(SG):
                    pool.indirect_dma_start(RI[:, k, g, :], None, table[:, :],
                                            bass.IndirectOffsetOnAxis(ap=sloti[:, 0, g:g + 1], axis=0)
                                            ).then_inc(ev("rows_gathered"), 16)

            def carry_waits():
                pool.sem_inc(ev("pool_waits_met"), 1)

            def gather_loop(name, table, ring, free):
                staged = sem(name + "_indices_staged")
                with pool.Fori(0, ITER) as i:
                    for h in range(2):
                        pool.wait_ge(free, i * RING + (h + 1) * HALF)
                        pool.tensor_copy(istage[:, h, :], SRCI[:, bass.ds(i * RING + h * HALF, HALF)]).then_inc(staged, 1)
                        pool.wait_ge(staged, i * 2 + h + 1)
                        carry_waits()
                        for k in range(HALF):
                            q = h * HALF + k
                            pool.indirect_dma_start(ring[:, q, :], None, table[:, :],
                                                    bass.IndirectOffsetOnAxis(ap=istage[:, h, k:k + 1], axis=0)
                                                    ).then_inc(landed[q], 16)

            pool.wait_ge(ev("column_copied"), 5)
            pool.wait_ge(ev("as_stored"), 16)
            gather_loop("a", as_dram, GR[:, :, 0:HEADS], ev("a_ring_free"))
            def clear_sums():
                pool.memset(ACCB[:, :], 0.0).then_inc(ev("sums_cleared"), 1)

            pool.wait_ge(stage_done, STAGE["ex_argument"])
            clear_sums()
            pool.wait_ge(ev("h0_stored"), 16)
            gather_loop("l0", h_dram, GR[:, :, :], ev("l0_messages"))
            pool.wait_ge(ev("l0_res"), 1)
            clear_sums()
            pool.wait_ge(ev("l1_h"), 1)
            pool.memset(T12[:, 0:(NT + 1) * D], 0.0).then_inc(ev("zeros_made"), 1)
            pool.wait_ge(ev("h1_stored"), 16)
            gather_loop("l1", h_dram, GR[:, :, :], ev("l1_sums"))
            base = 3 * ITER * 16
            staged = sem("l2_indices_staged")
            pool.wait_ge(ev("acc_zero_stored"), 16 * NACC)
            pool.wait_ge(stage_done, STAGE["scatter_rows_made"])
            with pool.Fori(0, ITER) as i:
                for h in range(2):
                    for q in range(h * HALF, (h + 1) * HALF):
                        pool.wait_ge(landed[q], i * 16 + base)
                    pool.tensor_copy(istage[:, h, :], SCI[:, bass.ds(i * RING + h * HALF, HALF)]).then_inc(staged, 1)
                    pool.wait_ge(staged, i * 2 + h + 1)
                    for k in range(HALF):
                        q = h * HALF + k
                        pool.wait_ge(ev("l2_sum_copied"), i * RING + q + 3)
                        pool.wait_ge(landed[(q + NACC) % RING], i * 16 + base + (16 if q >= NACC else 0))
                        carry_waits()
                        pool.indirect_dma_start(acc_dram[q % NACC][:, :],
                                                bass.IndirectOffsetOnAxis(ap=istage[:, h, k:k + 1], axis=0),
                                                GR[:, q, :], None, compute_op=ALU.add).then_inc(landed[q], 16)
            for q in range(RING):
                pool.wait_ge(landed[q], base + ITER * 16)
            pool.sem_inc(ev("scatters_done"), 1)
            pool.wait_ge(stage_done, STAGE["x3_made"])
            clear_sums()
            pool.memset(GE, 1.0).then_inc(ev("l3_rings_set"), 1)
            pool.memset(A3, 0.0).then_inc(ev("l3_rings_set"), 1)
            pool.wait_ge(ev("p_stored"), 16)
            base = 4 * ITER * 16
            staged = sem("l3_indices_staged")

            def gather_step(i, q):
                c = q % RING
                h, k = divmod(c, HALF)
                if k == 0:
                    for b in range(c, c + HALF):
                        pool.wait_ge(landed[b], (fills3(i, q) - 1) * 16 + base)
                    pool.tensor_copy(istage[:, h, :], SRCI[:, bass.ds(i * RING3 + q, HALF)]).then_inc(staged, 1)
                    pool.wait_ge(staged, fills3(i, q) * 2 - 1 + h)
                pool.wait_ge(ev("l3_edge_copied"), i * RING3 + q + 3)
                carry_waits()
                pool.indirect_dma_start(HC3[:, q % RING3, :], None, p_dram[:, :],
                                        bass.IndirectOffsetOnAxis(ap=istage[:, h, k:k + 1], axis=0),
                                        compute_op=ALU.add).then_inc(landed[c], 16)

            steps3(pool, gather_step)

        @block.tensor
        def _(pe):
            def transpose_nodes(tile):
                for t in range(NT):
                    last = pe.transpose(NODES[:, t, :], tile[:, t, :], ident[:, :])
                return last

            def project(tile_t, w):
                for t in range(NT):
                    last = pe.matmul(NODES[:, t, :], tile_t[:, t, :], w, start=True, stop=True)
                return last

            def node_sums(tile, n):
                pe.wait_ge(bn_in, n)
                pe.matmul(bank(7, D), ones[:, :], whole_tiles_sum, start=True, stop=False)
                last = pe.matmul(bank(7, D), ones[0:LAST, :], tile[0:LAST, NT - 1, :], start=False, stop=True)
                last.then_inc(bn_sums, 1)

            pe.wait_ge(ev("ends_made"), 1)
            for a in range(0, ET, 512):
                n = min(512, ET - a)
                last = pe.matmul(WIDE[:, a:a + n], ones[0:1, :], jend[0:1, 0, a:a + n], start=True, stop=True)
            last.then_inc(ev("ends_spread"), 1)
            pe.wait_ge(ev("x_loaded"), 32)
            pe.wait_ge(stage_done, STAGE["slots_made"])
            transpose_nodes(X).then_inc(ev("l0_xt"), 1)
            pe.wait_ge(ev("l0_xt_copied"), 1)
            pe.wait_ge(weights_loaded, 16 * WLOADS)
            project(ACC1B, W0s[:, :]).then_inc(ev("l0_h"), 1)
            pe.wait_ge(stage_done, STAGE["base_max"])
            pe.transpose(bank(7, P)[0:1, :], wsum[:, 0:1], ident[:, :]).then_inc(ev("base_max_turned"), 1)
            for n, (arr, b) in enumerate([(DL, 2), (SR, 4), (TR, 0), (HI, 2), (LO, 4)]):
                pe.wait_ge(stage_done, STAGE["rows_made"])
                if n >= 3:
                    pe.wait_ge(ev("column_copied"), n - 2)
                for g in range(SG):
                    last = pe.transpose(WIDE[:, b * 512 + g * P:b * 512 + (g + 1) * P], arr[:, g, :], ident[:, :])
                last.then_inc(ev("column_turned"), 1)
            pe.wait_ge(stage_done, STAGE["base_scale"])
            pe.matmul(bank(7, 2), ones[0:1, :], wsum[0:1, 2:4], start=True, stop=True).then_inc(ev("base_scale_spread"), 1)
            pe.wait_ge(stage_done, STAGE["a_zeros"])
            pe.wait_ge(stage_done, STAGE["att_made"])
            pe.matmul(bank(7, NT), ones[:, :], OTA[:, 0, 0, 0:NT], start=True, stop=False, skip_group_check=True
                      ).then_inc(ev("deg_cleared"), 1)
            pe.wait_ge(ev("deg_cleared"), 1)
            pe.sem_inc(ev("deg_ready"), 1)
            pe.wait_ge(ev("slots_loaded"), 32)
            pe.sem_inc(ev("a_turned"), 2)
            pe.sem_inc(ev("a_onehot_read"), 2)
            pe.sem_inc(ev("a_adas"), 2)
            with pe.Fori(0, ITER) as i:
                ts = tile_registers(ENG.PE, i)
                for h in range(2):
                    n = i * 2 + h + 1
                    pe.wait_ge(ev("a_onehot"), n)
                    pe.wait_ge(ev("a_turned_copied"), n)
                    for k in range(HALF):
                        last = pe.transpose(bank(h).bitcast(BF16)[:, k * P:(k + 1) * P], OHA[:, h, k, :], identb[:, :])
                    last.then_inc(ev("a_turned"), 1)
                    for k in range(HALF):
                        last = pe.matmul(bank(7, NT), LOA[:, h, k, :], HIA[:, h, k, 0:NT], start=False, stop=False,
                                         skip_group_check=True)
                    last.then_inc(ev("a_onehot_read"), 1)
                    pe.wait_ge(ev("a_turned_copied"), n + 2)
                    pe.wait_ge(ev("a_adas_copied"), n)
                    for k in range(HALF):
                        last = pe.matmul(bank(2 + h)[:, k * 8:(k + 1) * 8], OTA[:, h, k, :],
                                         ADN[:, bass.ds(ts[h * HALF + k], 1), :].rearrange("p a b -> p (a b)"),
                                         start=True, stop=True)
                    last.then_inc(ev("a_adas"), 1)
            pe.wait_ge(stage_done, STAGE["edge_values"])
            for hd in range(HEADS):
                if hd >= 2:
                    pe.wait_ge(ev("as_row_copied"), hd - 1)
                for g in range(SG):
                    last = pe.transpose(WIDE[:, (hd % 2) * 1024 + g * P:(hd % 2) * 1024 + (g + 1) * P],
                                        AS[:, g * P:(g + 1) * P, hd], ident[:, :])
                last.then_inc(ev("as_row"), 1)
            pe.wait_ge(stage_done, STAGE["slot_max_made"])
            for n in range(4):
                if n >= 2:
                    pe.wait_ge(ev("end_row_copied"), n - 1)
                for g in range(SG):
                    lane = 0 if n % 2 == 0 else P - 1
                    in_ = VT[:, g, :, lane] if n < 2 else DR[:, g, lane:lane + 1].broadcast_to([P, HEADS])
                    last = pe.transpose(WIDE[0:HEADS, (n % 2) * 1024 + g * P:(n % 2) * 1024 + (g + 1) * P], in_, ident[:, :])
                last.then_inc(ev("end_row"), 1)
            pe.wait_ge(stage_done, STAGE["carries_made"])
            for n, row in enumerate((R_CF, R_CB, R_LINK)):
                for g in range(SG):
                    last = pe.transpose(WIDE[:, 3072 + (n * SG + g) * HEADS:3072 + (n * SG + g + 1) * HEADS],
                                        row[:, g * P:(g + 1) * P], ident[0:HEADS, 0:HEADS])
            last.then_inc(ev("carries_turned"), 1)
            pe.wait_ge(stage_done, STAGE["max_made"])
            for n in range(HEADS + 1):
                if n >= 2:
                    pe.wait_ge(ev("max_copied"), n - 1)
                for g in range(SG):
                    in_ = VT[:, g, n, :] if n < HEADS else FIRST[:, g, :]
                    last = pe.transpose(WIDE[:, (n % 2) * 1024 + g * P:(n % 2) * 1024 + (g + 1) * P], in_, ident[:, :])
                last.then_inc(ev("max_turned"), 1)

            pe.wait_ge(ev("max_copied"), HEADS + 1)
            pe.sem_inc(ev("l0_sums"), RING)
            with pe.Fori(0, ITER) as i:
                for q in range(RING):
                    j = i * RING + q
                    pe.wait_ge(ev("l0_sums_added"), j + 1)
                    pe.wait_ge(ev("l0_messages"), j + 1 + RING)
                    pe.matmul(bank(q % MS, COLS0), OH[:, q % MS, :], MSG0[:, q % MS, :], start=True, stop=True
                              ).then_inc(ev("l0_sums"), 1)
            node_sums(T1, 1)
            transpose_nodes(X).then_inc(ev("l0_xt2"), 1)
            node_sums(T1, 2)
            pe.wait_ge(ev("l0_xt2_copied"), 1)
            project(ACC1, resWs[:, :]).then_inc(ev("l0_res"), 1)
            node_sums(H, 3)
            node_sums(H, 4)
            pe.wait_ge(stage_done, STAGE["x1_made"])
            transpose_nodes(X).then_inc(ev("l1_xt"), 1)
            pe.wait_ge(ev("l1_xt_copied"), 1)
            project(T1, W1Ts[:, :]).then_inc(ev("l1_h"), 1)
            pe.wait_ge(stage_done, STAGE["l1_ready"])
            pe.sem_inc(ev("l1_sums"), RING)
            pe.sem_inc(ev("l1_types_turned"), 2)
            pe.sem_inc(ev("l1_coefs"), 2)

            def sources(j, r):
                pe.wait_ge(ev("l1_repeats"), j + 1)
                pe.matmul(bank(2 + r, P), SRCH[:, bass.ds(j, 1)].broadcast_to([P, P]), identh[:, :], start=True, stop=True
                          ).then_inc(ev("l1_sources"), 1)

            sources(0, 0)
            with pe.Fori(0, ITER) as i:
                for h in range(2):
                    n = i * 2 + h + 1
                    for k in range(HALF):
                        q = h * HALF + k
                        j = i * RING + q
                        sources(j + 1, (q + 1) % 2)
                        pe.wait_ge(ev("l1_sums_added"), j + 1)
                        pe.wait_ge(ev("l1_onehot"), j + 1)
                        pe.wait_ge(landed[q], i * 16 + (2 * ITER * 16 + 16))
                        pe.matmul(bank(L1_BANKS[q % MS], D), OH[:, q % MS, :], GR[:, q, :], start=True, stop=True
                                  ).then_inc(ev("l1_sums"), 1)
                        if k == 0:
                            pe.wait_ge(ev("l1_type_onehot"), n)
                            pe.wait_ge(ev("l1_coefs_copied"), n)
                            for kk in range(HALF):
                                last = pe.transpose(bank(4).bitcast(BF16)[:, kk * P:(kk + 1) * P], OHT[:, h, kk, :], identb[:, :])
                            last.then_inc(ev("l1_types_turned"), 1)
                        if k == 2:
                            pe.wait_ge(ev("l1_types_copied"), n)
                        for kk in ((), (), (0, 1), (2, 3), (4,))[k]:
                            c = 3 * P + kk * BASES
                            for part in range(3):
                                last = pe.matmul(bank(4)[:, c:c + BASES], OTT[0:REL, h, kk, :], coefb[:, part, :],
                                                 start=(part == 0), stop=(part == 2))
                    last.then_inc(ev("l1_coefs"), 1)
            pe.wait_ge(stage_done, STAGE["l2_scaled"])
            transpose_nodes(T1).then_inc(ev("l2_xt"), 1)
            pe.wait_ge(ev("l2_xt_copied"), 1)
            for t in range(NT):
                if t >= 4:
                    pe.wait_ge(ev("l2_y_copied"), t - 3)
                pe.matmul(bank(t % 4), T2[:, t, :], bas[:, :, :].rearrange("p b f -> p (b f)"), start=True, stop=True
                          ).then_inc(ev("l2_y"), 1)
            pe.wait_ge(stage_done, STAGE["l2_y_parts"])
            pe.sem_inc(ev("l2_turned"), MS)
            pe.sem_inc(ev("l2_gathered"), MS)
            pe.sem_inc(ev("l2_summed"), MS)

            def turn(j, q):
                pe.wait_ge(ev("l2_onehot"), j + 1)
                pe.wait_ge(ev("l2_turned_copied"), j + 1)
                turned = bank(7, P).bitcast(F16)
                pe.transpose(turned[:, 0:P], OH2[:, q % MS, :], identh[:, :])
                pe.transpose(turned[:, P:2 * P], SRCH[:, bass.ds(j, 1)].broadcast_to([P, P]), identh[:, :]
                             ).then_inc(ev("l2_turned"), 1)

            def gather(j, q, t):
                pe.wait_ge(ev("l2_turned_copied"), j + 2)
                pe.wait_ge(ev("l2_mixed"), j + 1)
                for k, part in enumerate(YP):
                    last = pe.matmul(bank(q % MS), OT2[:, q % MS, 0, :], part[:, bass.ds(t, 1), :].rearrange("p a b -> p (a b)"),
                                     start=(k == 0), stop=(k == 1))
                last.then_inc(ev("l2_gathered"), 1)

            ts = tile_registers(ENG.PE, 0)
            turn(0, 0)
            for j in range(3):
                turn(j + 1, j + 1)
                gather(j, j, ts[j])
            with pe.Fori(0, ITER) as i:
                ts = tile_registers(ENG.PE, i, 3)
                for q in range(RING):
                    j = i * RING + q
                    pe.wait_ge(ev("l2_mixed"), j + 1 + MS)
                    pe.wait_ge(ev("l2_equal"), j + 1 + MS)
                    pe.wait_ge(ev("l2_sum_copied"), j + 1)
                    for k in range(2):
                        last = pe.matmul(bank(5 + q % 2, D), EQ[:, q % MS, :], MSG2[:, k, q % MS, :], start=(k == 0), stop=(k == 1))
                    last.then_inc(ev("l2_summed"), 1)
                    turn(j + 4, q + 4)
                    gather(j + 3, q + 3, ts[q])
            pe.wait_ge(stage_done, STAGE["x3_made"])
            transpose_nodes(X).then_inc(ev("l3_xt"), 1)
            pe.wait_ge(ev("l3_xt_copied"), 1)
            pe.wait_ge(stage_done, STAGE["l3_w1_centered"])
            for t in range(NT):
                if t >= 4:
                    pe.wait_ge(ev("l3_p_copied"), t - 3)
                pe.matmul(bank(t % 4, HID), T1[:, t, :], W1xs[:, :], start=True, stop=True).then_inc(ev("l3_p"), 1)
            pe.wait_ge(ev("l3_p_copied"), NT)
            for k in range(2):
                last = pe.transpose(WIDE[:, k * P:(k + 1) * P], W2s[:, k, :], ident[:, :])
            last.then_inc(ev("w2_turned"), 1)
            pe.wait_ge(ev("w2t_copied"), 1)
            for k in range(2):
                pe.matmul(WIDE[:, k * P:(k + 1) * P], W2T[:, k, :], Wus[:, 1, :], start=True, stop=True)
            pe.matmul(WIDE[:, 2 * P:3 * P], b2c[:, :].broadcast_to([P, P]), Wus[:, 1, :], start=True, stop=True
                      ).then_inc(ev("w2u"), 1)
            pe.wait_ge(ev("w2u_copied"), 1)
            project(T1, Wus[:, 0, :]).then_inc(ev("l3_xu"), 1)
            pe.sem_inc(ev("l3_sums"), MS)
            pe.sem_inc(ev("l3_edge_part"), RING)

            def edge_part(i, q):
                pe.wait_ge(attr_landed[q % RING], fills3(i, q) * 16)
                pe.wait_ge(ev("l3_edge_copied"), i * RING3 + q + 1)
                pe.matmul(bank(5 + q % 2, HID), A3[:, q % RING, :], W1es[:, :], start=True, stop=True
                          ).then_inc(ev("l3_edge_part"), 1)

            def sum_step(i, q):
                if exists(i, q + EDGE_AHEAD):
                    edge_part(i, q + EDGE_AHEAD)
                j = i * RING3 + q
                pe.wait_ge(ev("l3_sums_added"), j + 1)
                pe.wait_ge(ev("l3_gelu"), j + 1 + MS)
                pe.wait_ge(ev("l3_onehot"), j + 1)
                pe.matmul(bank(q % MS, COLS3), OH[:, q % MS, :], GE[:, q % MS, :], start=True, stop=True
                          ).then_inc(ev("l3_sums"), 1)

            pe.wait_ge(stage_done, STAGE["l3_ready"])
            for q in range(EDGE_AHEAD):
                edge_part(0, q)
            steps3(pe, sum_step)
            pe.wait_ge(ev("l3_sums_added"), SLOTS + MS)
            for n, src in enumerate((ACC3[:, :, 0:D], ACC3[:, :, D:2 * D])):
                transpose_nodes(src).then_inc(ev("l3_turned"), 1)
                pe.wait_ge(ev("l3_turned_copied"), n + 1)
            for t in range(NT):
                pe.matmul(NODES[:, t, :], T1[:, t, :], W2U[:, 0, :], start=True, stop=False)
                last = pe.matmul(NODES[:, t, :], T2[:, t, :], W2U[:, 1, :], start=False, stop=True)
            last.then_inc(ev("l3_u"), 1)

        @block.scalar
        def _(act):
            link = Chain(act, act_step)
            devs = [0]

            def copy(dst, src):
                return act.activation(dst, src, ACT.Copy)

            def deviation(n):
                devs[0] += 1
                act.wait_ge(var_ready, devs[0])
                act.activation(stat[:, 2, 0:n], stat[:, 1, 0:n], ACT.Sqrt).then_inc(dev_ready, 1)

            act.wait_ge(ev("l0_xt"), 1)
            copy(ACC1B, NODES).then_inc(ev("l0_xt_copied"), 1)
            for n, (dst, b) in enumerate([(DLC[:, :], 2), (SRC[:, :], 4), (TYC[:, :], 0), (HIC, 2), (LOC, 4)]):
                act.wait_ge(ev("column_turned"), n + 1)
                if n == 1:
                    link(copy(SRCI[:, :], WIDE[:, b * 512:b * 512 + SPAD]))
                copy(dst, WIDE[:, b * 512:b * 512 + SPAD]).then_inc(ev("column_copied"), 1)
            act.wait_ge(ev("deg_ready"), 1)
            act.sem_inc(ev("a_turned_copied"), 2)
            act.sem_inc(ev("a_adas_copied"), 2)
            with act.Fori(0, ITER) as i:
                for h in range(2):
                    act.wait_ge(ev("a_turned"), i * 2 + h + 3)
                    act.wait_ge(ev("a_adas"), i * 2 + h + 1)
                    copy(OTA[:, h, :, :].rearrange("p k e -> p (k e)"), bank(h).bitcast(BF16)[:, 0:HALF * P]
                         ).then_inc(ev("a_turned_copied"), 1)
                    act.wait_ge(ev("a_adas"), i * 2 + h + 3)
                    copy(ADAS[:, bass.ds(i * RING + h * HALF, HALF), :],
                         bank(2 + h)[:, 0:HALF * 8].rearrange("p (k c) -> p k c", c=8)).then_inc(ev("a_adas_copied"), 1)
            act.wait_ge(stage_done, STAGE["ex_argument"])
            act.activation(EXF[:, :, 0:HEADS], ADAS[:, :, 0:HEADS], ACT.Exp).then_inc(ev("ex"), 1)
            act.wait_ge(stage_done, STAGE["loop_argument"])
            act.activation(SMN[:, 1, :, :], SMN[:, 0, :, :], ACT.Exp).then_inc(ev("loop_ex"), 1)
            act.wait_ge(ev("l0_xt2"), 1)
            copy(ACC1, NODES).then_inc(ev("l0_xt2_copied"), 1)
            deviation(D)
            deviation(NT)
            deviation(D)
            deviation(NT)
            deviation(2 * NT)
            act.wait_ge(ev("l1_xt"), 1)
            copy(T1, NODES).then_inc(ev("l1_xt_copied"), 1)
            act.sem_inc(ev("l1_coefs_copied"), 1)
            with act.Fori(0, ITER) as i:
                for h in range(2):
                    n = i * 2 + h + 1
                    act.wait_ge(ev("l1_types_turned"), n + 2)
                    act.wait_ge(ev("l1_coefs"), n)
                    copy(OTT[:, h, :, :].rearrange("p k e -> p (k e)"), bank(4).bitcast(BF16)[:, 0:HALF * P]
                         ).then_inc(ev("l1_types_copied"), 1)
                    act.wait_ge(ev("l1_coefs"), n + 2)
                    copy(COEF[:, bass.ds(i * RING + h * HALF, HALF), :],
                         bank(4)[:, 3 * P:3 * P + HALF * BASES].rearrange("p (k b) -> p k b", b=BASES)
                         ).then_inc(ev("l1_coefs_copied"), 1)
            deviation(NT)
            deviation(NT)
            act.wait_ge(ev("l2_xt"), 1)
            copy(T2, NODES).then_inc(ev("l2_xt_copied"), 1)
            for t in range(NT):
                act.wait_ge(ev("l2_y"), t + 1)
                copy(YP[0][:, t, :], bank(t % 4)).then_inc(ev("l2_y_high"), 1)
            act.sem_inc(ev("l2_turned_copied"), 1)
            act.sem_inc(ev("l2_sum_copied"), 2)

            def copy_turned(j, q):
                act.wait_ge(ev("l2_turned"), j + 1 + MS)
                act.wait_ge(ev("l2_gathered"), j + 1)
                act.wait_ge(ev("l2_equal"), j + 1)
                copy(OT2[:, q % MS, :, :].rearrange("p a b -> p (a b)"), bank(7, P).bitcast(F16)).then_inc(ev("l2_turned_copied"), 1)

            def mix_first(j, q):
                act.wait_ge(ev("l2_gathered"), j + 1 + MS)
                act.wait_ge(ev("l2_summed"), j + 1)
                for b in (1, 0):
                    last = act.activation(MSG2[:, b, q % MS, :], bank(q % MS)[:, b * D:(b + 1) * D], ACT.Copy,
                                          scale=COEF[:, bass.ds(j, 1), b:b + 1].rearrange("p a b -> p (a b)"))
                last.then_inc(ev("l2_mixed_first"), 1)

            copy_turned(0, 0)
            copy_turned(1, 1)
            act.wait_ge(stage_done, STAGE["l2_coef_tail"])
            mix_first(0, 0)
            copy_turned(2, 2)
            mix_first(1, 1)
            copy_turned(3, 3)
            with act.Fori(0, ITER) as i:
                for q in range(RING):
                    j = i * RING + q
                    mix_first(j + 2, q + 2)
                    act.wait_ge(ev("l2_summed"), j + 1 + MS)
                    act.wait_ge(landed[q], i * 16 + 3 * ITER * 16)
                    copy(GR[:, q, :], bank(5 + q % 2, D)).then_inc(ev("l2_sum_copied"), 1)
                    copy_turned(j + 4, q + 4)
            deviation(NT)
            act.wait_ge(ev("l3_xt"), 1)
            copy(T1, NODES).then_inc(ev("l3_xt_copied"), 1)
            act.wait_ge(ev("w2_turned"), 1)
            copy(W2T.rearrange("p k f -> p (k f)"), WIDE[:, 0:2 * P]).then_inc(ev("w2t_copied"), 1)
            act.wait_ge(ev("w2u"), 1)
            link(copy(W2U.rearrange("p k f -> p (k f)"), WIDE[:, 0:2 * P]))
            copy(B2U[:, :], WIDE[:, 2 * P:3 * P]).then_inc(ev("w2u_copied"), 1)
            act.sem_inc(ev("l3_edge_copied"), 2)
            act.sem_inc(ev("l3_squares"), 2)
            act.sem_inc(ev("l3_gelu"), MS)

            def copy_edge_part(i, q):
                j = i * RING3 + q
                act.wait_ge(ev("l3_edge_part"), j + 1 + RING)
                act.wait_ge(ev("l3_scaled"), j + 1)
                copy(HC3[:, q % RING3, :], bank(5 + q % 2, HID)).then_inc(ev("l3_edge_copied"), 1)

            def squares(i, q):
                c = q % RING3
                act.wait_ge(landed[q % RING], fills3(i, q) * 16 + 4 * ITER * 16)
                act.wait_ge(ev("l3_squares"), i * RING3 + q + 1)
                act.activation(SQ[:, q % 2, :], HC3[:, c, :], ACT.Square, accum_out=SS[:, 0, c:c + 1]
                               ).then_inc(ev("l3_squares"), 1)

            def gelu_step(i, q):
                if exists(i, q + COPY_AHEAD):
                    copy_edge_part(i, q + COPY_AHEAD)
                if exists(i, q + SQUARES_AHEAD):
                    squares(i, q + SQUARES_AHEAD)
                j = i * RING3 + q
                act.wait_ge(ev("l3_normed"), j + 1)
                act.wait_ge(ev("l3_sums"), j + 1)
                act.activation(GE[:, q % MS, 0:HID], ZB[:, q % MS, :], ACT.Gelu).then_inc(ev("l3_gelu"), 1)

            act.wait_ge(stage_done, STAGE["l3_ready"])
            for q in range(COPY_AHEAD):
                copy_edge_part(0, q)
            for q in range(SQUARES_AHEAD):
                squares(0, q)
            steps3(act, gelu_step)
            for n, dst in enumerate((T1, T2)):
                act.wait_ge(ev("l3_turned"), n + 1)
                copy(dst, NODES).then_inc(ev("l3_turned_copied"), 1)
            deviation(NT)
            act.wait_ge(stage_done, STAGE["u_normed"])
            act.activation(T1, T1, ACT.Gelu).then_inc(ev("u_gelu"), 1)
            deviation(NT)

        @block.vector
        def _(v):
            link = Chain(v, dve_step)
            devs, bns, stages = [0], [0], []

            def made(name):
                assert name == STAGES[len(stages)]
                stages.append(name)
                v.sem_inc(stage_done, 1)

            def tt(out, a, b, op):
                return v.tensor_tensor(out, a, b, op)

            def ts1(out, a, s, op, s2=None, op2=None):
                if op2 is None:
                    return v.tensor_scalar(out, a, s, None, op)
                return v.tensor_scalar(out, a, s, s2, op, op2)

            def inverse_deviation(n):
                devs[0] += 1
                v.wait_ge(dev_ready, devs[0])
                link(v.reciprocal(stat[:, 3, 0:n], stat[:, 2, 0:n]))

            def layer_norm(dst, src):
                for t in range(NT):
                    last = v.bn_stats(out=row_stats[:, t, :], in_=src[:, t, :])
                link(last)
                for t in range(NT):
                    last = v.bn_aggr(out=mean_var[:, t, :], in_=row_stats[:, t, :])
                link(last)
                link(ts1(stat[:, 1, 0:NT], mean_var[:, :, 1], EPS, ALU.add))
                v.sem_inc(var_ready, 1)
                inverse_deviation(NT)
                for t in range(NT):
                    last = ts1(dst[:, t, :], src[:, t, :], mean_var[:, t, 0:1], ALU.subtract, stat[:, 3, t:t + 1], ALU.mult)
                link(last)

            def affine(tile, gain, shift):
                link(tt(tile, tile, over_tiles(gain), ALU.mult))
                link(tt(tile, tile, over_tiles(shift), ALU.add))

            def batch_norm(tile, squares, gain, shift):
                link(v.tensor_reduce(whole_tiles_sum, tile[:, 0:NT - 1, :].rearrange("p t f -> p f t"), AX_X, ALU.add))
                v.sem_inc(bn_in, 1)
                v.wait_ge(bn_sums, bns[0] + 1)
                link(ts1(stat[:, 0, :], bank(7, D), 1.0 / N, ALU.mult))
                link(tt(squares, tile, over_tiles(stat[:, 0, :]), ALU.subtract))
                link(tt(tile, squares, squares, ALU.mult))
                link(v.tensor_reduce(whole_tiles_sum, tile[:, 0:NT - 1, :].rearrange("p t f -> p f t"), AX_X, ALU.add))
                v.sem_inc(bn_in, 1)
                v.wait_ge(bn_sums, bns[0] + 2)
                bns[0] += 2
                link(ts1(stat[:, 1, :], bank(7, D), 1.0 / N, ALU.mult, EPS, ALU.add))
                v.sem_inc(var_ready, 1)
                inverse_deviation(D)
                link(tt(stat[:, 3, :], stat[:, 3, :], gain, ALU.mult))
                link(tt(tile, squares, over_tiles(stat[:, 3, :]), ALU.mult))
                link(tt(tile, tile, over_tiles(shift), ALU.add))

            def leaky(out, z):
                return v.scalar_tensor_tensor(out=out, in0=z, scalar=0.2, in1=z, op0=ALU.mult, op1=ALU.max)

            link(v.memset(W1es[:, :], 0.0))
            v.memset(X[:, NT - 1, :], 0.0).then_inc(ev("padding_zero"), 1)
            link(v.memset(ones[:, :], 1.0))
            v.wait_ge(ev("iotas"), 4)
            link(ts1(ident[:, :], iota[:, :], pcol[:, 0:1], ALU.is_equal))
            link(ts1(identb[:, :], iota[:, :], pcol[:, 0:1], ALU.is_equal))
            link(v.tensor_copy(identh[:, :], ident[:, :]))
            link(ts1(tri[:, :], iota[:, :], pcol[:, 0:1], ALU.is_lt))
            link(ts1(trashcol[:, 0:1], pcol[:, :], float(TRASH), ALU.add))
            link(ts1(trashcol[:, 1:2], pcol[:, :], float(TRASH - NPAD // 2), ALU.add))
            link(v.tensor_copy(iotab[:, :], iota[:, :]))
            v.wait_ge(ev("ends_loaded"), 16)
            link(v.tensor_single_scalar(jendi[0:1, 1, :], jendi[0:1, 0, :], 7, ALU.arith_shift_right))
            link(v.tensor_copy(jend[0:1, 0, :], jendi[0:1, 1, :]))
            tt(jend[0:1, 0, :], jend[0:1, 0, :], jend[0:1, 1, :], ALU.add).then_inc(ev("ends_made"), 1)
            v.wait_ge(ev("ends_spread"), 1)
            for g in range(SG):
                link(v.tensor_scalar(T12[:, 0:ET], WIDE[:, 0:ET], jcol[:, g:g + 1], 0.0, ALU.is_lt, ALU.add,
                                     accum_out=slots[:, 0, g:g + 1]))
            link(ts1(slots[:, 0, :], slots[:, 0, :], float(ET - 1), ALU.min))
            link(tt(slots[:, 1, :], jcol[:, :], slots[:, 0, :], ALU.subtract))
            link(ts1(slots[:, 1, :], slots[:, 1, :], float(NT - 1), ALU.min))
            link(ts1(slots[:, 2, :], slots[:, 1, :], -float(P), ALU.mult))
            link(v.tensor_copy(sloti[:, :, :], slots[:, 0:2, :]))
            made("slots_made")
            v.wait_ge(weights_loaded, 16 * WLOADS)
            link(ts1(coef[:, 0:BASES], coef[:, 0:BASES], coef[:, BASES:BASES + 1], ALU.mult))
            flat_bases = bas[:, :, :].rearrange("p b f -> p (b f)")
            link(v.tensor_reduce(wsum[:, 0:1], flat_bases, AX_X, ALU.max))
            link(v.tensor_reduce(wsum[:, 1:2], flat_bases, AX_X, ALU.min))
            link(v.scalar_tensor_tensor(out=wsum[:, 0:1], in0=wsum[:, 1:2], scalar=-1.0, in1=wsum[:, 0:1], op0=ALU.mult, op1=ALU.max))
            made("base_max")
            v.wait_ge(ev("l0_h"), 1)
            link(v.tensor_copy(H[:, :, :], NODES))
            for n, (name, lo) in enumerate((("att_dst", 0), ("att_src", 4))):
                link(tt(ACC1, H[:, :, :], over_tiles(V(name)), ALU.mult))
                link(v.tensor_reduce(ADN[:, :, lo:lo + 4], ACC1.rearrange("p t (h c) -> p t h c", h=HEADS), AX_X, ALU.add))
            made("att_made")
            v.wait_ge(ev("rows_gathered"), 16 * 3 * SG)
            link(v.tensor_copy(DR, RI[:, 0]))
            link(v.tensor_copy(SR, RI[:, 1]))
            link(v.tensor_copy(TR, RI[:, 2]))
            link(v.tensor_single_scalar(HII, RI[:, 1], 7, ALU.arith_shift_right))
            link(v.tensor_copy(HI, HII))
            link(v.scalar_tensor_tensor(out=LO, in0=HI, scalar=-float(P), in1=SR, op0=ALU.mult, op1=ALU.add))
            for g in range(SG):
                link(ts1(DL[:, g, :], DR[:, g, :], slots[:, 2, g:g + 1], ALU.add))
            link(ts1(VALID, DL, 0.0, ALU.is_ge))
            link(v.scalar_tensor_tensor(out=VALID, in0=DL, scalar=float(P), in1=VALID, op0=ALU.is_lt, op1=ALU.mult))
            link(v.scalar_tensor_tensor(out=HI, in0=HI, scalar=-float(P), in1=VALID, op0=ALU.add, op1=ALU.mult))
            link(ts1(HI, HI, float(P), ALU.add))
            made("rows_made")
            v.wait_ge(ev("base_max_turned"), 1)
            link(v.tensor_reduce(wsum[0:1, 1:2], bank(7, P)[0:1, :], AX_X, ALU.max))
            link(ts1(wsum[0:1, 1:2], wsum[0:1, 1:2], 2.0 ** -100, ALU.max))
            link(v.tensor_single_scalar(scalei[0:1, 0:1], wsum[0:1, 1:2].bitcast(I32), 0x7F800000, ALU.bitwise_and))
            link(ts1(wsum[0:1, 2:3], scalei[0:1, 0:1].bitcast(F32), 2.0 ** -7, ALU.mult))
            link(v.reciprocal(wsum[0:1, 3:4], wsum[0:1, 2:3]))
            made("base_scale")
            v.wait_ge(ev("base_scale_spread"), 1)
            link(v.tensor_copy(wsum[:, 2:4], bank(7, 2)))
            link(ts1(bas[:, :, :], bas[:, :, :], wsum[:, 3:4], ALU.mult))
            link(ts1(coef[:, 0:BASES], coef[:, 0:BASES], wsum[0:REL, 2:3], ALU.mult))
            for part in range(3):
                link(v.tensor_copy(coefb[:, part, :], coef[:, 0:BASES]))
                if part < 2:
                    link(tt(coef[:, 0:BASES], coef[:, 0:BASES], coefb[:, part, :], ALU.subtract))
            link(v.memset(OTA[:, 0, 0, :], 0.0))
            link(v.memset(AS[:, SLOTS:SPAD, :], 0.0))
            link(v.memset(ADAS[:, SLOTS:SPAD, :], 0.0))
            made("a_zeros")
            v.wait_ge(ev("column_copied"), 5)
            link(ts1(SRC[:, :], SRC[:, :], -float(NPAD // 2), ALU.add))
            v.sem_inc(ev("a_ring_free"), RING)
            with v.Fori(0, ITER) as i:
                for h in range(2):
                    n = i * 2 + h + 1
                    at = i * RING + h * HALF
                    v.wait_ge(ev("a_onehot_read"), n)
                    v.wait_ge(ev("a_turned"), n)
                    for k in range(HALF):
                        j = at + k
                        ts1(OHA[:, h, k, :], iotab[:, :], DLC[:, bass.ds(j, 1)], ALU.is_equal)
                        ts1(LOA[:, h, k, :], iotab[:, :], LOC[:, bass.ds(j, 1)], ALU.is_equal)
                        last = ts1(HIA[:, h, k, 0:NT], iotab[:, 0:NT], HIC[:, bass.ds(j, 1)], ALU.is_equal)
                    last.then_inc(ev("a_onehot"), 1)
                    for q in range(h * HALF, (h + 1) * HALF):
                        v.wait_ge(landed[q], i * 16 + 16)
                    v.tensor_copy(AS[:, bass.ds(at, HALF), :], GR[:, h * HALF:(h + 1) * HALF, 0:HEADS]).then_inc(ev("a_ring_free"), HALF)
            v.wait_ge(ev("a_ring_free"), SLOTS + RING)
            v.wait_ge(ev("a_adas_copied"), 2 * ITER + 2)
            v.wait_ge(ev("a_onehot_read"), 2 * ITER + 2)
            link(v.tensor_copy(DIS[:, 1, :], bank(7, NT)))
            made("edge_values")
            link(tt(FIRST[:, :, 1:P], DR[:, :, 1:P], DR[:, :, 0:P - 1], ALU.is_equal))
            link(v.memset(FIRST[:, :, 0:1], 0.0))
            link(ts1(AT, FIRST.unsqueeze(2).broadcast_to([P, SG, HEADS, P]), BIG, ALU.mult, -BIG, ALU.add))
            for hd in range(HEADS):
                v.wait_ge(ev("as_row"), hd + 1)
                b = (hd % 2) * 1024
                last = v.tensor_copy(VT[:, :, hd, :], WIDE[:, b:b + SPAD].rearrange("p (g l) -> p g l", l=P))
                last.then_inc(ev("as_row_copied"), 1)
            v.wait_ge(ev("as_row_copied"), HEADS)
            flat = SPAD * HEADS
            link(v.tensor_tensor_scan(ACCB[:, 0:flat], T12[:, flat:2 * flat], T12[:, 0:flat], -BIG, ALU.add, ALU.max))
            link(ts1(AT[:, :, :, 0:P - 1], FIRST[:, :, 1:P].unsqueeze(2).broadcast_to([P, SG, HEADS, P - 1]), BIG, ALU.mult,
                     -BIG, ALU.add))
            link(v.memset(AT[:, :, :, P - 1:P], -BIG))
            link(v.tensor_tensor_scan(T12[:, 0:flat][:, ::-1], T12[:, flat:2 * flat][:, ::-1], ACCB[:, 0:flat][:, ::-1],
                                      -BIG, ALU.add, ALU.max))
            made("slot_max_made")
            for n, row in enumerate((R_FM, R_LM, R_FD, R_LD)):
                v.wait_ge(ev("end_row"), n + 1)
                b = (n % 2) * 1024
                link(v.tensor_copy(row, WIDE[0:HEADS, b:b + SPAD]))
                v.sem_inc(ev("end_row_copied"), 1)
            link(tt(R_W, R_FD, R_LD, ALU.is_equal))
            link(v.memset(R_LINK[:, 0:1], 0.0))
            link(tt(R_LINK[:, 1:SPAD], R_FD[:, 1:SPAD], R_LD[:, 0:SPAD - 1], ALU.is_equal))
            link(tt(R_A, R_LINK, R_W, ALU.mult))
            link(ts1(R_A, R_A, BIG, ALU.mult, -BIG, ALU.add))
            link(v.tensor_tensor_scan(R_OUT, R_A, R_LM, -BIG, ALU.add, ALU.max))
            link(v.memset(R_CF[:, 0:1], -BIG))
            link(ts1(R_CF[:, 1:SPAD], R_LINK[:, 1:SPAD], BIG, ALU.mult, -BIG, ALU.add))
            link(tt(R_CF[:, 1:SPAD], R_CF[:, 1:SPAD], R_OUT[:, 0:SPAD - 1], ALU.add))
            link(tt(R_A[:, 0:SPAD - 1], R_LINK[:, 1:SPAD], R_W[:, 0:SPAD - 1], ALU.mult))
            link(v.memset(R_A[:, SPAD - 1:SPAD], 0.0))
            link(ts1(R_A, R_A, BIG, ALU.mult, -BIG, ALU.add))
            link(v.tensor_tensor_scan(R_OUT[:, ::-1], R_A[:, ::-1], R_FM[:, ::-1], -BIG, ALU.add, ALU.max))
            link(v.memset(R_CB[:, SPAD - 1:SPAD], -BIG))
            link(ts1(R_CB[:, 0:SPAD - 1], R_LINK[:, 1:SPAD], BIG, ALU.mult, -BIG, ALU.add))
            link(tt(R_CB[:, 0:SPAD - 1], R_CB[:, 0:SPAD - 1], R_OUT[:, 1:SPAD], ALU.add))
            made("carries_made")
            v.wait_ge(ev("carries_turned"), 1)
            link(v.tensor_copy(carry[:, :, :, :].rearrange("p n g h -> p (n g h)"), WIDE[:, 3072:3072 + 3 * SG * HEADS]))
            for c, lane in ((0, 0), (1, P - 1)):
                link(tt(AT[:, :, 0, :], DR, DR[:, :, lane:lane + 1].broadcast_to([P, SG, P]), ALU.is_equal))
                link(ts1(AT[:, :, 0, :], AT[:, :, 0, :], BIG, ALU.mult, -BIG, ALU.add))
                for g in range(SG):
                    for hd in range(HEADS):
                        last = v.scalar_tensor_tensor(out=VT[:, g, hd, :], in0=AT[:, g, 0, :], scalar=carry[:, c, g, hd:hd + 1],
                                                      in1=VT[:, g, hd, :], op0=ALU.add, op1=ALU.max)
                link(last)
            link(ts1(FIRST[:, :, 0], carry[:, 2, :, 0], 1.0, ALU.mult))
            link(v.scalar_tensor_tensor(out=FIRST, in0=FIRST, scalar=0.5, in1=VALID, op0=ALU.is_lt, op1=ALU.mult))
            made("max_made")
            for n in range(HEADS + 1):
                v.wait_ge(ev("max_turned"), n + 1)
                b = (n % 2) * 1024
                dst = MT[:, :, n] if n < HEADS else FIRSTC
                link(v.tensor_copy(dst, WIDE[:, b:b + SPAD]))
                v.sem_inc(ev("max_copied"), 1)
            link(tt(MT, MT, ADAS[:, :, 4:8], ALU.max))
            link(tt(EXF[:, :, 4:8], MT, FIRSTC.unsqueeze(2).broadcast_to([P, SPAD, HEADS]), ALU.mult))
            link(v.tensor_copy(EXF[:, :, 8], FIRSTC))
            link(tt(AS, AS, ADAS[:, :, 0:4], ALU.add))
            link(leaky(AS, AS))
            link(tt(MT, MT, ADAS[:, :, 0:4], ALU.add))
            link(leaky(MT, MT))
            link(tt(ADAS[:, :, 0:4], AS, MT, ALU.subtract))
            made("ex_argument")
            v.wait_ge(ev("ex"), 1)

            def add_sums(name, acc, q, j, t, credit, banks=tuple(range(MS))):
                v.wait_ge(ev(name + "_sums"), j + 1 + credit)
                v.wait_ge(ev(name + "_sums_added"), j + MS)
                a = acc[:, bass.ds(t, 1), :].rearrange("p a b -> p (a b)")
                tt(a, a, bank(banks[q % MS], acc.shape[-1]), ALU.add).then_inc(ev(name + "_sums_added"), 1)

            v.wait_ge(ev("sums_cleared"), 1)
            v.wait_ge(ev("slots_loaded"), 32)
            v.sem_inc(ev("l0_sums_added"), MS)
            v.sem_inc(ev("l0_messages"), RING)
            with v.Fori(0, ITER) as i:
                tiles = tile_registers(ENG.DVE, i)
                for q in range(RING + 1):
                    if q < RING:
                        j = i * RING + q
                        r = q % MS
                        v.wait_ge(ev("l0_sums"), j + 1 + RING - MS)
                        ts1(OH[:, r, :], iota[:, :], DLC[:, bass.ds(j, 1)], ALU.is_equal)
                        v.tensor_copy(MSG0[:, r, D:COLS0], EXF[:, bass.ds(j, 1), :].rearrange("p a b -> p (a b)")
                                      )
                        v.wait_ge(landed[q], i * 16 + (ITER * 16 + 16))
                        tt(MSG0[:, r, 0:D].rearrange("p (h c) -> p h c", h=HEADS), GR[:, q, :].rearrange("p (h c) -> p h c", h=HEADS),
                           EXF[:, bass.ds(j, 1), 0:HEADS].rearrange("p a b -> p (a b)").unsqueeze(2).broadcast_to([P, HEADS, HC]),
                           ALU.mult).then_inc(ev("l0_messages"), 1)
                    if q >= 1:
                        add_sums("l0", ACC0, q - 1, i * RING + q - 1, tiles[q - 1], RING)
            v.wait_ge(ev("l0_sums_added"), SLOTS + MS)
            EXL = SMN[:, 1, :, :]
            link(ts1(HAS[:, :], ACC0[:, :, COLS0 - 1], BIG, ALU.mult, -BIG, ALU.add))
            link(tt(SMN[:, 2, :, :], ACC0[:, :, D + 4:D + 8], HAS[:, :].unsqueeze(2).broadcast_to([P, NT, HEADS]), ALU.add))
            link(tt(SMN[:, 2, :, :], SMN[:, 2, :, :], ADN[:, :, 4:8], ALU.max))
            link(tt(SMN[:, 2, :, :], SMN[:, 2, :, :], ADN[:, :, 0:4], ALU.add))
            link(leaky(SMN[:, 2, :, :], SMN[:, 2, :, :]))
            link(tt(SMN[:, 3, :, :], ADN[:, :, 4:8], ADN[:, :, 0:4], ALU.add))
            link(leaky(SMN[:, 3, :, :], SMN[:, 3, :, :]))
            link(tt(SMN[:, 0, :, :], SMN[:, 3, :, :], SMN[:, 2, :, :], ALU.subtract))
            made("loop_argument")
            v.wait_ge(ev("loop_ex"), 1)
            link(tt(SMN[:, 2, :, :], ACC0[:, :, D:D + 4], EXL, ALU.add))
            link(v.reciprocal(SMN[:, 3, :, :], SMN[:, 2, :, :]))
            by_head = [P, NT, HEADS, HC]
            T1H, HH = T1.rearrange("p t (h c) -> p t h c", h=HEADS), H[:, :, :].rearrange("p t (h c) -> p t h c", h=HEADS)
            link(tt(T1H, HH, EXL.unsqueeze(3).broadcast_to(by_head), ALU.mult))
            link(tt(T1, T1, ACC0[:, :, 0:D], ALU.add))
            link(tt(T1H, T1H, SMN[:, 3, :, :].unsqueeze(3).broadcast_to(by_head), ALU.mult))
            link(tt(T1, T1, over_tiles(V("bias")), ALU.add))
            batch_norm(T1, T2, V("bn_g"), V("bn_b"))
            layer_norm(T1, T1)
            affine(T1, V("ln_g"), V("ln_b"))
            v.wait_ge(ev("l0_res"), 1)
            link(tt(H[:, :, :], NODES, over_tiles(V("res_b")), ALU.add))
            batch_norm(H[:, :, :], T2, V("bnres_g"), V("bnres_b"))
            link(tt(T1, T1, H[:, :, :], ALU.add))
            link(v.scalar_tensor_tensor(out=X[:, :, :], in0=T1, scalar=0.0, in1=X[:, :, :], op0=ALU.max, op1=ALU.add))
            layer_norm(X, X)
            made("x1_made")
            link(ts1(stat[:, 1, 0:NT], DIS[:, 1, :], 1.0, ALU.add))
            link(ts1(stat[:, 1, NT:2 * NT], DIS[:, 1, :], 1.0, ALU.max))
            link(ts1(HAS[:, :], DIS[:, 1, :], 0.0, ALU.is_gt))
            v.sem_inc(var_ready, 1)
            inverse_deviation(2 * NT)
            link(v.tensor_copy(DIS[:, 0, :], stat[:, 3, 0:NT]))
            link(tt(DIS[:, 1, :], stat[:, 3, NT:2 * NT], HAS[:, :], ALU.mult))
            v.wait_ge(ev("l1_h"), 1)
            link(tt(H[:, :, :], NODES, over_tiles(V("b_l1")), ALU.add))
            link(tt(H[:, :, :], H[:, :, :], over_features(DIS[:, 0, :]), ALU.mult))
            made("h1_made")
            v.wait_ge(ev("sums_cleared"), 2)
            link(v.tensor_copy(SRCH, SRC[:, :]))
            link(v.memset(OHT, 0.0))
            link(v.memset(DUP, 0.0))
            v.sem_inc(ev("l1_sums_added"), MS)
            v.sem_inc(ev("l1_repeats"), 2)
            made("l1_ready")

            def l1_types(at, h, n):
                v.wait_ge(ev("l1_types_turned"), n)
                for k in range(HALF):
                    last = ts1(OHT[:, h, k, 0:REL], iotab[:, 0:REL], TYC[:, bass.ds(at + k, 1)], ALU.is_equal)
                last.then_inc(ev("l1_type_onehot"), 1)

            def l1_onehot(j, q):
                v.wait_ge(ev("l1_sums"), j + 1 + RING - MS)
                ts1(OH[:, q % MS, :], iota[:, :], DLC[:, bass.ds(j, 1)], ALU.is_equal).then_inc(ev("l1_onehot"), 1)

            l1_types(0, 0, 1)
            l1_onehot(0, 0)
            with v.Fori(0, ITER) as i:
                tiles = tile_registers(ENG.DVE, i)
                for q in range(RING):
                    j = i * RING + q
                    l1_onehot(j + 1, q + 1)
                    v.wait_ge(ev("l1_sources"), j + 1)
                    v.wait_ge(ev("l1_repeats"), j + 1)
                    v.scalar_tensor_tensor(out=JUNK[:, q % 2, :], in0=bank(2 + q % 2, P),
                                           scalar=SRC[:, bass.ds(j, 1)], in1=tri[:, :], op0=ALU.is_equal,
                                           op1=ALU.mult, accum_out=DUP[:, bass.ds(j, 1)]).then_inc(ev("l1_repeats"), 1)
                    if q % HALF == 1:
                        h = 1 - q // HALF
                        l1_types(i * RING + (q // HALF + 1) * HALF, h, i * 2 + q // HALF + 2)
                    if q >= 1:
                        add_sums("l1", ACC1, q - 1, j - 1, tiles[q - 1], RING, L1_BANKS)
                add_sums("l1", ACC1, RING - 1, i * RING + RING - 1, tiles[RING - 1], RING, L1_BANKS)
            v.wait_ge(ev("l1_repeats"), SLOTS + 2)
            link(ts1(FIRSTSRC, DUP, 0.5, ALU.is_lt))
            link(v.scalar_tensor_tensor(out=FIRSTSRC, in0=SRC[:, :], scalar=trashcol[:, 1:2], in1=FIRSTSRC,
                                        op0=ALU.subtract, op1=ALU.mult))
            link(ts1(SCI, FIRSTSRC, trashcol[:, 0:1], ALU.add))
            v.wait_ge(ev("l1_coefs_copied"), 2 * ITER + 1)
            made("scatter_rows_made")
            v.wait_ge(ev("l1_sums_added"), SLOTS + MS)
            v.wait_ge(ev("h1_stored"), 16)
            v.wait_ge(ev("acc_zero_stored"), 16 * NACC)
            link(tt(T1, ACC1, H[:, :, :], ALU.add))
            link(tt(T1, T1, over_features(DIS[:, 0, :]), ALU.mult))
            link(ts1(T1, T1, 0.0, ALU.max))
            layer_norm(T1, T1)
            affine(T1, V("g_l1"), V("be_l1"))
            link(v.scalar_tensor_tensor(out=X[:, :, :], in0=X[:, :, :], scalar=2.0, in1=T1, op0=ALU.mult, op1=ALU.add))
            layer_norm(X, X)
            link(tt(T1, X[:, :, :], over_features(DIS[:, 1, :]), ALU.mult))
            made("l2_scaled")
            for t in range(NT):
                v.wait_ge(ev("l2_y_high"), t + 1)
                tt(YP[1][:, t, :], bank(t % 4), YP[0][:, t, :], ALU.subtract).then_inc(ev("l2_y_copied"), 1)
            v.wait_ge(ev("l2_y_copied"), NT)
            link(v.memset(COEF[:, SLOTS:SPAD, :], 0.0))
            made("l2_y_parts")
            made("l2_coef_tail")
            v.sem_inc(ev("l2_equal"), MS)
            v.sem_inc(ev("l2_mixed"), MS)

            def onehot(j, q):
                v.wait_ge(ev("l2_turned"), j + 1)
                ts1(OH2[:, q % MS, :], iotab[:, :], DLC[:, bass.ds(j, 1)], ALU.is_equal).then_inc(ev("l2_onehot"), 1)

            def equal(j, q):
                v.wait_ge(ev("l2_turned_copied"), j + 2)
                v.wait_ge(ev("l2_summed"), j + 1)
                ts1(EQ[:, q % MS, :], OT2[:, q % MS, 1, :], SRC[:, bass.ds(j, 1)], ALU.is_equal).then_inc(ev("l2_equal"), 1)

            for j in range(5):
                onehot(j, j)
            for j in range(2):
                equal(j, j)
            with v.Fori(0, ITER) as i:
                for q in range(RING):
                    j = i * RING + q

                    def mix(b):
                        v.scalar_tensor_tensor(out=MSG2[:, 0, q % MS, :], in0=bank(q % MS)[:, b * D:(b + 1) * D],
                                               scalar=COEF[:, bass.ds(j, 1), b:b + 1].rearrange("p a b -> p (a b)"),
                                               in1=MSG2[:, 0, q % MS, :], op0=ALU.mult, op1=ALU.add
                                               ).then_inc(ev("l2_mixed" if b == BASES - 1 else "l2_mixing"), 1)

                    v.wait_ge(ev("l2_mixed_first"), j + 1)
                    mix(2)
                    onehot(j + 5, q + 5)
                    equal(j + 2, q + 2)
                    v.wait_ge(ev("l2_mixing"), j + 1)
                    mix(3)
            v.wait_ge(ev("l2_equal"), SLOTS + 2 + MS)
            v.wait_ge(ev("l2_turned_copied"), SLOTS + 5)
            made("l2_mixes_done")
            v.wait_ge(ev("acc_loaded"), 16 * NACC)
            for part in (T2, ACC1, ACC1B, H[:, :, :]):
                link(tt(T1, T1, part, ALU.add))
            link(tt(T1, T1, over_features(DIS[:, 1, :]), ALU.mult))
            link(tt(X[:, :, :], X[:, :, :], T1, ALU.add))
            layer_norm(X, X)
            made("x3_made")
            for n, w in enumerate((W1xs[:, :], W1es[0:EDIM, :], B1[:, :])):
                k = w.shape[0]
                link(v.tensor_reduce(wsum[0:k, n:n + 1], w, AX_X, ALU.add))
                link(ts1(wsum[0:k, n:n + 1], wsum[0:k, n:n + 1], -1.0 / HID, ALU.mult))
                link(ts1(w, w, wsum[0:k, n:n + 1], ALU.add))
            link(ts1(G1[:, :], G1[:, :], HID ** 0.5, ALU.mult))
            made("l3_w1_centered")
            for t in range(NT):
                v.wait_ge(ev("l3_p"), t + 1)
                tt(PN[:, t, :], bank(t % 4, HID), B1[:, :], ALU.add).then_inc(ev("l3_p_copied"), 1)
            v.wait_ge(ev("l3_p_copied"), NT)
            made("p_made")
            v.wait_ge(ev("l3_xu"), 1)
            link(tt(H[:, :, :], NODES, over_tiles(V("bu")), ALU.add))
            v.wait_ge(ev("sums_cleared"), 3)
            v.wait_ge(ev("l3_rings_set"), 2)
            v.sem_inc(ev("l3_sums_added"), MS)
            v.sem_inc(ev("l3_scaled"), RING3)
            made("l3_ready")

            def inverse(i, q, n):
                at = q % RING3
                vv, half_exp, y, a = [SS[:, k, at:at + RING] for k in (1, 2, 3, 2)]
                if n == 0:
                    v.wait_ge(ev("l3_squares"), i * RING3 + q + RING + 2)
                else:
                    v.wait_ge(ev("l3_inverse"), (i * (RING3 // RING) + q // RING) * INV_STEPS + n)
                if n == 0:
                    op = ts1(vv, SS[:, 0, at:at + RING], HID * EPS, ALU.add)
                elif n == 1:
                    op = v.tensor_single_scalar(half_exp.bitcast(I32), vv.bitcast(I32), 1, ALU.arith_shift_right)
                elif n == 2:
                    op = ts1(y.bitcast(I32), half_exp.bitcast(I32), -1.0, ALU.mult, float(0x5f3759df), ALU.add)
                elif n % 3 == 0:
                    op = v.scalar_tensor_tensor(out=a, in0=y, scalar=-0.5, in1=y, op0=ALU.mult, op1=ALU.mult)
                elif n % 3 == 1:
                    op = tt(a, a, vv, ALU.mult)
                else:
                    op = v.scalar_tensor_tensor(out=y, in0=a, scalar=1.5, in1=y, op0=ALU.add, op1=ALU.mult)
                op.then_inc(ev("l3_inverse"), 1)

            def norm(i, q):
                j = i * RING3 + q
                c, r = q % RING3, q % MS
                h, k = q // RING * RING + RING, q % RING - INV_FROM
                ahead = exists(i, h) and 0 <= k < INV_STEPS // 3
                if q % RING == 0:
                    v.wait_ge(ev("l3_inverse"), (i * (RING3 // RING) + q // RING + 1) * INV_STEPS)
                v.wait_ge(ev("l3_gelu"), j + 1)
                v.scalar_tensor_tensor(out=ZB[:, r, :], in0=HC3[:, c, :], scalar=SS[:, 3, c:c + 1], in1=G1[:, :],
                                       op0=ALU.mult, op1=ALU.mult).then_inc(ev("l3_scaled"), 1)
                if ahead:
                    inverse(i, h, 3 * k)
                v.wait_ge(ev("l3_sums"), j + 1)
                ts1(OH[:, r, :], iota[:, :], DLC[:, bass.ds(j, 1)], ALU.is_equal).then_inc(ev("l3_onehot"), 1)
                if ahead:
                    inverse(i, h, 3 * k + 1)
                v.wait_ge(ev("l3_scaled"), j + 1 + RING3)
                tt(ZB[:, r, :], ZB[:, r, :], BE1[:, :], ALU.add).then_inc(ev("l3_normed"), 1)
                if ahead:
                    inverse(i, h, 3 * k + 2)

            def add_step(i, q):
                if q % RING == 0:
                    tiles[:] = tile_registers(ENG.DVE, i, q, RING3)
                if exists(i, q + 2):
                    norm(i, q + 2)
                add_sums("l3", ACC3, q, i * RING3 + q, tiles[q % RING], MS)

            tiles = []
            for n in range(INV_STEPS):
                inverse(0, 0, n)
            for q in range(2):
                norm(0, q)
            steps3(v, add_step)
            v.wait_ge(ev("l3_sums_added"), SLOTS + MS)
            for t in range(NT):
                last = v.scalar_tensor_tensor(out=H[:, t, :], in0=B2U[:, :], scalar=ACC3[:, t, HID:HID + 1], in1=H[:, t, :],
                                              op0=ALU.mult, op1=ALU.add)
            link(last)
            v.wait_ge(ev("l3_u"), 1)
            link(tt(T1, NODES, H[:, :, :], ALU.add))
            layer_norm(T1, T1)
            affine(T1, V("gu"), V("beu"))
            made("u_normed")
            v.wait_ge(ev("u_gelu"), 1)
            link(v.scalar_tensor_tensor(out=X[:, :, :], in0=X[:, :, :], scalar=2.0, in1=T1, op0=ALU.mult, op1=ALU.add))
            layer_norm(X, X)
            made("out_made")


def kernel(**inputs):
    import numpy as np
    import concourse.bacc as bacc
    from concourse.bass_utils import run_bass_kernel_spmd

    nc = bacc.Bacc("TRN2", target_bir_lowering=False, num_devices=1)
    arrays = {}

    def feed(name, a):
        a = np.ascontiguousarray(a)
        arrays[name] = a
        return nc.dram_tensor(name, a.shape, mybir.dt.from_np(a.dtype), kind="ExternalInput").ap()

    def tiles_of_edges(a, pad):
        whole = np.full((ET * P,) + a.shape[1:], pad, a.dtype)
        whole[:E] = a
        return whole.reshape((ET, P) + a.shape[1:])

    g = {k: np.asarray(a) for k, a in inputs.items()}
    vec_from = {"att_src": "L0_gnn_att_src", "att_dst": "L0_gnn_att_dst", "bias": "L0_gnn_bias", "bn_g": "L0_gnn_bn_gamma",
                "bn_b": "L0_gnn_bn_beta", "ln_g": "L0_gnn_ln_gamma", "ln_b": "L0_gnn_ln_beta", "res_b": "L0_gnn_res_b",
                "bnres_g": "L0_gnn_bnres_gamma", "bnres_b": "L0_gnn_bnres_beta", "b_l1": "L1_gnn_b", "g_l1": "L1_gnn_gamma",
                "be_l1": "L1_gnn_beta", "bu": "L3_gnn_bu", "gu": "L3_gnn_gu", "beu": "L3_gnn_beu"}
    args = dict(
        x=feed("in_x", g["x"]),
        src_t=feed("in_src", tiles_of_edges(g["src"], PAD_NODE)),
        dst_t=feed("in_dst", tiles_of_edges(g["dst"], PAD_NODE)),
        typ_t=feed("in_type", tiles_of_edges(g["edge_type_50"], 0)),
        attr_t=feed("in_attr", tiles_of_edges(g["edge_attr_32"], 0).transpose(0, 2, 1).reshape(ET, EDIM * P)),
        W0=feed("in_w0", g["L0_gnn_W"]),
        resW=feed("in_res_w", g["L0_gnn_res_W"]),
        vec={k: feed("in_" + k, g[s].reshape(D)) for k, s in vec_from.items()},
        W1T=feed("in_l1_w", g["L1_gnn_W"].T),
        bases=feed("in_bases", g["L2_gnn_bases"]),
        comps=feed("in_comps", g["L2_gnn_comps"]),
        alpha=feed("in_alpha", g["L2_gnn_alpha"]),
        W1x=feed("in_l3_w1x", g["L3_gnn_W1"][:D]),
        W1e=feed("in_l3_w1e", g["L3_gnn_W1"][D:]),
        b1=feed("in_l3_b1", g["L3_gnn_b1"]),
        g1=feed("in_l3_g1", g["L3_gnn_g1"]),
        be1=feed("in_l3_be1", g["L3_gnn_be1"]),
        W2=feed("in_l3_w2", g["L3_gnn_W2"]),
        b2=feed("in_l3_b2", g["L3_gnn_b2"]),
        Wu=feed("in_l3_wu", g["L3_gnn_Wu"]),
    )
    out = nc.dram_tensor("out_0", (N, D), F32, kind="ExternalOutput").ap()
    gnn_stack(nc, out=out, **args)
    r = run_bass_kernel_spmd(nc, [arrays], core_ids=[0])
    return r.results[0]["out_0"]
```
